# Optimizing a Trainium2 kernel written in Bass

```python
import numpy as np
import jax
import jax.numpy as jnp

def _softmax(x, axis=-1):
    return jax.nn.softmax(x, axis=axis)

def _gelu(x):
    return jax.nn.gelu(x, approximate=True)

def _silu(x):
    return jax.nn.silu(x)

def _sigmoid(x):
    return jax.nn.sigmoid(x)

def _layernorm(x, axis=-1, eps=1e-05):
    m = jnp.mean(x, axis=axis, keepdims=True)
    v = jnp.var(x, axis=axis, keepdims=True)
    return (x - m) / jnp.sqrt(v + eps)

def _scatter_add(tgt, idx, src, axis=0):
    return tgt.at[idx].add(src)

def _segment_sum(src, seg, n):
    return jax.ops.segment_sum(src, seg, n)
kernel_name = 'mk_gnn_resnorm_d4_gnn_r32_359e8f'

def setup_inputs(seed: int=0):
    np.random.seed(seed)
    _w = jnp.asarray

    def _rec_inputs():
        import jax
        import jax.numpy as jnp
        _gk = jax.random.key(seed)
        x = -0.0003713 + 1 * jax.random.normal(jax.random.fold_in(_gk, 1), (3125, 256), jnp.float32)
        src = jax.random.randint(jax.random.fold_in(_gk, 2), (50000,), 0, 3125, jnp.int32)
        dst = jax.random.randint(jax.random.fold_in(_gk, 3), (50000,), 0, 3125, jnp.int32)
        _o = jnp.argsort(dst, stable=True)
        src = src[_o]
        dst = dst[_o]
        edge_attr_10 = jax.random.uniform(jax.random.fold_in(_gk, 13), (50000, 10), jnp.float32, 0.0, 1)
        edge_attr_128 = -5.16925e-05 + 1.00005 * jax.random.normal(jax.random.fold_in(_gk, 14), (50000, 128), jnp.float32)
        edge_attr_4 = 0.00109026 + 0.999989 * jax.random.normal(jax.random.fold_in(_gk, 15), (50000, 4), jnp.float32)
        edge_attr_64 = 0.000189758 + 1.00013 * jax.random.normal(jax.random.fold_in(_gk, 16), (50000, 64), jnp.float32)
        return (x, src, dst, edge_attr_10, edge_attr_128, edge_attr_4, edge_attr_64)
    x, src, dst, edge_attr_10, edge_attr_128, edge_attr_4, edge_attr_64 = _rec_inputs()

    def _L0_gnn_setup():
        import jax, jax.numpy as jnp
        import numpy as np
        MUL = 64
        N_NODES = 50000
        N_EDGES = 25000
        NUM_NEIGHBORS = 16.0
        SILU_NORM = 1.679177
        key = jax.random.key(seed)
        ks = jax.random.split(key, 9)
        node_in = jax.random.normal(ks[0], (N_NODES, 4 * MUL), dtype=jnp.float32)
        edge_src = jax.random.randint(ks[1], (N_EDGES,), 0, N_NODES)
        edge_dst = jax.random.randint(ks[2], (N_EDGES,), 0, N_NODES)
        edge_attr = jax.random.normal(ks[3], (N_EDGES, 4), dtype=jnp.float32)
        edge_len_emb = jax.random.uniform(ks[4], (N_EDGES, 10), dtype=jnp.float32)
        w_00_0 = jax.random.normal(ks[5], (MUL, MUL), dtype=jnp.float32)
        w_11_0 = jax.random.normal(ks[6], (MUL, MUL), dtype=jnp.float32)
        w_01_1 = jax.random.normal(ks[7], (MUL, MUL), dtype=jnp.float32)
        w_10_1 = jax.random.normal(ks[8], (MUL, MUL), dtype=jnp.float32)
        kf = jax.random.split(jax.random.fold_in(key, 1), 2)
        fc_w1 = jax.random.normal(kf[0], (10, 64), dtype=jnp.float32)
        fc_w2 = jax.random.normal(kf[1], (64, 1), dtype=jnp.float32)
        return {'node_in': node_in, 'edge_attr': edge_attr, 'edge_len_emb': edge_len_emb, 'w_00_0': w_00_0, 'w_11_0': w_11_0, 'w_01_1': w_01_1, 'w_10_1': w_10_1, 'fc_w1': fc_w1, 'fc_w2': fc_w2, 'edge_src': edge_src, 'edge_dst': edge_dst}
    _L0_gnn_all = _L0_gnn_setup()
    _L0_gnn_in = {k: v for k, v in _L0_gnn_all.items() if k in ('w_00_0', 'w_11_0', 'w_01_1', 'w_10_1', 'fc_w1', 'fc_w2')}
    del _L0_gnn_all

    def _L1_gnn_setup():
        import jax, jax.numpy as jnp
        import numpy as np
        N_NODES = 10000
        N_EDGES = 10000
        D_FEAT = 256
        N_LAYERS = 4
        EPS = 1e-16

        def _agnn_layer(h, src, dst, beta, num_nodes):
            h_norm = h * jax.lax.rsqrt(jnp.sum(h * h, axis=-1, keepdims=True) + EPS)
            cos = jnp.sum(h_norm[src] * h_norm[dst], axis=-1)
            logits = beta * cos
            m = jax.ops.segment_max(logits, dst, num_segments=num_nodes)
            ex = jnp.exp(logits - m[dst])
            denom = jax.ops.segment_sum(ex, dst, num_segments=num_nodes)
            alpha = ex / (denom[dst] + EPS)
            msg = alpha[:, None] * h[src]
            return jax.ops.segment_sum(msg, dst, num_segments=num_nodes)
        key = jax.random.key(seed)
        k1, k2, k3 = jax.random.split(key, 3)
        feats = jax.random.normal(k1, (N_NODES, D_FEAT), dtype=jnp.float32)
        src = jax.random.randint(k2, (N_EDGES,), 0, N_NODES, dtype=jnp.int32)
        dst = jax.random.randint(k3, (N_EDGES,), 0, N_NODES, dtype=jnp.int32)
        betas = jnp.ones((N_LAYERS,), dtype=jnp.float32)
        return {'feats': feats, 'src': src, 'dst': dst, 'betas': betas}
    _L1_gnn_all = _L1_gnn_setup()
    _L1_gnn_in = {k: v for k, v in _L1_gnn_all.items() if k in ('betas',)}
    del _L1_gnn_all

    def _L2_gnn_setup():
        import jax, jax.numpy as jnp
        import numpy as np
        N_NODES = 50000
        N_EDGES = 25000
        NODE_IN = 256
        EDGE_OUT = 64
        GLOBAL_IN = 128
        NODE_OUT = 256
        HIDDEN = 512
        N_GRAPHS = 64
        key = jax.random.key(seed)
        ks = jax.random.split(key, 8)
        x = jax.random.normal(ks[0], (N_NODES, NODE_IN), dtype=jnp.float32)
        edge_index = jax.random.randint(ks[1], (2, N_EDGES), 0, N_NODES, dtype=jnp.int64)
        edge_attr = jax.random.normal(ks[2], (N_EDGES, EDGE_OUT), dtype=jnp.float32)
        u = jax.random.normal(ks[3], (N_GRAPHS, GLOBAL_IN), dtype=jnp.float32)
        batch = jnp.sort(jax.random.randint(ks[4], (N_NODES,), 0, N_GRAPHS, dtype=jnp.int64))
        in_dim = NODE_IN + EDGE_OUT + GLOBAL_IN
        b1s = 1.0 / np.sqrt(in_dim)
        b2s = 1.0 / np.sqrt(HIDDEN)
        W1 = jax.random.uniform(ks[5], (in_dim, HIDDEN), dtype=jnp.float32, minval=-b1s, maxval=b1s)
        b1 = jnp.zeros((HIDDEN,), dtype=jnp.float32)
        W2 = jax.random.uniform(ks[6], (HIDDEN, NODE_OUT), dtype=jnp.float32, minval=-b2s, maxval=b2s)
        b2 = jnp.zeros((NODE_OUT,), dtype=jnp.float32)
        return {'x': x, 'edge_index': edge_index, 'edge_attr': edge_attr, 'u': u, 'batch': batch, 'W1': W1, 'b1': b1, 'W2': W2, 'b2': b2}
    _L2_gnn_all = _L2_gnn_setup()
    _L2_gnn_in = {k: v for k, v in _L2_gnn_all.items() if k in ('u', 'W1', 'b1', 'W2', 'b2')}
    del _L2_gnn_all

    def _L3_gnn_setup():
        import jax, jax.numpy as jnp
        import numpy as np
        N_NODES = 50000
        N_EDGES = 25000
        IN_DIM = 256
        OUT_DIM = 256
        EDGE_DIM = 128
        BN_EPS = 1e-05
        key = jax.random.key(seed)
        ks = jax.random.split(key, 10)
        s = lambda d: 1.0 / np.sqrt(d)
        return {'x': jax.random.normal(ks[0], (N_NODES, IN_DIM), dtype=jnp.float32), 'edge_index': jax.random.randint(ks[1], (2, N_EDGES), 0, N_NODES, dtype=jnp.int64), 'edge_attr': jax.random.normal(ks[2], (N_EDGES, EDGE_DIM), dtype=jnp.float32), 'W_edge': jax.random.uniform(ks[3], (EDGE_DIM, IN_DIM), jnp.float32, -s(EDGE_DIM), s(EDGE_DIM)), 'b_edge': jnp.zeros((IN_DIM,), jnp.float32), 'W1': jax.random.uniform(ks[4], (IN_DIM, OUT_DIM), jnp.float32, -s(IN_DIM), s(IN_DIM)), 'b1': jnp.zeros((OUT_DIM,), jnp.float32), 'W2': jax.random.uniform(ks[5], (OUT_DIM, OUT_DIM), jnp.float32, -s(OUT_DIM), s(OUT_DIM)), 'b2': jnp.zeros((OUT_DIM,), jnp.float32), 'eps': jnp.float32(0.0), 'gamma': jnp.ones((OUT_DIM,), jnp.float32), 'beta': jnp.zeros((OUT_DIM,), jnp.float32)}
    _L3_gnn_all = _L3_gnn_setup()
    _L3_gnn_in = {k: v for k, v in _L3_gnn_all.items() if k in ('W_edge', 'b_edge', 'W1', 'b1', 'W2', 'b2', 'eps', 'gamma', 'beta')}
    del _L3_gnn_all
    return {'x': x, 'src': src, 'dst': dst, 'edge_attr_10': edge_attr_10, 'edge_attr_128': edge_attr_128, 'edge_attr_4': edge_attr_4, 'edge_attr_64': edge_attr_64, 'L0_gnn_w_00_0': _L0_gnn_in['w_00_0'], 'L0_gnn_w_11_0': _L0_gnn_in['w_11_0'], 'L0_gnn_w_01_1': _L0_gnn_in['w_01_1'], 'L0_gnn_w_10_1': _L0_gnn_in['w_10_1'], 'L0_gnn_fc_w1': _L0_gnn_in['fc_w1'], 'L0_gnn_fc_w2': _L0_gnn_in['fc_w2'], 'L1_gnn_betas': _L1_gnn_in['betas'], 'L2_gnn_u': _L2_gnn_in['u'], 'L2_gnn_W1': _L2_gnn_in['W1'], 'L2_gnn_b1': _L2_gnn_in['b1'], 'L2_gnn_W2': _L2_gnn_in['W2'], 'L2_gnn_b2': _L2_gnn_in['b2'], 'L3_gnn_W_edge': _L3_gnn_in['W_edge'], 'L3_gnn_b_edge': _L3_gnn_in['b_edge'], 'L3_gnn_W1': _L3_gnn_in['W1'], 'L3_gnn_b1': _L3_gnn_in['b1'], 'L3_gnn_W2': _L3_gnn_in['W2'], 'L3_gnn_b2': _L3_gnn_in['b2'], 'L3_gnn_eps': _L3_gnn_in['eps'], 'L3_gnn_gamma': _L3_gnn_in['gamma'], 'L3_gnn_beta': _L3_gnn_in['beta']}

def reference(x, src, dst, edge_attr_10, edge_attr_128, edge_attr_4, edge_attr_64, L0_gnn_w_00_0, L0_gnn_w_11_0, L0_gnn_w_01_1, L0_gnn_w_10_1, L0_gnn_fc_w1, L0_gnn_fc_w2, L1_gnn_betas, L2_gnn_u, L2_gnn_W1, L2_gnn_b1, L2_gnn_W2, L2_gnn_b2, L3_gnn_W_edge, L3_gnn_b_edge, L3_gnn_W1, L3_gnn_b1, L3_gnn_W2, L3_gnn_b2, L3_gnn_eps, L3_gnn_gamma, L3_gnn_beta):
    import jax
    import jax.numpy as jnp

    def _L0_gnn_ref(node_in, edge_attr, edge_len_emb, w_00_0, w_11_0, w_01_1, w_10_1, fc_w1, fc_w2, edge_src, edge_dst):
        import jax, jax.numpy as jnp
        import numpy as np
        MUL = 64
        N_NODES = 50000
        N_EDGES = 25000
        NUM_NEIGHBORS = 16.0
        SILU_NORM = 1.679177
        src = node_in[edge_src]
        s0 = src[:, :MUL]
        s1 = src[:, MUL:].reshape(-1, MUL, 3)
        a0 = edge_attr[:, 0:1]
        a1 = edge_attr[:, 1:4]
        alpha = np.float32(1.0 / np.sqrt(2.0 * MUL))
        inv_sqrt3 = np.float32(1.0 / np.sqrt(3.0))
        out0 = alpha * (jnp.einsum('ei,io->eo', s0 * a0, w_00_0) + inv_sqrt3 * jnp.einsum('eim,em,io->eo', s1, a1, w_11_0))
        out1 = alpha * (jnp.einsum('ei,io,em->eom', s0, w_01_1, a1) + jnp.einsum('eim,io->eom', s1 * a0[:, :, None], w_10_1))
        msg_ang = jnp.concatenate([out0, out1.reshape(-1, 3 * MUL)], axis=1)
        h = jax.nn.silu(edge_len_emb @ fc_w1 / np.float32(np.sqrt(10.0))) * np.float32(SILU_NORM)
        msg_rad = h @ fc_w2 / np.float32(np.sqrt(64.0))
        messages = msg_ang * msg_rad
        agg = jax.ops.segment_sum(messages, edge_dst, num_segments=node_in.shape[0])
        return agg / np.float32(np.sqrt(NUM_NEIGHBORS))

    def _L1_gnn_ref(feats, src, dst, betas):
        import jax, jax.numpy as jnp
        import numpy as np
        N_NODES = 10000
        N_EDGES = 10000
        D_FEAT = 256
        N_LAYERS = 4
        EPS = 1e-16

        def _agnn_layer(h, src, dst, beta, num_nodes):
            h_norm = h * jax.lax.rsqrt(jnp.sum(h * h, axis=-1, keepdims=True) + EPS)
            cos = jnp.sum(h_norm[src] * h_norm[dst], axis=-1)
            logits = beta * cos
            m = jax.ops.segment_max(logits, dst, num_segments=num_nodes)
            ex = jnp.exp(logits - m[dst])
            denom = jax.ops.segment_sum(ex, dst, num_segments=num_nodes)
            alpha = ex / (denom[dst] + EPS)
            msg = alpha[:, None] * h[src]
            return jax.ops.segment_sum(msg, dst, num_segments=num_nodes)
        h = feats
        num_nodes = feats.shape[0]
        for i in range(N_LAYERS):
            h = _agnn_layer(h, src, dst, betas[i], num_nodes)
            h = jax.nn.relu(h)
        return h

    def _L2_gnn_ref(x, edge_index, edge_attr, u, batch, W1, b1, W2, b2):
        import jax, jax.numpy as jnp
        import numpy as np
        N_NODES = 50000
        N_EDGES = 25000
        NODE_IN = 256
        EDGE_OUT = 64
        GLOBAL_IN = 128
        NODE_OUT = 256
        HIDDEN = 512
        N_GRAPHS = 64
        n = x.shape[0]
        src = edge_index[0]
        sums = jax.ops.segment_sum(edge_attr, src, num_segments=n)
        counts = jax.ops.segment_sum(jnp.ones((edge_attr.shape[0],), edge_attr.dtype), src, num_segments=n)
        edge_attr_agg = sums / jnp.maximum(counts, 1.0)[:, None]
        u_expanded = u[batch]
        combined = jnp.concatenate([x, edge_attr_agg, u_expanded], axis=1)
        h = jax.nn.relu(combined @ W1 + b1)
        return h @ W2 + b2

    def _L3_gnn_ref(x, edge_index, edge_attr, W_edge, b_edge, W1, b1, W2, b2, eps, gamma, beta):
        import jax, jax.numpy as jnp
        import numpy as np
        N_NODES = 50000
        N_EDGES = 25000
        IN_DIM = 256
        OUT_DIM = 256
        EDGE_DIM = 128
        BN_EPS = 1e-05
        src, dst = (edge_index[0], edge_index[1])
        e = edge_attr @ W_edge + b_edge
        msg = jax.nn.relu(x[src] + e)
        agg = jax.ops.segment_sum(msg, dst, num_segments=x.shape[0])
        h = (1.0 + eps) * x + agg
        h = jax.nn.relu(h @ W1 + b1) @ W2 + b2
        mean = jnp.mean(h, axis=0)
        var = jnp.var(h, axis=0)
        h = (h - mean) * jax.lax.rsqrt(var + BN_EPS) * gamma + beta
        return jax.nn.relu(h)
    edge_index = jnp.stack([src, dst])
    batch0 = jnp.zeros((3125,), jnp.int32)
    x = _layernorm(x + _L0_gnn_ref(x, edge_attr_4, edge_attr_10, L0_gnn_w_00_0, L0_gnn_w_11_0, L0_gnn_w_01_1, L0_gnn_w_10_1, L0_gnn_fc_w1, L0_gnn_fc_w2, src, dst), axis=-1)
    x = _layernorm(x + _L1_gnn_ref(x, src, dst, L1_gnn_betas), axis=-1)
    x = _layernorm(x + _L2_gnn_ref(x, edge_index, edge_attr_64, L2_gnn_u, batch0, L2_gnn_W1, L2_gnn_b1, L2_gnn_W2, L2_gnn_b2), axis=-1)
    x = _layernorm(x + _L3_gnn_ref(x, edge_index, edge_attr_128, L3_gnn_W_edge, L3_gnn_b_edge, L3_gnn_W1, L3_gnn_b1, L3_gnn_W2, L3_gnn_b2, L3_gnn_eps, L3_gnn_gamma, L3_gnn_beta), axis=-1)
    return x

_drawn_inputs = setup_inputs


def setup_inputs(seed=0):
    import zlib

    import numpy as np

    out = dict(_drawn_inputs(seed))
    spreads = {'L1_gnn_betas': (1.0, 0.6),
     'L2_gnn_b1': (0.0, 0.1),
     'L2_gnn_b2': (0.0, 0.1),
     'L3_gnn_b_edge': (0.0, 0.1),
     'L3_gnn_b1': (0.0, 0.529),
     'L3_gnn_b2': (0.0, 0.8),
     'L3_gnn_gamma': (1.0, 0.2),
     'L3_gnn_beta': (0.0, 0.1)}
    factors = {}
    for name, (base, spread) in spreads.items():
        noise = np.random.default_rng([zlib.crc32(name.encode()), seed]).standard_normal(out[name].shape)
        drawn = base * np.exp(spread * noise) if base else spread * noise
        out[name] = jnp.asarray(drawn.astype(out[name].dtype))
    for name, factor in factors.items():
        out[name] = (out[name] * factor).astype(out[name].dtype)
    return out
```

```python
import math
from contextlib import ExitStack

import concourse.bass as bass
from concourse import mybir

F32 = mybir.dt.float32
F16 = mybir.dt.float16
I32 = mybir.dt.int32
ALU = mybir.AluOpType
ACT = mybir.ActivationFunctionType
AX = mybir.AxisListType

P = 128
N = 3125
E = 50000
D = 256
MUL = 64
W = -(-N // P)
NPAD = W * P
TAIL = N - (W - 1) * P
STEPS = -(-E // P) + W
EP = STEPS * P
PAD_ID = 16384
CELLS = NPAD * NPAD
TROWS = NPAD + P
TABLES = 4
RING = 4
UNROLL = 8
ITERS = STEPS // UNROLL
NO_EDGE = -1.0e30
SC = 400
NSC = NPAD // SC
SN = 1024.0
GROUPS = [(g, min(4, W - g)) for g in range(0, W, 4)]
HID = 512


class Tally:

    def __init__(self, sem, base):
        self.sem, self.n = sem, base

    def link(self, eng, ins):
        ins.then_inc(self.sem, 1)
        self.n = self.n + 1
        eng.wait_ge(self.sem, self.n)


def wait_pos(eng, sem, value):
    if not (isinstance(value, int) and value <= 0):
        eng.wait_ge(sem, value)


def window(t, w):
    return t[:, bass.ds(w, 1), :].rearrange("p w d -> p (w d)")


def for_pairs(eng, body):
    body(0, 0)
    body(1, 1)
    with eng.Fori(1, (W - 1) // 2) as i:
        body(i * 2, 0)
        body(i * 2 + 1, 1)


class Program:
    def __init__(self, nc, ctx, io):
        self.nc, self.ctx, self.io = nc, ctx, io
        self.sems = []
        self.ps = ctx.enter_context(nc.psum_tensor("ps", [P, 8, 512], F32))
        self.X = self.sb(ctx, "X", [P, W, D])
        self.iota = self.sb(ctx, "iota", [P, P])
        self.lower = self.sb(ctx, "lower", [P, P])
        self.ident = self.sb(ctx, "ident", [P, P])
        self.ident16 = self.sb(ctx, "ident16", [P, P], F16)
        self.part = self.sb(ctx, "part", [P, 1])
        self.win_col = self.sb(ctx, "win_col", [P, STEPS])
        self.win = self.sb(ctx, "win", [P, STEPS], I32)
        self.off = self.sb(ctx, "off", [P, STEPS], I32)

    def sb(self, ctx, name, shape, dt=F32):
        return ctx.enter_context(self.nc.sbuf_tensor(name, shape, dt))

    def sem(self, name):
        self.sems.append(self.nc.alloc_semaphore(name=name))
        return self.sems[-1]

    def end_stage(self):
        self.nc.clear_and_free_semaphores(self.sems)
        self.sems = []
        self.nc.all_engine_barrier()

    def setup(self):
        nc, io = self.nc, self.io
        loaded, zeroed = self.sem("su_loaded"), self.sem("su_zeroed")
        consts, chain, sums, zero_ready = self.sem("su_consts"), self.sem("su_chain"), self.sem("su_sums"), self.sem("su_zero_ready")
        part_ready, xpad = self.sem("su_part"), self.sem("su_xpad")
        pchain = self.sem("su_pchain")
        ZC = 8192
        with ExitStack() as ctx:
            sb = lambda name, shape, dt=F32: self.sb(ctx, name, shape, dt)
            zeros = sb("zeros", [P, ZC])
            ones = sb("ones", [P, P])
            dst_all = sb("dst_all", [P, STEPS], I32)
            dstf = sb("dstf", [P, STEPS])
            junk = sb("junk", [P, STEPS])
            step_no = sb("step_no", [P, STEPS])
            below = sb("below", [P, W + 1])
            start = sb("start", [P, W + 1])
            edges = sb("edges", [P, W])
            tiles_i = sb("tiles_i", [P, W], I32)
            tiles = sb("tiles", [P, W])
            first_step = sb("first_step", [P, W + 1])
            zero_w = sb("zero_w", [P, W])
            shift = sb("shift", [P, W])
            jump = sb("jump", [P, W])
            wsum = sb("wsum", [P, STEPS])
            osum = sb("osum", [P, STEPS])
            block = ctx.enter_context(nc.Block())

            @block.sync
            def _(sp):
                sp.dma_start(dst_all[:, :], io["dst_t"]).then_inc(loaded, 16)
                sp.wait_ge(xpad, 1)
                sp.dma_start(self.X[:, 0:W - 1, :],
                             io["x"][0:(W - 1) * P, :].rearrange("(w p) d -> p w d", p=P)).then_inc(loaded, 16)
                sp.dma_start(self.X[0:TAIL, W - 1, :], io["x"][(W - 1) * P:N, :]).then_inc(loaded, 16)
                sp.wait_ge(zero_ready, 1)
                flat = io["counts"][0:CELLS, :].rearrange("(k p f) o -> k p (f o)", p=P, f=3200)
                rounds = CELLS // (P * 3200)
                for k in range(rounds):
                    sp.dma_start(flat[k], zeros[:, 0:3200]).then_inc(zeroed, 16)
                sp.dma_start(io["sums"].rearrange("(p r) c -> p (r c)", p=P),
                             zeros[:, 0:TABLES * TROWS * 65 // P]).then_inc(zeroed, 16)
                sp.wait_ge(zeroed, 16 * (rounds + 1))
                sp.wait_ge(loaded, 48)

            @block.gpsimd
            def _(pool):
                nc.gpsimd.memset(zeros[:], 0.0).then_inc(zero_ready, 1)
                nc.gpsimd.iota(self.iota[:], [[1, P]], base=0, channel_multiplier=0,
                               allow_small_or_imprecise_dtypes=True)
                nc.gpsimd.iota(step_no[:], [[1, STEPS]], base=0, channel_multiplier=0,
                               allow_small_or_imprecise_dtypes=True)
                nc.gpsimd.iota(self.part[:], [[1, 1]], base=0, channel_multiplier=1,
                               allow_small_or_imprecise_dtypes=True)
                nc.gpsimd.memset(ones[:], 1.0).then_inc(pchain, 1)
                pool.wait_ge(pchain, 1)
                nc.gpsimd.affine_select(self.lower[:], ones[:], [[-1, P]], ALU.is_gt, 0.0, base=0,
                                        channel_multiplier=1)
                nc.gpsimd.affine_select(self.ident[:], ones[:], [[-1, P]], ALU.is_equal, 0.0, base=0,
                                        channel_multiplier=1).then_inc(pchain, 1)
                pool.wait_ge(pchain, 2)
                nc.gpsimd.tensor_copy(self.ident16[:], self.ident[:]).then_inc(consts, 1)

            @block.vector
            def _(dve):
                t = Tally(chain, 0)
                nc.vector.memset(self.X[:, W - 1, :], 0.0).then_inc(xpad, 1)
                nc.vector.memset(below[:, 0:1], 0.0)
                nc.vector.memset(zero_w[:], 0.0)
                dve.wait_ge(loaded, 16)
                dve.wait_ge(loaded, 48)
                t.link(dve, nc.vector.tensor_copy(dstf[:], dst_all[:]))
                for w in range(1, W + 1):
                    t.link(dve, nc.vector.tensor_scalar(junk[:], dstf[:], float(w * P), 0.0, ALU.is_lt,
                                                        ALU.add, accum_out=below[:, w:w + 1]))
                dve.sem_inc(part_ready, 1)
                dve.wait_ge(sums, 1)
                t.link(dve, nc.vector.tensor_copy(start[:], self.ps[:, 0, 0:W + 1]))
                t.link(dve, nc.vector.tensor_tensor(edges[:], start[:, 1:W + 1], start[:, 0:W], ALU.subtract))
                t.link(dve, nc.vector.tensor_scalar(tiles_i[:], edges[:], float(P - 1), None, ALU.add))
                t.link(dve, nc.vector.tensor_scalar(tiles_i[:], tiles_i[:], 7, None, ALU.arith_shift_right))
                t.link(dve, nc.vector.tensor_copy(tiles[:], tiles_i[:]))
                t.link(dve, nc.vector.memset(first_step[:, 0:1], 0.0))
                t.link(dve, nc.vector.tensor_tensor_scan(first_step[:, 1:W + 1], zero_w[:], tiles[:], 0.0,
                                                         ALU.add, ALU.add))
                t.link(dve, nc.vector.scalar_tensor_tensor(shift[:], first_step[:, 0:W], -float(P), start[:, 0:W],
                                                           ALU.mult, ALU.add))
                t.link(dve, nc.vector.tensor_tensor(jump[:, 1:W], shift[:, 1:W], shift[:, 0:W - 1], ALU.subtract))
                dve.wait_ge(consts, 1)
                nc.vector.memset(wsum[:], 0.0)
                t.link(dve, nc.vector.tensor_scalar(osum[:], step_no[:], float(P), None, ALU.mult))
                for w in range(1, W):
                    t.link(dve, nc.vector.scalar_tensor_tensor(wsum[:], step_no[:], first_step[:, w:w + 1],
                                                               wsum[:], ALU.is_ge, ALU.add))
                    t.link(dve, nc.vector.tensor_scalar(junk[:], step_no[:], first_step[:, w:w + 1],
                                                        jump[:, w:w + 1], ALU.is_ge, ALU.mult))
                    t.link(dve, nc.vector.tensor_tensor(osum[:], osum[:], junk[:], ALU.add))
                nc.vector.tensor_copy(self.win[:], wsum[:])
                nc.vector.tensor_copy(self.off[:], osum[:])
                nc.vector.tensor_scalar(self.win_col[:], wsum[:], float(P), None, ALU.mult)

            @block.tensor
            def _(pe):
                pe.wait_ge(consts, 1)
                pe.wait_ge(part_ready, 1)
                nc.tensor.matmul(self.ps[:, 0, 0:W + 1], ones[:], below[:], start=True,
                                 stop=True).then_inc(sums, 1)

    def layer0_edges(self, ACC):
        nc, io, ps = self.nc, self.io, self.ps
        ld = [self.sem(f"a_edges_in{k}") for k in range(RING)]
        xg = [self.sem(f"a_rows_in{k}") for k in range(RING)]
        ldc = [self.sem(f"a_ids_in{c}") for c in range(2)]
        once = self.sem("a_once")
        hid_ready, silu_ready, rad_ready = self.sem("a_hid"), self.sem("a_silu"), self.sem("a_rad")
        weighted, summed, added = self.sem("a_weighted"), self.sem("a_summed"), self.sem("a_added")
        ids_used, pairs_ready, pairs_done = self.sem("a_ids_used"), self.sem("a_pairs_ready"), self.sem("a_pairs_done")
        chain, keys, tick, acc0 = self.sem("a_chain"), self.sem("a_keys"), self.sem("a_tick"), self.sem("a_acc0")
        with ExitStack() as ctx:
            sb = lambda name, shape, dt=F32: self.sb(ctx, name, shape, dt)
            sd = sb("sd", [P, RING, 2], I32)
            attr = sb("attr", [P, RING, 4])
            emb = sb("emb", [10, RING, P])
            rows = sb("rows", [P, RING, D])
            fc1, fc2 = sb("fc1", [10, 64]), sb("fc2", [64, 1])
            hid = sb("hid", [64, 2, P])
            dl = sb("dl", [P, RING])
            ra = sb("ra", [P, RING, 4])
            oh = sb("oh", [P, RING, 4, P])
            ids = sb("ids", [P, 2, 2, 4 * P], I32)
            pair = sb("pair", [P, 2, 4 * P])
            key = sb("key", [P, STEPS])
            spare = sb("spare", [P, STEPS])
            kt = sb("kt", [P, 2, STEPS], I32)
            junk = sb("junk_a", [P, 2, 4, P])
            cnt = sb("cnt", [P, 2, 4])
            earlier = sb("earlier", [P, 2, 4])
            skip = sb("skip", [P, 2, 4])
            cellf = sb("cellf", [P, 2, 4])
            dump = sb("dump", [P, 1])
            cell = sb("cell", [P, 2, 4], I32)
            block = ctx.enter_context(nc.Block())

            def acc_ps(s2):
                return ps[:, 2 + s2, :]

            @block.sync
            def _(sp):
                sp.dma_start(fc1[:], io["fc_w1"]).then_inc(once, 16)
                sp.dma_start(fc2[:], io["fc_w2"]).then_inc(once, 16)
                sp.dma_start(kt[:, 0, :], io["src_t"]).then_inc(once, 16)
                sp.dma_start(kt[:, 1, :], io["dst_t"]).then_inc(once, 16)

                def body(i):
                    for j in range(UNROLL):
                        s, k = i * UNROLL + j, j % RING
                        if j % 4 == 0:
                            c = j // 4
                            q = (i * 2 + c) * 4 * P
                            wait_pos(sp, ids_used, i * 2 + c - 1)
                            for h in range(2):
                                sp.dma_start(ids[:, c, h, :], io["ids"][h:h + 1, bass.ds(q, 4 * P)]
                                             .to_broadcast([P, 4 * P])).then_inc(ldc[c], 16)
                        wait_pos(sp, summed, s - RING + 1)
                        o = sp.value_load(self.off[0:1, bass.ds(s, 1)], min_val=0, max_val=EP - P)
                        sp.dma_start(sd[:, k, :], io["sd"][bass.ds(o, P), :]).then_inc(ld[k], 16)
                        sp.dma_start(attr[:, k, :], io["attr4"][bass.ds(o, P), :]).then_inc(ld[k], 16)
                        sp.dma_start(emb[:, k, :], io["emb"][:, bass.ds(o, P)]).then_inc(ld[k], 16)

                body(0)
                with sp.Fori(1, ITERS) as i:
                    body(i)

            @block.gpsimd
            def _(pool):
                def body(i):
                    for j in range(UNROLL):
                        s, k = i * UNROLL + j, j % RING
                        pool.wait_ge(ld[k], 48 * (i * 2 + j // 4 + 1))
                        pool.sem_inc(tick, 1)
                        pool.indirect_dma_start(
                            out=rows[:, k, :], out_offset=None, in_=io["x"],
                            in_offset=bass.IndirectOffsetOnAxis(ap=sd[:, k, 0:1], axis=0)).then_inc(xg[k], 16)
                        if j % 4 == 0:
                            pool.wait_ge(pairs_ready, i * 2 + j // 4 + 1)
                            pool.sem_inc(tick, 1)
                        if not (isinstance(s, int) and s == 0):
                            pool.wait_ge(pairs_done, s * 16)
                            pool.sem_inc(tick, 1)
                        c, t = j // 4, j % 4
                        pool.indirect_dma_start(
                            out=io["counts"], out_offset=bass.IndirectOffsetOnAxis(ap=cell[:, c, t:t + 1], axis=0),
                            in_=cnt[:, c, t:t + 1], in_offset=None,
                            compute_op=ALU.add).then_inc(pairs_done, 16)

                body(0)
                with pool.Fori(1, ITERS) as i:
                    body(i)
                pool.wait_ge(pairs_done, 16 * STEPS)

            @block.scalar
            def _(act):
                def body(i):
                    for j in range(UNROLL):
                        s = i * UNROLL + j
                        act.wait_ge(hid_ready, s + 1)
                        wait_pos(act, rad_ready, s - 1)
                        nc.scalar.activation(hid[:, j % 2, :], ps[0:64, 0, (j % 2) * P:(j % 2 + 1) * P], ACT.Silu,
                                             scale=1.0 / math.sqrt(10.0)).then_inc(silu_ready, 1)

                body(0)
                with act.Fori(1, ITERS) as i:
                    body(i)

            @block.tensor
            def _(pe):
                pe.wait_ge(once, 64)

                def hidden(i, j):
                    s = i * UNROLL + j
                    k = j % RING
                    pe.wait_ge(ld[k], 48 * (i * 2 + (j // 4) + 1))
                    wait_pos(pe, silu_ready, s - 1)
                    nc.tensor.matmul(ps[0:64, 0, (j % 2) * P:(j % 2 + 1) * P], fc1[:], emb[:, k, :], start=True,
                                     stop=True).then_inc(hid_ready, 1)

                def radial(i, j):
                    s = i * UNROLL + j
                    pe.wait_ge(silu_ready, s + 1)
                    nc.tensor.matmul(ps[:, 1, j % RING:j % RING + 1], hid[:, j % 2, :], fc2[:], start=True,
                                     stop=True).then_inc(rad_ready, 1)

                def body(i, last=False):
                    for j in range(UNROLL):
                        s, k = i * UNROLL + j, j % RING
                        nxt = (i, j + 1) if j + 1 < UNROLL else (i + 1, 0)
                        more = not (last and j + 1 == UNROLL)
                        if more:
                            hidden(*nxt)
                        pe.wait_ge(xg[k], 16 * (i * 2 + j // 4 + 1))
                        pe.wait_ge(weighted, s + 1)
                        wait_pos(pe, added, s - 1)
                        out = acc_ps(j % 2).rearrange("p (c h m) -> p c h m", c=4, h=2)
                        xs = rows[:, k, :]
                        x1 = xs[:, MUL:D].rearrange("p (i m) -> p m i", m=3)
                        nc.tensor.matmul(out[:, 0, 0, :], oh[:, k, 0, :], xs[:, 0:MUL], start=True, stop=False,
                                         skip_group_check=True)
                        nc.tensor.matmul(out[:, 1:4, 1, :], oh[:, k, 0, :], x1, start=False, stop=False,
                                         skip_group_check=True)
                        for m in range(3):
                            nc.tensor.matmul(out[:, m + 1, 0, :], oh[:, k, m + 1, :], xs[:, 0:MUL], start=False,
                                             stop=False, skip_group_check=True)
                            last_mm = nc.tensor.matmul(out[:, 0, 1, :], oh[:, k, m + 1, :], x1[:, m, :], start=False,
                                                       stop=m == 2, skip_group_check=True)
                        last_mm.then_inc(summed, 1)
                        if more:
                            radial(*nxt)

                hidden(0, 0)
                radial(0, 0)
                body(0)
                with pe.Fori(1, ITERS - 1) as i:
                    body(i)
                body(ITERS - 1, last=True)

            @block.vector
            def _(dve):
                LINKS = UNROLL + 2 * 3
                nc.vector.memset(ACC[:], 0.0).then_inc(acc0, 1)
                dve.wait_ge(once, 64)
                nc.vector.scalar_tensor_tensor(key[:], kt[:, 1, :], float(NPAD), kt[:, 0, :], ALU.mult,
                                               ALU.add).then_inc(keys, 1)
                dve.wait_ge(keys, 1)
                nc.vector.tensor_scalar(spare[:], key[:], float(CELLS), None, ALU.is_ge).then_inc(keys, 1)
                nc.vector.tensor_scalar(dump[:], self.part[:], float(CELLS), None, ALU.add).then_inc(keys, 1)
                dve.wait_ge(keys, 3)
                dve.wait_ge(acc0, 1)

                def add(i, j):
                    s = i * UNROLL + j
                    w = dve.value_load(self.win[0:1, bass.ds(s, 1)], min_val=0, max_val=W - 1)
                    dve.wait_ge(summed, s + 1)
                    wait_pos(dve, added, s)
                    a = ACC[:, bass.ds(w * 512, 512)]
                    nc.vector.tensor_tensor(a, a, acc_ps(j % 2), ALU.add).then_inc(added, 1)

                def body(i, first=False):
                    t = Tally(chain, i * LINKS)
                    for j in range(UNROLL):
                        s, k = i * UNROLL + j, j % RING
                        if j % 4 == 0:
                            c = j // 4
                            dve.wait_ge(ldc[c], 32 * (i + 1))
                            wait_pos(dve, pairs_done, 16 * (i * UNROLL - UNROLL + 4 * c + 4) if not first else 0)
                            ins = nc.vector.scalar_tensor_tensor(pair[:, c, :], ids[:, c, 1, :], float(NPAD),
                                                                 ids[:, c, 0, :], ALU.mult, ALU.add)
                            ins.then_inc(ids_used, 1)
                            dve.wait_ge(ids_used, i * 2 + c + 1)
                            for q in range(4):
                                mine = key[:, bass.ds(i * UNROLL + 4 * c + q, 1)]
                                row = pair[:, c, q * P:(q + 1) * P]
                                nc.vector.tensor_scalar(junk[:, 0, q, :], row, mine, 0.0, ALU.is_equal, ALU.add,
                                                        accum_out=cnt[:, c, q:q + 1])
                                last = nc.vector.scalar_tensor_tensor(junk[:, 1, q, :], row, mine, self.lower[:],
                                                                      ALU.is_equal, ALU.mult,
                                                                      accum_out=earlier[:, c, q:q + 1])
                            t.link(dve, last)
                            mine = key[:, bass.ds(i * UNROLL + 4 * c, 4)]
                            t.link(dve, nc.vector.scalar_tensor_tensor(
                                skip[:, c, :], earlier[:, c, :], 0.5, spare[:, bass.ds(i * UNROLL + 4 * c, 4)],
                                ALU.is_gt, ALU.max))
                            t.link(dve, nc.vector.scalar_tensor_tensor(cellf[:, c, :], skip[:, c, :], 0.0, mine,
                                                                       ALU.is_equal, ALU.mult))
                            ins = nc.vector.scalar_tensor_tensor(cell[:, c, :], skip[:, c, :], dump[:],
                                                                 cellf[:, c, :], ALU.mult, ALU.add)
                            ins.then_inc(pairs_ready, 1)
                        dve.wait_ge(ld[k], 48 * (i * 2 + j // 4 + 1))
                        nc.vector.tensor_tensor(dl[:, k:k + 1], sd[:, k, 1:2], self.win_col[:, bass.ds(s, 1)],
                                                ALU.subtract)
                        dve.wait_ge(rad_ready, s + 1)
                        t.link(dve, nc.vector.tensor_scalar(ra[:, k, :], attr[:, k, :], ps[:, 1, k:k + 1], None,
                                                            ALU.mult))
                        for m in range(4):
                            last = nc.vector.tensor_scalar(oh[:, k, m, :], self.iota[:], dl[:, k:k + 1],
                                                           ra[:, k, m:m + 1], ALU.is_equal, ALU.mult)
                        last.then_inc(weighted, 1)
                        if not (first and j == 0):
                            add(*((i, j - 1) if j else (i - 1, UNROLL - 1)))

                body(0, first=True)
                with dve.Fori(1, ITERS) as i:
                    body(i)
                add(ITERS - 1, UNROLL - 1)

    def norm_end(self, ctx, tag, Y):
        nc = self.nc
        st = self.sb(ctx, tag + "_st", [P, W, 6])
        mv = self.sb(ctx, tag + "_mv", [P, W, 2])
        std = self.sb(ctx, tag + "_std", [P, W])
        epsc = self.sb(ctx, tag + "_eps", [P, 1])
        var_ready, std_ready = self.sem(tag + "_var"), self.sem(tag + "_stdr")
        rec_ready, written = self.sem(tag + "_rec"), self.sem(tag + "_norm")
        stats_ready = self.sem(tag + "_stats")

        def scalar_part(act):
            act.wait_ge(var_ready, 1)
            nc.scalar.activation(std[:], mv[:, :, 1], ACT.Sqrt, bias=epsc[:]).then_inc(std_ready, 1)

        def vector_begin(dve):
            nc.vector.memset(epsc[:], 1.0e-5).then_inc(rec_ready, 1)
            dve.wait_ge(rec_ready, 1)

        def vector_part(dve, summed, count):
            dve.wait_ge(summed, count)
            dve.sem_inc(stats_ready, 1)
            with dve.Fori(0, W) as w:
                nc.vector.bn_stats(window(st, w), window(Y, w)).then_inc(stats_ready, 1)
            dve.wait_ge(stats_ready, W + 1)
            for w in range(W):
                last = nc.vector.bn_aggr(mv[:, w, :], st[:, w, :])
            last.then_inc(var_ready, 1)
            dve.wait_ge(std_ready, 1)
            nc.vector.reciprocal(std[:], std[:]).then_inc(rec_ready, 1)
            dve.wait_ge(rec_ready, 2)

            with dve.Fori(0, W) as w:
                nc.vector.tensor_scalar(window(self.X, w), window(Y, w),
                                        mv[:, bass.ds(w, 1), 0:1].rearrange("p w d -> p (w d)"),
                                        std[:, bass.ds(w, 1)], ALU.subtract, ALU.mult).then_inc(written, 1)

        return scalar_part, vector_begin, vector_part, written

    def layer0_nodes(self, ACC):
        nc, io, ps = self.nc, self.io, self.ps
        loaded, scaled = self.sem("b_loaded"), self.sem("b_scaled")
        turned, moved, mixed, resid = self.sem("b_turned"), self.sem("b_moved"), self.sem("b_mixed"), self.sem("b_resid")
        staged = self.sem("b_staged")
        scale = 1.679177 / (math.sqrt(2.0 * MUL) * math.sqrt(64.0) * math.sqrt(16.0))
        with ExitStack() as ctx:
            wgt = self.sb(ctx, "wgt", [P, 2, MUL])
            stage = self.sb(ctx, "stage", [P, 2, 512])
            turn = self.sb(ctx, "turn", [P, 2, 512])
            Y = self.sb(ctx, "Yb", [P, W, D])
            scalar_part, vector_begin, vector_part, _ = self.norm_end(ctx, "bn", Y)
            block = ctx.enter_context(nc.Block())

            @block.sync
            def _(sp):
                sp.dma_start(wgt[0:MUL, 0, :], io["w_00_0"]).then_inc(loaded, 16)
                sp.dma_start(wgt[MUL:P, 0, :], io["w_11_0"]).then_inc(loaded, 16)
                sp.dma_start(wgt[0:MUL, 1, :], io["w_01_1"]).then_inc(loaded, 16)
                sp.dma_start(wgt[MUL:P, 1, :], io["w_10_1"]).then_inc(loaded, 16)

            @block.gpsimd
            def _(pool):
                def copy(w, k):
                    wait_pos(pool, turned, w - 1)
                    nc.gpsimd.tensor_copy(stage[:, k, :], ACC[:, bass.ds(w * 512, 512)]).then_inc(staged, 1)

                for_pairs(pool, copy)
                copy(W - 1, 0)

            @block.tensor
            def _(pe):
                pe.wait_ge(scaled, 1)

                def turn_window(w, k):
                    pe.wait_ge(staged, w + 1)
                    wait_pos(pe, moved, w - 1)
                    for c in range(4):
                        last = nc.tensor.transpose(ps[:, k, c * P:(c + 1) * P], stage[:, k, c * P:(c + 1) * P],
                                                   self.ident[:])
                    last.then_inc(turned, 1)

                def mix_window(w, k):
                    pe.wait_ge(moved, w + 1)
                    wait_pos(pe, resid, w - 1)
                    for c in range(4):
                        last = nc.tensor.matmul(ps[:, 2 + k, c * MUL:(c + 1) * MUL], turn[:, k, c * P:(c + 1) * P],
                                                wgt[:, min(c, 1), :], start=True, stop=True)
                    last.then_inc(mixed, 1)

                turn_window(0, 0)
                for_pairs(pe, lambda w, k: (turn_window(w + 1, 1 - k), mix_window(w, k)))
                mix_window(W - 1, 0)

            @block.scalar
            def _(act):
                act.wait_ge(loaded, 64)
                nc.scalar.mul(wgt[MUL:P, 0, :], wgt[MUL:P, 0, :], 1.0 / math.sqrt(3.0)).then_inc(scaled, 1)

                def move(w, k):
                    act.wait_ge(turned, w + 1)
                    wait_pos(act, mixed, w - 1)
                    nc.scalar.copy(turn[:, k, :], ps[:, k, :]).then_inc(moved, 1)

                for_pairs(act, move)
                move(W - 1, 0)
                scalar_part(act)

            @block.vector
            def _(dve):
                vector_begin(dve)

                def residual(w, k):
                    dve.wait_ge(mixed, w + 1)
                    y, x = window(Y, w), window(self.X, w)
                    nc.vector.scalar_tensor_tensor(y[:, 0:MUL], ps[:, 2 + k, 0:MUL], scale, x[:, 0:MUL], ALU.mult,
                                                   ALU.add)
                    ins = nc.vector.scalar_tensor_tensor(
                        y[:, MUL:D].rearrange("p (o m) -> p m o", m=3),
                        ps[:, 2 + k, MUL:D].rearrange("p (m o) -> p m o", m=3), scale,
                        x[:, MUL:D].rearrange("p (o m) -> p m o", m=3), ALU.mult, ALU.add)
                    ins.then_inc(resid, 1)

                for_pairs(dve, residual)
                residual(W - 1, 0)
                vector_part(dve, resid, W)

    def log_counts(self):
        nc, io = self.nc, self.io
        HALF = NPAD // 2
        cin = [self.sem(f"c_in{k}") for k in range(2)]
        cout = [self.sem(f"c_out{k}") for k in range(2)]
        clipped, logged, summed = self.sem("c_clipped"), self.sem("c_logged"), self.sem("c_summed")
        with ExitStack() as ctx:
            c = self.sb(ctx, "c_cnt", [P, 2, HALF])
            one = self.sb(ctx, "c_one", [P, 2, HALF])
            none = self.sb(ctx, "c_none", [P, 2, HALF])
            res = self.sb(ctx, "c_res", [P, 2, HALF])
            table = io["counts"][0:CELLS, :].rearrange("(w p f) o -> w p (f o)", p=P, f=NPAD)
            block = ctx.enter_context(nc.Block())

            def piece(i, k):
                return table[bass.ds(i, 1), :, k * HALF:(k + 1) * HALF].rearrange("w p f -> p (w f)")

            def loop(eng, body):
                body(0)
                with eng.Fori(1, W) as i:
                    body(i)

            @block.sync
            def _(sp):
                def body(i):
                    for k in range(2):
                        wait_pos(sp, clipped, 2 * i + k - 1)
                        sp.dma_start(c[:, k, :], piece(i, k)).then_inc(cin[k], 16)
                loop(sp, body)

            @block.vector
            def _(dve):
                def body(i):
                    for k in range(2):
                        dve.wait_ge(cin[k], 16 * (i + 1))
                        wait_pos(dve, summed, 2 * i + k - 1)
                        nc.vector.tensor_scalar(none[:, k, :], c[:, k, :], 0.0, NO_EDGE, ALU.is_equal, ALU.mult)
                        nc.vector.tensor_scalar(one[:, k, :], c[:, k, :], 1.0, None, ALU.max).then_inc(clipped, 1)
                    for k in range(2):
                        dve.wait_ge(logged, 2 * i + k + 1)
                        wait_pos(dve, cout[k], 16 * i)
                        nc.vector.tensor_tensor(res[:, k, :], none[:, k, :], one[:, k, :],
                                                ALU.add).then_inc(summed, 1)
                loop(dve, body)

            @block.scalar
            def _(act):
                def body(i):
                    for k in range(2):
                        act.wait_ge(clipped, 2 * i + k + 1)
                        nc.scalar.activation(one[:, k, :], one[:, k, :], ACT.Ln).then_inc(logged, 1)
                loop(act, body)

            @block.gpsimd
            def _(pool):
                def body(i):
                    for k in range(2):
                        pool.wait_ge(summed, 2 * i + k + 1)
                        pool.dma_start(piece(i, k), res[:, k, :]).then_inc(cout[k], 16)
                loop(pool, body)
                for k in range(2):
                    pool.wait_ge(cout[k], 16 * W)

    def attention(self, layer, H, out, T, HS, betas):
        nc, ps = self.nc, self.ps
        n = f"l{layer}_"
        squared, eps_added, rooted, inverted = (self.sem(n + x) for x in ("sq", "eps", "root", "inv"))
        scaled, turned, t_high, t_low = (self.sem(n + x) for x in ("scaled", "turned", "thigh", "tlow"))
        h_high, h_low = self.sem(n + "hhigh"), self.sem(n + "hlow")
        with ExitStack() as ctx:
            ss = self.sb(ctx, n + "ss", [P, W])
            junk = self.sb(ctx, n + "junk", [P, 2, D])
            hn = self.sb(ctx, n + "hn", [P, 2, D])
            block = ctx.enter_context(nc.Block())

            @block.scalar
            def _(act):
                def square(w, k):
                    wait_pos(act, squared, w - 1)
                    nc.scalar.activation(junk[:, k, :], window(H, w), ACT.Square,
                                         accum_out=ss[:, bass.ds(w, 1)]).then_inc(squared, 1)
                for_pairs(act, square)
                square(W - 1, 0)
                act.wait_ge(eps_added, 1)
                nc.scalar.activation(ss[:], ss[:], ACT.Sqrt).then_inc(rooted, 1)

                def parts(w, k):
                    nc.scalar.copy(window(HS[0], w), window(H, w)).then_inc(h_high, 1)
                    act.wait_ge(turned, w + 1)
                    nc.scalar.activation(T[0][:, :, bass.ds(w * P, P)],
                                         ps[:, k, 0:D].rearrange("p (t n) -> p t n", t=2), ACT.Copy,
                                         scale=SN).then_inc(t_high, 1)
                for_pairs(act, parts)
                parts(W - 1, 0)

            @block.gpsimd
            def _(pool):
                def low(w, k):
                    pool.wait_ge(h_high, w + 1)
                    nc.gpsimd.tensor_tensor(window(HS[1], w), window(H, w), window(HS[0], w),
                                            ALU.subtract).then_inc(h_low, 1)
                for_pairs(pool, low)
                low(W - 1, 0)

            @block.vector
            def _(dve):
                dve.wait_ge(squared, W)
                nc.vector.tensor_scalar(ss[:], ss[:], 1.0e-16, None, ALU.add).then_inc(eps_added, 1)
                dve.wait_ge(rooted, 1)
                nc.vector.reciprocal(ss[:], ss[:]).then_inc(inverted, 1)
                dve.wait_ge(inverted, 1)

                def scale(w, k):
                    wait_pos(dve, turned, w - 1)
                    nc.vector.tensor_scalar(hn[:, k, :], window(H, w), ss[:, bass.ds(w, 1)], None,
                                            ALU.mult).then_inc(scaled, 1)

                def low(w, k):
                    dve.wait_ge(t_high, w + 1)
                    part = bass.ds(w * P, P)
                    nc.vector.scalar_tensor_tensor(T[1][:, :, part],
                                                   ps[:, k, 0:D].rearrange("p (t n) -> p t n", t=2), SN,
                                                   T[0][:, :, part], ALU.mult, ALU.subtract).then_inc(t_low, 1)
                scale(0, 0)
                for_pairs(dve, lambda w, k: (scale(w + 1, 1 - k), low(w, k)))
                low(W - 1, 0)

            @block.tensor
            def _(pe):
                def turn(w, k):
                    pe.wait_ge(scaled, w + 1)
                    wait_pos(pe, t_low, w - 1)
                    for t in range(2):
                        last = nc.tensor.transpose(ps[:, k, t * P:(t + 1) * P], hn[:, k, t * P:(t + 1) * P],
                                                   self.ident[:])
                    last.then_inc(turned, 1)
                for_pairs(pe, turn)
                turn(W - 1, 0)

        log_in, scored, logits = (self.sem(n + x) for x in ("log_in", "scored", "logits"))
        max_ready, exp_ready, e_high, e_low = (self.sem(n + x) for x in ("max", "exp", "ehigh", "elow"))
        e_turned, moved_a, moved_v = (self.sem(n + x) for x in ("eturned", "moved_a", "moved_v"))
        mixed, done, chain = (self.sem(n + x) for x in ("mixed", "done", "chain"))
        BY_ACT = [True, True, True, False, True, False, True]
        A_MOVES, V_MOVES = sum(BY_ACT), len(BY_ACT) - sum(BY_ACT)
        G = len(GROUPS)
        with ExitStack() as ctx:
            lc = self.sb(ctx, n + "lc", [P, NPAD])
            L = self.sb(ctx, n + "L", [P, NPAD])
            Ex = self.sb(ctx, n + "E", [P, NPAD])
            parts = [self.sb(ctx, n + f"e{x}", [P, 2, NPAD], F16) for x in ("hi", "lo")]
            PT = self.sb(ctx, n + "PT", [P, W, 2, P], F16)
            mx, neg, den, rden = (self.sb(ctx, n + x, [P, 2]) for x in ("mx", "neg", "den", "rden"))
            table = self.io["counts"][0:CELLS, :].rearrange("(w p f) o -> w p (f o)", p=P, f=NPAD)
            block = ctx.enter_context(nc.Block())

            def bank16(g):
                return ps[:, 4 + g % 2, :].bitcast(F16)

            @block.sync
            def _(sp):
                def load(w, k):
                    wait_pos(sp, logits, NSC * w)
                    sp.dma_start(lc[:], table[bass.ds(w, 1), :, :].rearrange("w p f -> p (w f)")).then_inc(log_in, 16)
                for_pairs(sp, load)
                load(W - 1, 0)

            @block.tensor
            def _(pe):
                def scores(w):
                    for c in range(NSC):
                        wait_pos(pe, logits, NSC * w + c - 3)
                        cols = slice(c * SC, (c + 1) * SC)
                        q = bass.ds(w * P, P)
                        for t in range(2):
                            for a, b in ((0, 0), (0, 1), (1, 0)):
                                last = nc.tensor.matmul(ps[:, c % 4, 0:SC], T[a][:, t, q], T[b][:, t, cols],
                                                        start=(t, a, b) == (0, 0, 0), stop=(t, a) == (1, 1))
                        last.then_inc(scored, 1)

                def turn(w, k, g):
                    t0, m = GROUPS[g]
                    for t in range(m):
                        for h in range(2):
                            last = nc.tensor.transpose(bank16(g)[:, (2 * t + h) * P:(2 * t + h + 1) * P],
                                                       parts[h][:, k, (t0 + t) * P:(t0 + t + 1) * P],
                                                       self.ident16[:])
                    last.then_inc(e_turned, 1)

                def mix(w, k):
                    pe.wait_ge(e_high, w + 1)
                    pe.wait_ge(e_low, w + 1)
                    wait_pos(pe, done, w - 1)
                    turn(w, k, 0)
                    for g, (t0, m) in enumerate(GROUPS):
                        if g + 1 < G:
                            turn(w, k, g + 1)
                        if BY_ACT[g]:
                            pe.wait_ge(moved_a, A_MOVES * w + sum(BY_ACT[:g + 1]))
                        else:
                            pe.wait_ge(moved_v, V_MOVES * w + g + 1 - sum(BY_ACT[:g + 1]))
                        for t in range(t0, t0 + m):
                            for a, b in ((0, 0), (0, 1), (1, 0)):
                                last = nc.tensor.matmul(ps[:, 6 + k, 0:D], PT[:, t, a, :], HS[b][:, t, :],
                                                        start=(t, a, b) == (0, 0, 0), stop=(t, a) == (W - 1, 1))
                    last.then_inc(mixed, 1)

                scores(0)
                for_pairs(pe, lambda w, k: (scores(w + 1), mix(w, k)))
                mix(W - 1, 0)

            def move(w, k, g):
                t0, m = GROUPS[g]
                return PT[:, t0:t0 + m, :, :].rearrange("p t h n -> p (t h n)"), bank16(g)[:, 0:m * 2 * P]

            @block.scalar
            def _(act):
                def moves(w, k, groups):
                    for g in groups:
                        act.wait_ge(e_turned, G * w + g + 1)
                        out_, in_ = move(w, k, g)
                        nc.scalar.copy(out_, in_).then_inc(moved_a, 1)

                def exps(w, k):
                    act.wait_ge(max_ready, w + 1)
                    wait_pos(act, e_low, w)
                    nc.scalar.activation(Ex[:], L[:], ACT.Exp, bias=neg[:, k:k + 1],
                                         accum_out=den[:, k:k + 1]).then_inc(exp_ready, 1)

                def high(w, k):
                    act.wait_ge(exp_ready, w + 1)
                    wait_pos(act, e_turned, G * (w - 1))
                    nc.scalar.copy(parts[0][:, k, :], Ex[:]).then_inc(e_high, 1)

                exps(0, 0)
                high(0, 0)
                for_pairs(act, lambda w, k: (moves(w, k, [0, 1, 2]), exps(w + 1, 1 - k), moves(w, k, [4]),
                                             high(w + 1, 1 - k), moves(w, k, [6])))
                moves(W - 1, 0, [0, 1, 2, 4, 6])

            @block.vector
            def _(dve):
                def logit(w, k):
                    dve.wait_ge(log_in, 16 * (w + 1))
                    wait_pos(dve, exp_ready, w)
                    for c in range(NSC):
                        cols = slice(c * SC, (c + 1) * SC)
                        dve.wait_ge(scored, NSC * w + c + 1)
                        nc.vector.scalar_tensor_tensor(L[:, cols], ps[:, c % 4, 0:SC], betas[:, layer:layer + 1],
                                                       lc[:, cols], ALU.mult, ALU.add).then_inc(logits, 1)
                    dve.wait_ge(logits, NSC * (w + 1))
                    t = Tally(chain, w * 3 - 2 if not isinstance(w, int) or w else 0)
                    t.link(dve, nc.vector.tensor_reduce(mx[:, k:k + 1], L[:], AX.X, ALU.max))
                    nc.vector.tensor_scalar(neg[:, k:k + 1], mx[:, k:k + 1], -1.0, None,
                                            ALU.mult).then_inc(max_ready, 1)

                def moves(w, k):
                    for g in (3, 5):
                        dve.wait_ge(e_turned, G * w + g + 1)
                        out_, in_ = move(w, k, g)
                        nc.vector.tensor_copy(out_, in_).then_inc(moved_v, 1)

                def low(w, k):
                    dve.wait_ge(e_high, w + 1)
                    wait_pos(dve, e_turned, G * (w - 1))
                    nc.vector.tensor_tensor(parts[1][:, k, :], Ex[:], parts[0][:, k, :],
                                            ALU.subtract).then_inc(e_low, 1)

                def finish(w, k):
                    t = Tally(chain, w * 3 + (1 if isinstance(w, int) and w == W - 1 else 2))
                    t.link(dve, nc.vector.reciprocal(rden[:, k:k + 1], den[:, k:k + 1]))
                    t.link(dve, nc.vector.scalar_tensor_tensor(rden[:, k:k + 1], mx[:, k:k + 1], 0.1 * NO_EDGE,
                                                               rden[:, k:k + 1], ALU.is_gt, ALU.mult))
                    dve.wait_ge(mixed, w + 1)
                    nc.vector.tensor_scalar(window(out, w), ps[:, 6 + k, 0:D], rden[:, k:k + 1], 0.0, ALU.mult,
                                            ALU.max).then_inc(done, 1)

                logit(0, 0)
                low(0, 0)
                for_pairs(dve, lambda w, k: (logit(w + 1, 1 - k), moves(w, k), low(w + 1, 1 - k), finish(w, k)))
                moves(W - 1, 0)
                finish(W - 1, 0)

    def load_betas(self, betas):
        nc = self.nc
        loaded, scaled = self.sem("beta_in"), self.sem("beta_scaled")
        with nc.Block() as block:
            @block.sync
            def _(sp):
                sp.dma_start(betas[:], self.io["betas"].to_broadcast([P, 4])).then_inc(loaded, 16)

            @block.vector
            def _(dve):
                dve.wait_ge(loaded, 16)
                nc.vector.tensor_scalar(betas[:], betas[:], 1.0 / (SN * SN), None, ALU.mult).then_inc(scaled, 1)

    def add_norm(self, tag, Z):
        nc = self.nc
        summed = self.sem(tag + "_summed")
        with ExitStack() as ctx:
            Y = self.sb(ctx, tag + "_Y", [P, W, D])
            scalar_part, vector_begin, vector_part, _ = self.norm_end(ctx, tag, Y)
            block = ctx.enter_context(nc.Block())

            @block.scalar
            def _(act):
                scalar_part(act)

            @block.vector
            def _(dve):
                vector_begin(dve)

                nc.vector.tensor_tensor(Y[:], self.X[:], Z[:], ALU.add).then_inc(summed, 1)
                vector_part(dve, summed, 1)

    def attribute_sums(self):
        nc, io, ps = self.nc, self.io, self.ps
        C = MUL + 1
        lda = [self.sem(f"s_attr_in{k}") for k in range(RING)]
        ldi = [self.sem(f"s_ids_in{c}") for c in range(2)]
        tab = [self.sem(f"s_table{k}") for k in range(TABLES)]
        once, consts, spared = self.sem("s_once"), self.sem("s_consts"), self.sem("s_spared")
        equal, merged, copied = self.sem("s_equal"), self.sem("s_merged"), self.sem("s_copied")
        placed, chain, tick, ids_used = self.sem("s_placed"), self.sem("s_chain"), self.sem("s_tick"), self.sem("s_used")
        with ExitStack() as ctx:
            sb = lambda name, shape, dt=F32: self.sb(ctx, name, shape, dt)
            attr = sb("s_attr", [P, RING, C])
            ids = sb("s_ids", [P, 2, 4 * P], I32)
            idf = sb("s_idf", [P, 2, 4 * P])
            src_i = sb("s_src_i", [P, STEPS], I32)
            srcf = sb("s_srcf", [P, STEPS])
            spare = sb("s_spare", [P, STEPS])
            base = sb("s_base", [P, TABLES])
            dump = sb("s_dump", [P, TABLES])
            home = sb("s_home", [P, 2, 4])
            same = sb("s_same", [P, RING, P])
            junk = sb("s_junk", [P, RING, P])
            earlier = sb("s_earlier", [P, 2, 4])
            skip = sb("s_skip", [P, 2, 4])
            keep = sb("s_keep", [P, 2, 4])
            spot = sb("s_spot", [P, 2, 4])
            place = sb("s_place", [P, 2, 4], I32)
            total = sb("s_total", [P, RING, C])
            block = ctx.enter_context(nc.Block())

            def loop(eng, body):
                body(0)
                with eng.Fori(1, ITERS) as i:
                    body(i)

            @block.sync
            def _(sp):
                sp.dma_start(src_i[:], io["src_t"]).then_inc(once, 16)

                def body(i):
                    for j in range(UNROLL):
                        s, k = i * UNROLL + j, j % RING
                        if j % 4 == 0:
                            c = j // 4
                            wait_pos(sp, ids_used, i * 2 + c - 1)
                            sp.dma_start(ids[:, c, :], io["ids"][0:1, bass.ds((i * 2 + c) * 4 * P, 4 * P)]
                                         .to_broadcast([P, 4 * P])).then_inc(ldi[c], 16)
                        wait_pos(sp, merged, s - RING + 1)
                        sp.dma_start(attr[:, k, 0:MUL],
                                     io["attr64"][bass.ds(s * P, P), :]).then_inc(lda[k], 16)
                loop(sp, body)

            @block.gpsimd
            def _(pool):
                nc.gpsimd.memset(attr[:, :, MUL:C], 1.0).then_inc(consts, 1)
                nc.gpsimd.iota(base[:], [[TROWS, TABLES]], base=0, channel_multiplier=0,
                               allow_small_or_imprecise_dtypes=True)
                nc.gpsimd.iota(dump[:], [[TROWS, TABLES]], base=NPAD, channel_multiplier=1,
                               allow_small_or_imprecise_dtypes=True).then_inc(consts, 1)

                def body(i):
                    for j in range(UNROLL):
                        s, k, c, t = i * UNROLL + j, j % RING, j // 4, j % 4
                        pool.wait_ge(copied, s + 1)
                        pool.sem_inc(tick, 1)
                        if t == 0:
                            pool.wait_ge(placed, i * 2 + c + 1)
                            pool.sem_inc(tick, 1)
                        if not (isinstance(i, int) and j < TABLES):
                            pool.wait_ge(tab[k], 16 * (i * 2 + c))
                            pool.sem_inc(tick, 1)
                        pool.indirect_dma_start(
                            out=io["sums"], out_offset=bass.IndirectOffsetOnAxis(ap=place[:, c, t:t + 1], axis=0),
                            in_=total[:, k, :], in_offset=None, compute_op=ALU.add).then_inc(tab[k], 16)
                loop(pool, body)
                for k in range(TABLES):
                    pool.wait_ge(tab[k], 16 * (STEPS // TABLES))

            @block.vector
            def _(dve):
                dve.wait_ge(once, 16)
                dve.wait_ge(consts, 2)
                nc.vector.tensor_copy(srcf[:], src_i[:]).then_inc(spared, 1)
                dve.wait_ge(spared, 1)
                nc.vector.tensor_scalar(spare[:], srcf[:], float(N), None, ALU.is_ge).then_inc(spared, 1)
                dve.wait_ge(spared, 2)
                LINKS = 2 * 3

                def body(i):
                    t = Tally(chain, i * LINKS)
                    for c in range(2):
                        dve.wait_ge(ldi[c], 16 * (i + 1))
                        nc.vector.tensor_copy(idf[:, c, :], ids[:, c, :]).then_inc(ids_used, 1)
                        dve.wait_ge(ids_used, i * 2 + c + 1)
                        for q in range(4):
                            mine = srcf[:, bass.ds(i * UNROLL + 4 * c + q, 1)]
                            row = idf[:, c, q * P:(q + 1) * P]
                            wait_pos(dve, merged, i * UNROLL + 4 * c + q - RING + 1)
                            nc.vector.tensor_scalar(same[:, q, :], row, mine, None, ALU.is_equal).then_inc(equal, 1)
                            last = nc.vector.scalar_tensor_tensor(junk[:, q, :], row, mine, self.lower[:],
                                                                  ALU.is_equal, ALU.mult,
                                                                  accum_out=earlier[:, c, q:q + 1])
                        t.link(dve, last)
                        cols = bass.ds(i * UNROLL + 4 * c, 4)
                        nc.vector.scalar_tensor_tensor(home[:, c, :], srcf[:, cols], 0.0, base[:], ALU.add, ALU.add)
                        t.link(dve, nc.vector.scalar_tensor_tensor(skip[:, c, :], earlier[:, c, :], 0.5,
                                                                   spare[:, cols], ALU.is_gt, ALU.max))
                        nc.vector.scalar_tensor_tensor(keep[:, c, :], skip[:, c, :], 0.0, home[:, c, :],
                                                       ALU.is_equal, ALU.mult)
                        t.link(dve, nc.vector.tensor_tensor(spot[:, c, :], skip[:, c, :], dump[:], ALU.mult))
                        if not (isinstance(i, int) and i == 0):
                            for k in range(TABLES):
                                dve.wait_ge(tab[k], 16 * (2 * i + c - 1))
                        nc.vector.tensor_tensor(place[:, c, :], spot[:, c, :], keep[:, c, :],
                                                ALU.add).then_inc(placed, 1)
                loop(dve, body)

            @block.tensor
            def _(pe):
                def body(i):
                    for j in range(UNROLL):
                        s, k = i * UNROLL + j, j % RING
                        pe.wait_ge(equal, s + 1)
                        pe.wait_ge(lda[k], 16 * (i * 2 + j // 4 + 1))
                        wait_pos(pe, copied, s - 1)
                        nc.tensor.matmul(ps[:, j % 2, 0:C], same[:, k, :], attr[:, k, :], start=True,
                                         stop=True).then_inc(merged, 1)
                loop(pe, body)

            @block.scalar
            def _(act):
                def body(i):
                    for j in range(UNROLL):
                        s, k = i * UNROLL + j, j % RING
                        act.wait_ge(merged, s + 1)
                        if not (isinstance(i, int) and j < RING):
                            act.wait_ge(tab[k], 16 * (i * 2 + j // 4))
                        nc.scalar.copy(total[:, k, :], ps[:, j % 2, 0:C]).then_inc(copied, 1)
                loop(act, body)

    def layer2_nodes(self):
        nc, io, ps = self.nc, self.io, self.ps
        C = MUL + 1
        KH = HID // P
        loaded, u_ready, bias_sum, bias_ready = (self.sem("g_" + x) for x in ("loaded", "u", "bsum", "bias"))
        tab_in, mean_ready, turned, moved = (self.sem("g_" + x) for x in ("tab", "mean", "turned", "moved"))
        hid_ready, hid_moved, o_ready, resid, chain, consts, staged = (self.sem("g_" + x) for x in (
            "hid", "hmoved", "o", "resid", "chain", "consts", "staged"))
        with ExitStack() as ctx:
            sb = lambda name, shape, dt=F32: self.sb(ctx, name, shape, dt)
            W1x = sb("W1x", [P, 2, HID])
            W1a = sb("W1a", [MUL, HID])
            W1u = sb("W1u", [P, HID])
            W2 = sb("W2", [P, KH, D])
            ucol = sb("ucol", [P, 1])
            b1 = sb("b1", [P, KH])
            bias = sb("bias", [P, KH])
            b2 = sb("b2", [1, D])
            ones = sb("g_ones", [1, P])
            tabs = sb("tabs", [P, 4, TABLES, C])
            pair = sb("g_pair", [P, 4, 2, C])
            summ = sb("g_sum", [P, 4, C])
            inv = sb("g_inv", [P, 4])
            mean = sb("g_mean", [P, 4, P])
            stage = sb("g_stage", [P, 4, D])
            xT = sb("xT", [P, 3, 4 * P])
            hid = sb("g_hidT", [P, KH, 4 * P])
            Y = sb("Yg", [P, W, D])
            scalar_part, vector_begin, vector_part, _ = self.norm_end(ctx, "gn", Y)
            sums = io["sums"].rearrange("(t r) c -> t r c", t=TABLES)
            block = ctx.enter_context(nc.Block())

            def loop(eng, body):
                body(0, 4)
                with eng.Fori(1, W // 4) as i:
                    body(i, 4)
                body(W // 4, W % 4)

            @block.sync
            def _(sp):
                sp.dma_start(W1x[:], io["W1"][0:D, :].rearrange("(t p) n -> p t n", p=P)).then_inc(loaded, 16)
                sp.dma_start(W1a[:], io["W1"][D:D + MUL, :]).then_inc(loaded, 16)
                sp.dma_start(W1u[:], io["W1"][D + MUL:D + MUL + P, :]).then_inc(loaded, 16)
                sp.dma_start(W2[:], io["W2"].rearrange("(t p) n -> p t n", p=P)).then_inc(loaded, 16)
                sp.dma_start(ucol[:], io["u"][0:1, :].rearrange("o p -> p o"),
                             allow_slow_non_contiguous=True).then_inc(loaded, 16)
                sp.dma_start(b1[:], io["b1"]).then_inc(loaded, 16)
                sp.dma_start(b2[:], io["b2"]).then_inc(loaded, 16)

                def body(i, m):
                    wait_pos(sp, mean_ready, i)
                    for w in range(m):
                        sp.dma_start(tabs[:, w, :, :],
                                     sums[:, bass.ds((i * 4 + w) * P, P), :].rearrange("t p c -> p t c")
                                     ).then_inc(tab_in, 16)
                loop(sp, body)

            @block.gpsimd
            def _(pool):
                def body(i, m):
                    wait_pos(pool, turned, 3 * i)
                    nc.gpsimd.tensor_copy(stage[:, 0:m, :], self.X[:, bass.ds(i * 4, m), :]).then_inc(staged, 1)
                loop(pool, body)

            @block.vector
            def _(dve):
                vector_begin(dve)
                nc.vector.memset(mean[:], 0.0)
                nc.vector.memset(ones[:], 1.0).then_inc(consts, 1)
                dve.wait_ge(consts, 1)
                dve.wait_ge(loaded, 112)
                dve.wait_ge(bias_sum, 1)
                nc.vector.tensor_tensor(bias[:], ps[:, 7, 0:KH], b1[:], ALU.add).then_inc(bias_ready, 1)

                def means(t, i, m):
                    dve.wait_ge(tab_in, 64 * i + 16 * m)
                    t.link(dve, nc.vector.tensor_tensor(pair[:, 0:m], tabs[:, 0:m, 0:2, :], tabs[:, 0:m, 2:4, :],
                                                        ALU.add))
                    t.link(dve, nc.vector.tensor_tensor(summ[:, 0:m], pair[:, 0:m, 0, :], pair[:, 0:m, 1, :],
                                                        ALU.add))
                    t.link(dve, nc.vector.tensor_scalar(inv[:, 0:m], summ[:, 0:m, MUL], 1.0, None, ALU.max))
                    t.link(dve, nc.vector.reciprocal(inv[:, 0:m], inv[:, 0:m]))
                    wait_pos(dve, moved, 3 * i)
                    for w in range(m):
                        last = nc.vector.tensor_scalar(mean[:, w, 0:MUL], summ[:, w, 0:MUL], inv[:, w:w + 1], None,
                                                       ALU.mult)
                    last.then_inc(mean_ready, 1)

                def body(i, m):
                    t = Tally(chain, i * 4)
                    means(t, i, m)
                    for w in range(m):
                        dve.wait_ge(o_ready, 4 * i + w + 1)
                        y = window(Y, 4 * i + w)
                        nc.vector.tensor_tensor(y, ps[:, 5 + w % 2, 0:D], window(self.X, 4 * i + w),
                                                ALU.add).then_inc(resid, 1)
                loop(dve, body)
                vector_part(dve, resid, W)

            @block.tensor
            def _(pe):
                pe.wait_ge(loaded, 112)
                pe.wait_ge(consts, 1)
                for t in range(KH):
                    last = nc.tensor.matmul(ps[:, 7, t:t + 1], W1u[:, t * P:(t + 1) * P], ucol[:], start=True,
                                            stop=True)
                last.then_inc(bias_sum, 1)

                def body(i, m):
                    n = m * P
                    pe.wait_ge(staged, i + 1)
                    for t in range(2):
                        for w in range(m):
                            last = nc.tensor.transpose(ps[:, t, w * P:(w + 1) * P],
                                                       stage[:, w, t * P:(t + 1) * P], self.ident[:])
                        last.then_inc(turned, 1)
                    pe.wait_ge(mean_ready, i + 1)
                    for w in range(m):
                        last = nc.tensor.transpose(ps[:, 2, w * P:(w + 1) * P], mean[:, w, :], self.ident[:])
                    last.then_inc(turned, 1)
                    pe.wait_ge(moved, 3 * i + 3)
                    for h in range(KH):
                        if h >= 2:
                            pe.wait_ge(hid_moved, KH * i + h - 1)
                        cols = slice(h * P, (h + 1) * P)
                        out = ps[:, 3 + h % 2, 0:n]
                        nc.tensor.matmul(out, W1x[:, 0, cols], xT[:, 0, 0:n], start=True, stop=False)
                        nc.tensor.matmul(out, W1x[:, 1, cols], xT[:, 1, 0:n], start=False, stop=False)
                        nc.tensor.matmul(out, W1a[:, cols], xT[0:MUL, 2, 0:n], start=False,
                                         stop=True).then_inc(hid_ready, 1)
                    pe.wait_ge(hid_moved, KH * (i + 1))
                    for w in range(m):
                        wait_pos(pe, resid, 4 * i + w - 1)
                        out = ps[:, 5 + w % 2, 0:D]
                        for h in range(KH):
                            nc.tensor.matmul(out, hid[:, h, w * P:(w + 1) * P], W2[:, h, :], start=h == 0, stop=False)
                        nc.tensor.matmul(out, ones[:], b2[:], start=False, stop=True).then_inc(o_ready, 1)
                loop(pe, body)

            @block.scalar
            def _(act):
                act.wait_ge(bias_ready, 1)

                def body(i, m):
                    n = m * P
                    wait_pos(act, o_ready, 4 * i)
                    for t in range(3):
                        rows = P if t < 2 else MUL
                        act.wait_ge(turned, 3 * i + t + 1)
                        nc.scalar.copy(xT[0:rows, t, 0:n], ps[0:rows, t, 0:n]).then_inc(moved, 1)
                    for h in range(KH):
                        act.wait_ge(hid_ready, KH * i + h + 1)
                        nc.scalar.activation(hid[:, h, 0:n], ps[:, 3 + h % 2, 0:n], ACT.Relu,
                                             bias=bias[:, h:h + 1]).then_inc(hid_moved, 1)
                loop(act, body)
                scalar_part(act)

    def layer3_edges(self, AGG):
        nc, io, ps = self.nc, self.io, self.ps
        ld = [self.sem(f"h_edges_in{k}") for k in range(RING)]
        xg = [self.sem(f"h_rows_in{k}") for k in range(RING)]
        once, biased, stored, zeroed = (self.sem("h_" + x) for x in ("once", "biased", "stored", "zeroed"))
        edge_ready, pre_ready, msg_ready, hot = (self.sem("h_" + x) for x in ("edge", "pre", "msg", "hot"))
        summed, added, chain, tick = (self.sem("h_" + x) for x in ("summed", "added", "chain", "tick"))
        with ExitStack() as ctx:
            sb = lambda name, shape, dt=F32: self.sb(ctx, name, shape, dt)
            We = sb("We", [P, D])
            be = sb("be", [P, D])
            XB = sb("XB", [P, W, D])
            sd = sb("h_sd", [P, RING, 2], I32)
            attr = sb("h_attr", [P, RING, P])
            rows = sb("h_rows", [P, RING, D])
            pre = sb("h_pre", [P, 2, D])
            msg = sb("h_msg", [P, RING, D])
            dl = sb("h_dl", [P, RING])
            oh = sb("h_oh", [P, RING, P])
            block = ctx.enter_context(nc.Block())

            @block.sync
            def _(sp):
                sp.dma_start(We[:], io["W_edge"]).then_inc(once, 16)
                sp.dma_start(be[:], io["b_edge"].to_broadcast([P, D])).then_inc(once, 16)
                sp.wait_ge(biased, W)
                sp.dma_start(io["rows3"].rearrange("(w p) d -> p w d", p=P), XB[:]).then_inc(stored, 16)

                def body(i):
                    for j in range(UNROLL):
                        s, k = i * UNROLL + j, j % RING
                        wait_pos(sp, summed, s - RING + 1)
                        o = sp.value_load(self.off[0:1, bass.ds(s, 1)], min_val=0, max_val=EP - P)
                        sp.dma_start(sd[:, k, :], io["sd"][bass.ds(o, P), :]).then_inc(ld[k], 16)
                        sp.dma_start(attr[:, k, :], io["attr128"][:, bass.ds(o, P)]).then_inc(ld[k], 16)
                body(0)
                with sp.Fori(1, ITERS) as i:
                    body(i)
                sp.wait_ge(stored, 16)

            @block.gpsimd
            def _(pool):
                pool.wait_ge(stored, 16)
                pool.sem_inc(tick, 1)

                def body(i):
                    for j in range(UNROLL):
                        k = j % RING
                        pool.wait_ge(ld[k], 32 * (i * 2 + j // 4 + 1))
                        pool.sem_inc(tick, 1)
                        pool.indirect_dma_start(
                            out=rows[:, k, :], out_offset=None, in_=io["rows3"],
                            in_offset=bass.IndirectOffsetOnAxis(ap=sd[:, k, 0:1], axis=0)).then_inc(xg[k], 16)
                body(0)
                with pool.Fori(1, ITERS) as i:
                    body(i)

            @block.tensor
            def _(pe):
                pe.wait_ge(once, 32)

                def edge(i, j):
                    s = i * UNROLL + j
                    pe.wait_ge(ld[j % RING], 32 * (i * 2 + j // 4 + 1))
                    wait_pos(pe, pre_ready, s - 1)
                    nc.tensor.matmul(ps[:, j % 2, 0:D], attr[:, j % RING, :], We[:], start=True,
                                     stop=True).then_inc(edge_ready, 1)

                def body(i, last=False):
                    for j in range(UNROLL):
                        s, k = i * UNROLL + j, j % RING
                        if not (last and j + 1 == UNROLL):
                            edge(*((i, j + 1) if j + 1 < UNROLL else (i + 1, 0)))
                        pe.wait_ge(msg_ready, s + 1)
                        pe.wait_ge(hot, s + 1)
                        wait_pos(pe, added, s - 1)
                        nc.tensor.matmul(ps[:, 2 + j % 2, 0:D], oh[:, k, :], msg[:, k, :], start=True,
                                         stop=True).then_inc(summed, 1)
                edge(0, 0)
                body(0)
                with pe.Fori(1, ITERS - 1) as i:
                    body(i)
                body(ITERS - 1, last=True)

            @block.scalar
            def _(act):
                def body(i):
                    for j in range(UNROLL):
                        s, k = i * UNROLL + j, j % RING
                        act.wait_ge(pre_ready, s + 1)
                        wait_pos(act, summed, s - RING + 1)
                        nc.scalar.activation(msg[:, k, :], pre[:, j % 2, :], ACT.Relu).then_inc(msg_ready, 1)
                body(0)
                with act.Fori(1, ITERS) as i:
                    body(i)

            @block.vector
            def _(dve):
                dve.wait_ge(once, 32)
                nc.vector.memset(AGG[:], 0.0).then_inc(zeroed, 1)
                with dve.Fori(0, W) as w:
                    nc.vector.tensor_tensor(window(XB, w), window(self.X, w), be[:], ALU.add).then_inc(biased, 1)
                dve.wait_ge(zeroed, 1)

                def add(i, j):
                    s = i * UNROLL + j
                    w = dve.value_load(self.win[0:1, bass.ds(s, 1)], min_val=0, max_val=W - 1)
                    dve.wait_ge(summed, s + 1)
                    wait_pos(dve, added, s)
                    a = window(AGG, w)
                    nc.vector.tensor_tensor(a, a, ps[:, 2 + j % 2, 0:D], ALU.add).then_inc(added, 1)

                def body(i, first=False):
                    t = Tally(chain, i * UNROLL)
                    for j in range(UNROLL):
                        s, k = i * UNROLL + j, j % RING
                        dve.wait_ge(ld[k], 32 * (i * 2 + j // 4 + 1))
                        t.link(dve, nc.vector.tensor_tensor(dl[:, k:k + 1], sd[:, k, 1:2],
                                                            self.win_col[:, bass.ds(s, 1)], ALU.subtract))
                        nc.vector.tensor_scalar(oh[:, k, :], self.iota[:], dl[:, k:k + 1], None,
                                                ALU.is_equal).then_inc(hot, 1)
                        dve.wait_ge(xg[k], 16 * (i * 2 + j // 4 + 1))
                        dve.wait_ge(edge_ready, s + 1)
                        wait_pos(dve, msg_ready, s - 1)
                        nc.vector.tensor_tensor(pre[:, j % 2, :], ps[:, j % 2, 0:D], rows[:, k, :],
                                                ALU.add).then_inc(pre_ready, 1)
                        if not (first and j == 0):
                            add(*((i, j - 1) if j else (i - 1, UNROLL - 1)))
                body(0, first=True)
                with dve.Fori(1, ITERS) as i:
                    body(i)
                add(ITERS - 1, UNROLL - 1)

    def layer3_nodes(self, AGG):
        nc, io, ps = self.nc, self.io, self.ps
        loaded, eps1, h_ready, turned, moved = (self.sem("i_" + x) for x in ("loaded", "eps1", "h", "turned", "moved"))
        z1, r1, z2, r2 = (self.sem("i_" + x) for x in ("z1", "r1", "z2", "r2"))
        chain, bvar, bstd, coef, act_done, back, resid = (self.sem("i_" + x) for x in (
            "chain", "bvar", "bstd", "coef", "act", "back", "resid"))
        stored, bn_eps = self.sem("i_stored"), self.sem("i_bneps")
        CH = [(c, min(512, N - c)) for c in range(0, N, 512)]
        with ExitStack() as ctx:
            sb = lambda name, shape, dt=F32: self.sb(ctx, name, shape, dt)
            V1, V2 = sb("V1", [P, 2, D]), sb("V2", [P, 2, D])
            c1, c2, gamma, beta = (sb("i_" + x, [P, 2]) for x in ("c1", "c2", "gamma", "beta"))
            eps = sb("i_eps", [P, 1])
            beps = sb("i_beps", [P, 1])
            stage = sb("i_stage", [P, 4 * D])
            zr = sb("zr", [P, 2, 2, P])
            hT = sb("hT", [P, 2, 512])
            gT = sb("gT", [P, 2, 512])
            Z = sb("Zi", [P, 2, NPAD])
            bst = sb("i_bst", [P, 2, len(CH), 6])
            bmv = sb("i_bmv", [P, 2, 2])
            bsd = sb("i_bsd", [P, 2])
            mul, shf = sb("i_mul", [P, 2]), sb("i_shf", [P, 2])
            Y = sb("Yi", [P, W, D])
            scalar_part, vector_begin, vector_part, written = self.norm_end(ctx, "last", Y)
            block = ctx.enter_context(nc.Block())

            def loop(eng, body):
                body(0, 4)
                with eng.Fori(1, W // 4) as i:
                    body(i, 4)
                body(W // 4, W % 4)

            @block.sync
            def _(sp):
                for name, tile in (("V1", V1), ("V2", V2)):
                    sp.dma_start(tile[:], io[name].rearrange("(t p) n -> p t n", p=P)).then_inc(loaded, 16)
                for name, tile in (("c1", c1), ("c2", c2), ("gamma", gamma), ("beta", beta)):
                    sp.dma_start(tile[:], io[name]).then_inc(loaded, 16)
                sp.dma_start(eps[:], io["eps"].to_broadcast([P, 1])).then_inc(loaded, 16)
                sp.wait_ge(written, W)
                sp.dma_start(io["out"][0:(W - 1) * P, :].rearrange("(w p) d -> p w d", p=P),
                             self.X[:, 0:W - 1, :]).then_inc(stored, 16)
                sp.dma_start(io["out"][(W - 1) * P:N, :], self.X[0:TAIL, W - 1, :]).then_inc(stored, 16)
                sp.wait_ge(stored, 32)

            @block.vector
            def _(dve):
                vector_begin(dve)
                dve.wait_ge(loaded, 112)
                nc.vector.memset(beps[:], 1.0e-5).then_inc(bn_eps, 1)
                nc.vector.tensor_scalar(eps[:], eps[:], 1.0, None, ALU.add).then_inc(eps1, 1)
                dve.wait_ge(eps1, 1)

                def update(i, m):
                    wait_pos(dve, turned, 2 * i)
                    group = lambda x: x[:, bass.ds(i * 4, m), :].rearrange("p w d -> p (w d)")
                    nc.vector.scalar_tensor_tensor(stage[:, 0:m * D], group(self.X), eps[:], group(AGG),
                                                   ALU.mult, ALU.add).then_inc(h_ready, 1)
                loop(dve, update)
                t = Tally(chain, 0)
                dve.wait_ge(r2, 2 * (W // 4 + 1))
                for h in range(2):
                    for c, (lo, m) in enumerate(CH):
                        nc.vector.bn_stats(bst[:, h, c, :], Z[:, h, lo:lo + m])
                t.link(dve, nc.vector.engine_nop())
                for h in range(2):
                    nc.vector.bn_aggr(bmv[:, h, :], bst[:, h, :, :].rearrange("p c s -> p (c s)"))
                nc.vector.engine_nop().then_inc(bvar, 1)
                dve.wait_ge(bstd, 1)
                t.link(dve, nc.vector.reciprocal(bsd[:], bsd[:]))
                t.link(dve, nc.vector.tensor_tensor(mul[:], gamma[:], bsd[:], ALU.mult))
                t.link(dve, nc.vector.tensor_tensor(shf[:], bmv[:, :, 0], mul[:], ALU.mult))
                nc.vector.tensor_tensor(shf[:], beta[:], shf[:], ALU.subtract).then_inc(coef, 1)

                def residual(w, k):
                    dve.wait_ge(back, w + 1)
                    nc.vector.tensor_tensor(window(Y, w), ps[:, k, 0:D], window(self.X, w), ALU.add).then_inc(resid, 1)
                for_pairs(dve, residual)
                residual(W - 1, 0)
                vector_part(dve, resid, W)

            @block.tensor
            def _(pe):
                pe.wait_ge(loaded, 112)

                def body(i, m):
                    n = m * P
                    pe.wait_ge(h_ready, i + 1)
                    for t in range(2):
                        for w in range(m):
                            last = nc.tensor.transpose(ps[:, t, w * P:(w + 1) * P],
                                                       stage[:, w * D + t * P:w * D + (t + 1) * P], self.ident[:])
                        last.then_inc(turned, 1)
                    pe.wait_ge(moved, 2 * i + 2)
                    for h in range(2):
                        out = ps[:, 2 + h, 0:n]
                        for t in range(2):
                            last = nc.tensor.matmul(out, V1[:, t, h * P:(h + 1) * P], hT[:, t, 0:n], start=t == 0,
                                                    stop=t == 1)
                        last.then_inc(z1, 1)
                    pe.wait_ge(r1, 2 * i + 2)
                    for h in range(2):
                        wait_pos(pe, r2, 2 * i)
                        out = ps[:, 4 + h, 0:n]
                        for t in range(2):
                            last = nc.tensor.matmul(out, V2[:, t, h * P:(h + 1) * P], gT[:, t, 0:n], start=t == 0,
                                                    stop=t == 1)
                        last.then_inc(z2, 1)
                loop(pe, body)

                def turn(w, k):
                    pe.wait_ge(act_done, 2 * w + 2)
                    wait_pos(pe, resid, w - 1)
                    for h in range(2):
                        last = nc.tensor.transpose(ps[:, k, h * P:(h + 1) * P], zr[:, k, h, :], self.ident[:])
                    last.then_inc(back, 1)
                for_pairs(pe, turn)
                turn(W - 1, 0)

            @block.scalar
            def _(act):
                act.wait_ge(loaded, 112)

                def body(i, m):
                    n = m * P
                    wait_pos(act, z1, 2 * i)
                    for t in range(2):
                        act.wait_ge(turned, 2 * i + t + 1)
                        nc.scalar.copy(hT[:, t, 0:n], ps[:, t, 0:n]).then_inc(moved, 1)
                    wait_pos(act, z2, 2 * i)
                    for h in range(2):
                        act.wait_ge(z1, 2 * i + h + 1)
                        nc.scalar.activation(gT[:, h, 0:n], ps[:, 2 + h, 0:n], ACT.Relu,
                                             bias=c1[:, h:h + 1]).then_inc(r1, 1)
                    for h in range(2):
                        act.wait_ge(z2, 2 * i + h + 1)
                        nc.scalar.activation(Z[:, h, bass.ds(i * 512, n)], ps[:, 4 + h, 0:n], ACT.Identity,
                                             bias=c2[:, h:h + 1]).then_inc(r2, 1)
                loop(act, body)
                act.wait_ge(bvar, 1)
                act.wait_ge(bn_eps, 1)
                nc.scalar.activation(bsd[:], bmv[:, :, 1], ACT.Sqrt, bias=beps[:]).then_inc(bstd, 1)
                act.wait_ge(coef, 1)

                def relu(w, k):
                    wait_pos(act, back, w - 1)
                    for h in range(2):
                        nc.scalar.activation(zr[:, k, h, :], Z[:, h, bass.ds(w * P, P)], ACT.Relu,
                                             bias=shf[:, h:h + 1], scale=mul[:, h:h + 1]).then_inc(act_done, 1)
                for_pairs(act, relu)
                relu(W - 1, 0)
                scalar_part(act)


def gnn_stack(nc, io):
    with ExitStack() as ctx:
        prog = Program(nc, ctx, io)
        prog.setup()
        prog.end_stage()
        with ExitStack() as inner:
            ACC = prog.sb(inner, "ACC", [P, W * 512])
            prog.layer0_edges(ACC)
            prog.end_stage()
            prog.layer0_nodes(ACC)
            prog.end_stage()
        prog.log_counts()
        prog.end_stage()
        with ExitStack() as inner:
            H = prog.sb(inner, "H", [P, W, D])
            with ExitStack() as deep:
                T = [prog.sb(deep, f"T{x}", [P, 2, NPAD], F16) for x in ("hi", "lo")]
                HS = [prog.sb(deep, f"H{x}", [P, W, D], F16) for x in ("hi", "lo")]
                betas = prog.sb(deep, "betas", [P, 4])
                prog.load_betas(betas)
                prog.end_stage()
                for layer in range(4):
                    prog.attention(layer, H if layer else prog.X, H, T, HS, betas)
                    prog.end_stage()
            prog.add_norm("e", H)
            prog.end_stage()
        prog.attribute_sums()
        prog.end_stage()
        prog.layer2_nodes()
        prog.end_stage()
        with ExitStack() as inner:
            AGG = prog.sb(inner, "AGG", [P, W, D])
            prog.layer3_edges(AGG)
            prog.end_stage()
            prog.layer3_nodes(AGG)


def kernel(**inputs):
    import numpy as np
    import concourse.bacc as bacc
    from concourse.bass_utils import run_bass_kernel_spmd

    nc = bacc.Bacc("TRN2", target_bir_lowering=False, num_devices=1)
    a = {name: np.asarray(value) for name, value in inputs.items()}
    src, dst = a["src"], a["dst"]
    spare = EP - E
    src_in = np.concatenate([src, np.zeros(spare, src.dtype)])
    src_id = np.concatenate([src, np.full(spare, PAD_ID, src.dtype)])
    dst_id = np.concatenate([dst, np.full(spare, PAD_ID, dst.dtype)])
    rows = lambda v: np.concatenate([v, np.zeros((spare, v.shape[1]), v.dtype)])
    arrays = {
        "x": a["x"],
        "sd": np.stack([src_in, dst_id], axis=1),
        "ids": np.stack([src_id, dst_id]),
        "src_t": src_id.reshape(STEPS, P).T,
        "dst_t": dst_id.reshape(STEPS, P).T,
        "attr4": rows(a["edge_attr_4"]),
        "emb": rows(a["edge_attr_10"]).T,
        "attr64": rows(a["edge_attr_64"]),
        "attr128": rows(a["edge_attr_128"]).T,
        "w_00_0": a["L0_gnn_w_00_0"], "w_11_0": a["L0_gnn_w_11_0"],
        "w_01_1": a["L0_gnn_w_01_1"], "w_10_1": a["L0_gnn_w_10_1"],
        "fc_w1": a["L0_gnn_fc_w1"], "fc_w2": a["L0_gnn_fc_w2"],
        "betas": a["L1_gnn_betas"].reshape(1, 4),
        "u": a["L2_gnn_u"], "W1": a["L2_gnn_W1"], "b1": a["L2_gnn_b1"].reshape(4, P).T,
        "W2": a["L2_gnn_W2"], "b2": a["L2_gnn_b2"].reshape(1, D),
        "W_edge": a["L3_gnn_W_edge"], "b_edge": a["L3_gnn_b_edge"].reshape(1, D),
        "V1": a["L3_gnn_W1"], "c1": a["L3_gnn_b1"].reshape(2, P).T,
        "V2": a["L3_gnn_W2"], "c2": a["L3_gnn_b2"].reshape(2, P).T,
        "eps": a["L3_gnn_eps"].reshape(1, 1),
        "gamma": a["L3_gnn_gamma"].reshape(2, P).T, "beta": a["L3_gnn_beta"].reshape(2, P).T,
    }
    arrays = {f"in_{name}": np.ascontiguousarray(value) for name, value in arrays.items()}
    io = {name[3:]: nc.dram_tensor(name, v.shape, mybir.dt.from_np(v.dtype), kind="ExternalInput").ap()
          for name, v in arrays.items()}
    io["counts"] = nc.dram_tensor("counts", (CELLS + P, 1), F32, kind="Internal").ap()
    io["sums"] = nc.dram_tensor("sums", (TABLES * TROWS, 65), F32, kind="Internal").ap()
    io["rows3"] = nc.dram_tensor("rows3", (NPAD, D), F32, kind="Internal").ap()
    io["out"] = nc.dram_tensor("out", (N, D), F32, kind="ExternalOutput").ap()
    gnn_stack(nc, io)
    result = run_bass_kernel_spmd(nc, [arrays], core_ids=[0])
    return result.results[0]["out"]
```

```python
import math
from contextlib import ExitStack

import concourse.bass as bass
from concourse import mybir

F32 = mybir.dt.float32
F16 = mybir.dt.float16
I32 = mybir.dt.int32
ALU = mybir.AluOpType
ACT = mybir.ActivationFunctionType
AX = mybir.AxisListType

P = 128
N = 3125
E = 50000
D = 256
MUL = 64
W = -(-N // P)
NPAD = W * P
TAIL = N - (W - 1) * P
STEPS = -(-E // P) + W
EP = STEPS * P
PAD_ID = 16384
CELLS = NPAD * NPAD
TROWS = NPAD + P
TABLES = 4
RING = 16
GB = 4
UNROLL = 4 * GB
ITERS = STEPS // UNROLL
ACW = 640
NO_EDGE = -1.0e30
SC = 400
NSC = NPAD // SC
SN = 1024.0
GROUPS = [(g, min(4, W - g)) for g in range(0, W, 4)]
HID = 512


class Tally:

    def __init__(self, sem, base):
        self.sem, self.n = sem, base

    def link(self, eng, ins):
        ins.then_inc(self.sem, 1)
        self.n = self.n + 1
        eng.wait_ge(self.sem, self.n)


def wait_pos(eng, sem, value):
    if not (isinstance(value, int) and value <= 0):
        eng.wait_ge(sem, value)


def window(t, w):
    return t[:, bass.ds(w, 1), :].rearrange("p w d -> p (w d)")


def for_pairs(eng, body):
    body(0, 0)
    body(1, 1)
    with eng.Fori(1, (W - 1) // 2) as i:
        body(i * 2, 0)
        body(i * 2 + 1, 1)


class Program:
    def __init__(self, nc, ctx, io):
        self.nc, self.ctx, self.io = nc, ctx, io
        self.sems = []
        self.ps = ctx.enter_context(nc.psum_tensor("ps", [P, 8, 512], F32))
        self.zeroed = nc.alloc_semaphore(name="zeroed")
        self.zero_count = 16 * (W + -(-TABLES * TROWS * 65 // (P * NPAD)))
        self.X = self.sb(ctx, "X", [P, W, D])
        self.iota = self.sb(ctx, "iota", [P, P])
        self.lower = self.sb(ctx, "lower", [P, P])
        self.ident = self.sb(ctx, "ident", [P, P])
        self.ident16 = self.sb(ctx, "ident16", [P, P], F16)
        self.part = self.sb(ctx, "part", [P, 1])
        self.win_col = self.sb(ctx, "win_col", [P, STEPS])
        self.win = self.sb(ctx, "win", [P, STEPS], I32)
        self.off = self.sb(ctx, "off", [P, STEPS], I32)

    def sb(self, ctx, name, shape, dt=F32):
        return ctx.enter_context(self.nc.sbuf_tensor(name, shape, dt))

    def sem(self, name):
        self.sems.append(self.nc.alloc_semaphore(name=name))
        return self.sems[-1]

    def end_stage(self):
        self.nc.clear_and_free_semaphores(self.sems)
        self.sems = []
        self.nc.all_engine_barrier()

    def setup(self):
        nc, io = self.nc, self.io
        loaded = self.sem("su_loaded")
        consts, chain, sums, zero_ready = self.sem("su_consts"), self.sem("su_chain"), self.sem("su_sums"), self.sem("su_zero_ready")
        part_ready, xpad = self.sem("su_part"), self.sem("su_xpad")
        pchain = self.sem("su_pchain")
        with ExitStack() as ctx:
            sb = lambda name, shape, dt=F32: self.sb(ctx, name, shape, dt)
            zeros = self.zeros
            ones = sb("ones", [P, P])
            dst_all = sb("dst_all", [P, STEPS], I32)
            dstf = sb("dstf", [P, STEPS])
            junk = sb("junk", [P, STEPS])
            step_no = sb("step_no", [P, STEPS])
            below = sb("below", [P, W + 1])
            start = sb("start", [P, W + 1])
            edges = sb("edges", [P, W])
            tiles_i = sb("tiles_i", [P, W], I32)
            tiles = sb("tiles", [P, W])
            first_step = sb("first_step", [P, W + 1])
            zero_w = sb("zero_w", [P, W])
            shift = sb("shift", [P, W])
            jump = sb("jump", [P, W])
            wsum = sb("wsum", [P, STEPS])
            osum = sb("osum", [P, STEPS])
            block = ctx.enter_context(nc.Block())

            @block.sync
            def _(sp):
                sp.dma_start(dst_all[:, :], io["dst_t"]).then_inc(loaded, 16)
                sp.wait_ge(xpad, 1)
                sp.dma_start(self.X[:, 0:W - 1, :],
                             io["x"][0:(W - 1) * P, :].rearrange("(w p) d -> p w d", p=P)).then_inc(loaded, 16)
                sp.dma_start(self.X[0:TAIL, W - 1, :], io["x"][(W - 1) * P:N, :]).then_inc(loaded, 16)
                sp.wait_ge(zero_ready, 1)
                flat = io["counts"][0:CELLS, :].rearrange("(k p f) o -> k p (f o)", p=P, f=NPAD)
                for k in range(W):
                    sp.dma_start(flat[k], zeros[:]).then_inc(self.zeroed, 16)
                sums = io["sums"].rearrange("(p r) c -> p (r c)", p=P)
                width = TABLES * TROWS * 65 // P
                for lo in range(0, width, NPAD):
                    n = min(NPAD, width - lo)
                    sp.dma_start(sums[:, lo:lo + n], zeros[:, 0:n]).then_inc(self.zeroed, 16)
                sp.wait_ge(loaded, 48)

            @block.gpsimd
            def _(pool):
                nc.gpsimd.memset(zeros[:], 0.0).then_inc(zero_ready, 1)
                nc.gpsimd.iota(self.iota[:], [[1, P]], base=0, channel_multiplier=0,
                               allow_small_or_imprecise_dtypes=True)
                nc.gpsimd.iota(step_no[:], [[1, STEPS]], base=0, channel_multiplier=0,
                               allow_small_or_imprecise_dtypes=True)
                nc.gpsimd.iota(self.part[:], [[1, 1]], base=0, channel_multiplier=1,
                               allow_small_or_imprecise_dtypes=True)
                nc.gpsimd.memset(ones[:], 1.0).then_inc(pchain, 1)
                pool.wait_ge(pchain, 1)
                nc.gpsimd.affine_select(self.lower[:], ones[:], [[-1, P]], ALU.is_gt, 0.0, base=0,
                                        channel_multiplier=1)
                nc.gpsimd.affine_select(self.ident[:], ones[:], [[-1, P]], ALU.is_equal, 0.0, base=0,
                                        channel_multiplier=1).then_inc(pchain, 1)
                pool.wait_ge(pchain, 2)
                nc.gpsimd.tensor_copy(self.ident16[:], self.ident[:]).then_inc(consts, 1)

            @block.vector
            def _(dve):
                t = Tally(chain, 0)
                nc.vector.memset(self.X[:, W - 1, :], 0.0).then_inc(xpad, 1)
                nc.vector.memset(below[:, 0:1], 0.0)
                nc.vector.memset(zero_w[:], 0.0)
                dve.wait_ge(loaded, 16)
                dve.wait_ge(loaded, 48)
                t.link(dve, nc.vector.tensor_copy(dstf[:], dst_all[:]))
                for w in range(1, W + 1):
                    t.link(dve, nc.vector.tensor_scalar(junk[:], dstf[:], float(w * P), 0.0, ALU.is_lt,
                                                        ALU.add, accum_out=below[:, w:w + 1]))
                dve.sem_inc(part_ready, 1)
                dve.wait_ge(sums, 1)
                t.link(dve, nc.vector.tensor_copy(start[:], self.ps[:, 0, 0:W + 1]))
                t.link(dve, nc.vector.tensor_tensor(edges[:], start[:, 1:W + 1], start[:, 0:W], ALU.subtract))
                t.link(dve, nc.vector.tensor_scalar(tiles_i[:], edges[:], float(P - 1), None, ALU.add))
                t.link(dve, nc.vector.tensor_scalar(tiles_i[:], tiles_i[:], 7, None, ALU.arith_shift_right))
                t.link(dve, nc.vector.tensor_copy(tiles[:], tiles_i[:]))
                t.link(dve, nc.vector.memset(first_step[:, 0:1], 0.0))
                t.link(dve, nc.vector.tensor_tensor_scan(first_step[:, 1:W + 1], zero_w[:], tiles[:], 0.0,
                                                         ALU.add, ALU.add))
                t.link(dve, nc.vector.scalar_tensor_tensor(shift[:], first_step[:, 0:W], -float(P), start[:, 0:W],
                                                           ALU.mult, ALU.add))
                t.link(dve, nc.vector.tensor_tensor(jump[:, 1:W], shift[:, 1:W], shift[:, 0:W - 1], ALU.subtract))
                dve.wait_ge(consts, 1)
                nc.vector.memset(wsum[:], 0.0)
                t.link(dve, nc.vector.tensor_scalar(osum[:], step_no[:], float(P), None, ALU.mult))
                for w in range(1, W):
                    t.link(dve, nc.vector.scalar_tensor_tensor(wsum[:], step_no[:], first_step[:, w:w + 1],
                                                               wsum[:], ALU.is_ge, ALU.add))
                    t.link(dve, nc.vector.tensor_scalar(junk[:], step_no[:], first_step[:, w:w + 1],
                                                        jump[:, w:w + 1], ALU.is_ge, ALU.mult))
                    t.link(dve, nc.vector.tensor_tensor(osum[:], osum[:], junk[:], ALU.add))
                nc.vector.tensor_copy(self.win[:], wsum[:])
                nc.vector.tensor_copy(self.off[:], osum[:])
                nc.vector.tensor_scalar(self.win_col[:], wsum[:], float(P), None, ALU.mult)

            @block.tensor
            def _(pe):
                pe.wait_ge(consts, 1)
                pe.wait_ge(part_ready, 1)
                nc.tensor.matmul(self.ps[:, 0, 0:W + 1], ones[:], below[:], start=True,
                                 stop=True).then_inc(sums, 1)

    def layer0_edges(self, ACC):
        nc, io, ps = self.nc, self.io, self.ps
        ld = [self.sem(f"a_edges_in{k}") for k in range(RING)]
        xg = [self.sem(f"a_rows_in{k}") for k in range(RING)]
        ldc = [self.sem(f"a_ids_in{c}") for c in range(4)]
        once = self.sem("a_once")
        hid_ready, silu_ready, rad_ready = self.sem("a_hid"), self.sem("a_silu"), self.sem("a_rad")
        factors, scaled, hot = self.sem("a_factors"), self.sem("a_scaled"), self.sem("a_hot")
        summed, added = self.sem("a_summed"), self.sem("a_added")
        ids_used, pairs_ready, pairs_done = self.sem("a_ids_used"), self.sem("a_pairs_ready"), self.sem("a_pairs_done")
        chain, keys, tick = self.sem("a_chain"), self.sem("a_keys"), self.sem("a_tick")
        with ExitStack() as ctx:
            sb = lambda name, shape, dt=F32: self.sb(ctx, name, shape, dt)
            sd = sb("sd", [P, RING, 2], I32)
            attr = sb("attr", [P, RING, 4])
            emb = sb("emb", [10, RING, P])
            rows = sb("rows", [P, RING, D])
            fc1, fc2 = sb("fc1", [10, 64]), sb("fc2", [64, 1])
            hid = sb("hid", [64, 2, 4 * P])
            dl = sb("dl", [P, 2, 4])
            ra = sb("ra", [P, 2, 4, 4])
            prod = sb("prod", [P, 2, ACW])
            oh = sb("oh", [P, 4, P])
            ids = sb("ids", [P, 4, 2, 4 * P], I32)
            pair = sb("pair", [P, 4 * P])
            key = sb("key", [P, STEPS])
            spare = sb("spare", [P, STEPS])
            kt = sb("kt", [P, 2, STEPS], I32)
            junk = sb("junk_a", [P, 4, 8 * P])
            cnt = sb("cnt", [P, 2, 4])
            earlier = sb("earlier", [P, 2, 2, 4])
            skip = sb("skip", [P, 2, 4])
            cellf = sb("cellf", [P, 2, 4])
            dump = sb("dump", [P, 4])
            cell = sb("cell", [P, 2, 4], I32)
            block = ctx.enter_context(nc.Block())

            def acc_ps(p):
                return ps[:, 2 + 2 * p:4 + 2 * p, :].rearrange("p b n -> p (b n)")[:, 0:ACW]

            def group(i, b):
                return i * GB + b, (4 * b) % RING, i + b // GB

            @block.sync
            def _(sp):
                sp.dma_start(fc1[:], io["fc_w1"]).then_inc(once, 16)
                sp.dma_start(fc2[:], io["fc_w2"]).then_inc(once, 16)
                sp.dma_start(kt[:, 0, :], io["src_t"]).then_inc(once, 16)
                sp.dma_start(kt[:, 1, :], io["dst_t"]).then_inc(once, 16)

                def body(i):
                    for b in range(GB):
                        g, k0, _ = group(i, b)
                        wait_pos(sp, ids_used, g - 3)
                        for h in range(2):
                            sp.dma_start(ids[:, b, h, :], io["ids"][h:h + 1, bass.ds(g * 4 * P, 4 * P)]
                                         .to_broadcast([P, 4 * P])).then_inc(ldc[b], 16)
                        for q in range(4):
                            s, k = g * 4 + q, k0 + q
                            wait_pos(sp, summed, s - RING + 1)
                            o = sp.value_load(self.off[0:1, bass.ds(s, 1)], min_val=0, max_val=EP - P)
                            sp.dma_start(sd[:, k, :], io["sd"][bass.ds(o, P), :]).then_inc(ld[k], 16)
                            sp.dma_start(attr[:, k, :], io["attr4"][bass.ds(o, P), :]).then_inc(ld[k], 16)
                            sp.dma_start(emb[:, k, :], io["emb"][:, bass.ds(o, P)]).then_inc(ld[k], 16)

                body(0)
                with sp.Fori(1, ITERS) as i:
                    body(i)

            @block.gpsimd
            def _(pool):
                def gather(i, b):
                    _, k0, it = group(i, b)
                    for k in range(k0, k0 + 4):
                        pool.wait_ge(ld[k], 48 * (it + 1))
                        pool.sem_inc(tick, 1)
                        pool.indirect_dma_start(
                            out=rows[:, k, :], out_offset=None, in_=io["x_blocks"],
                            in_offset=bass.IndirectOffsetOnAxis(ap=sd[:, k, 0:1], axis=0)).then_inc(xg[k], 16)

                def scatter(i, b):
                    g, _, _ = group(i, b)
                    pool.wait_ge(pairs_ready, g + 1)
                    pool.sem_inc(tick, 1)
                    if not (isinstance(i, int) and i == 0 and b == 0):
                        pool.wait_ge(pairs_done, g * 64)
                        pool.sem_inc(tick, 1)
                    for t in range(4):
                        pool.indirect_dma_start(
                            out=io["counts"],
                            out_offset=bass.IndirectOffsetOnAxis(ap=cell[:, b % 2, t:t + 1], axis=0),
                            in_=cnt[:, b % 2, t:t + 1], in_offset=None,
                            compute_op=ALU.add).then_inc(pairs_done, 16)

                def body(i, last=False):
                    for b in range(GB):
                        scatter(i, b)
                        if not (last and b + 2 >= GB):
                            gather(i, b + 2)

                gather(0, 0)
                gather(0, 1)
                pool.wait_ge(self.zeroed, self.zero_count)
                pool.sem_inc(tick, 1)
                body(0)
                with pool.Fori(1, ITERS - 1) as i:
                    body(i)
                body(ITERS - 1, last=True)
                pool.wait_ge(pairs_done, 16 * STEPS)

            @block.scalar
            def _(act):
                def silu(i, b):
                    h, _, _ = group(i, b)
                    act.wait_ge(hid_ready, h + 1)
                    wait_pos(act, rad_ready, h - 1)
                    nc.scalar.activation(hid[:, b % 2, :], ps[0:64, 0, :], ACT.Silu,
                                         scale=1.0 / math.sqrt(10.0)).then_inc(silu_ready, 1)

                def body(i, last=False):
                    for b in range(GB):
                        g, k0, it = group(i, b)
                        if not (last and b + 1 == GB):
                            silu(i, b + 1)
                        act.wait_ge(factors, g + 1)
                        for q in range(4):
                            s, k = g * 4 + q, k0 + q
                            act.wait_ge(xg[k], 16 * (it + 1))
                            wait_pos(act, summed, s - 1)
                            nc.scalar.activation(prod[:, q % 2, 0:D], rows[:, k, :], ACT.Copy,
                                                 scale=ra[:, b % 2, q, 0:1])
                            for m in range(1, 4):
                                both = rows[:, k, :].rearrange("p (c i) -> p c i", c=4)[:, 0:m + 1:m, :]
                                last_op = nc.scalar.activation(
                                    prod[:, q % 2, D + (m - 1) * P:D + m * P].rearrange("p (c i) -> p c i", c=2),
                                    both, ACT.Copy, scale=ra[:, b % 2, q, m:m + 1])
                            last_op.then_inc(scaled, 1)

                silu(0, 0)
                body(0)
                with act.Fori(1, ITERS - 1) as i:
                    body(i)
                body(ITERS - 1, last=True)

            @block.tensor
            def _(pe):
                pe.wait_ge(once, 64)

                def hidden(i, b):
                    h, k0, it = group(i, b)
                    for k in range(k0, k0 + 4):
                        pe.wait_ge(ld[k], 48 * (it + 1))
                    wait_pos(pe, silu_ready, h)
                    nc.tensor.matmul(ps[0:64, 0, :], fc1[:], emb[:, k0:k0 + 4, :].rearrange("p k n -> p (k n)"),
                                     start=True, stop=True).then_inc(hid_ready, 1)

                def radial(i, b):
                    h, _, _ = group(i, b)
                    pe.wait_ge(silu_ready, h + 1)
                    wait_pos(pe, factors, h - 1)
                    for q in range(4):
                        c = (b % 2) * 4 + q
                        last = nc.tensor.matmul(ps[:, 1, c:c + 1], hid[:, b % 2, q * P:(q + 1) * P], fc2[:],
                                                start=True, stop=True)
                    last.then_inc(rad_ready, 1)

                def body(i, last=False):
                    for b in range(GB):
                        g, _, _ = group(i, b)
                        ahead = not (last and b + 1 == GB)
                        if ahead:
                            hidden(i, b + 1)
                        for q in range(4):
                            s = g * 4 + q
                            if ahead and q == 1:
                                radial(i, b + 1)
                            pe.wait_ge(hot, s + 1)
                            pe.wait_ge(scaled, s + 1)
                            wait_pos(pe, added, s - 1)
                            out = acc_ps(q % 2)
                            nc.tensor.matmul(out[:, 0:512], oh[:, q, :], prod[:, q % 2, 0:512], start=True,
                                             stop=True)
                            nc.tensor.matmul(out[:, 512:ACW], oh[:, q, :], prod[:, q % 2, 512:ACW], start=True,
                                             stop=True).then_inc(summed, 1)

                hidden(0, 0)
                radial(0, 0)
                body(0)
                with pe.Fori(1, ITERS - 1) as i:
                    body(i)
                body(ITERS - 1, last=True)

            @block.vector
            def _(dve):
                LINKS = 5
                nc.vector.memset(earlier[:], 0.0)
                nc.vector.memset(ACC[:], 0.0).then_inc(keys, 1)
                dve.wait_ge(once, 64)
                nc.vector.scalar_tensor_tensor(key[:], kt[:, 1, :], float(NPAD), kt[:, 0, :], ALU.mult,
                                               ALU.add).then_inc(keys, 1)
                dve.wait_ge(keys, 2)
                nc.vector.tensor_scalar(spare[:], key[:], float(CELLS), None, ALU.is_ge).then_inc(keys, 1)
                for t in range(4):
                    last = nc.vector.tensor_scalar(dump[:, t:t + 1], self.part[:], float(CELLS + t * P), None, ALU.add)
                last.then_inc(keys, 1)
                dve.wait_ge(keys, 4)

                def compare(i, b, q):
                    h, _, it = group(i, b)
                    c = b % 2
                    if q == 0:
                        dve.wait_ge(ldc[b % 4], 32 * (it + 1))
                        if not (isinstance(i, int) and i == 0 and b < 2):
                            dve.wait_ge(pairs_done, 64 * (h - 1))
                        nc.vector.scalar_tensor_tensor(pair[:], ids[:, b % 4, 1, :], float(NPAD), ids[:, b % 4, 0, :],
                                                       ALU.mult, ALU.add).then_inc(ids_used, 1)
                        dve.wait_ge(ids_used, h + 1)
                    mine = key[:, bass.ds(h * 4 + q, 1)]
                    nc.vector.tensor_scalar(junk[:, q, 0:4 * P], pair[:], mine, 0.0, ALU.is_equal, ALU.add,
                                            accum_out=cnt[:, c, q:q + 1])
                    if q:
                        nc.vector.tensor_scalar(junk[:, q, 4 * P:(4 + q) * P], pair[:, 0:q * P], mine, 0.0,
                                                ALU.is_equal, ALU.add, accum_out=earlier[:, c, 1, q:q + 1])
                    return nc.vector.scalar_tensor_tensor(junk[:, q, 7 * P:8 * P], pair[:, q * P:(q + 1) * P], mine,
                                                          self.lower[:], ALU.is_equal, ALU.mult,
                                                          accum_out=earlier[:, c, 0, q:q + 1])

                def cells(i, b, last_compare):
                    h, _, _ = group(i, b)
                    c = b % 2
                    t = Tally(chain, h * LINKS)
                    t.link(dve, last_compare)
                    t.link(dve, nc.vector.tensor_tensor(skip[:, c, :], earlier[:, c, 0, :], earlier[:, c, 1, :],
                                                        ALU.add))
                    t.link(dve, nc.vector.scalar_tensor_tensor(skip[:, c, :], skip[:, c, :], 0.5,
                                                               spare[:, bass.ds(h * 4, 4)], ALU.is_gt, ALU.max))
                    t.link(dve, nc.vector.scalar_tensor_tensor(cellf[:, c, :], skip[:, c, :], 0.0,
                                                               key[:, bass.ds(h * 4, 4)], ALU.is_equal, ALU.mult))
                    t.link(dve, nc.vector.tensor_tensor(skip[:, c, :], skip[:, c, :], dump[:], ALU.mult))
                    nc.vector.tensor_tensor(cell[:, c, :], skip[:, c, :], cellf[:, c, :],
                                            ALU.add).then_inc(pairs_ready, 1)

                def factor(i, b):
                    h, k0, it = group(i, b)
                    c = b % 2
                    for k in range(k0, k0 + 4):
                        dve.wait_ge(ld[k], 48 * (it + 1))
                    nc.vector.tensor_tensor(dl[:, c, :], sd[:, k0:k0 + 4, 1], self.win_col[:, bass.ds(h * 4, 4)],
                                            ALU.subtract)
                    dve.wait_ge(rad_ready, h + 1)
                    nc.vector.tensor_tensor(ra[:, c, :, :], attr[:, k0:k0 + 4, :],
                                            ps[:, 1, c * 4:c * 4 + 4].unsqueeze(2).to_broadcast([P, 4, 4]),
                                            ALU.mult).then_inc(factors, 1)

                def add(s, p):
                    w = dve.value_load(self.win[0:1, bass.ds(s, 1)], min_val=0, max_val=W - 1)
                    dve.wait_ge(summed, s + 1)
                    wait_pos(dve, added, s)
                    a = ACC[:, bass.ds(w * ACW, ACW)]
                    nc.vector.tensor_tensor(a, a, acc_ps(p), ALU.add).then_inc(added, 1)

                def body(i, first=False, last=False):
                    for b in range(GB):
                        g, _, _ = group(i, b)
                        ahead = not (last and b + 1 == GB)
                        dve.wait_ge(factors, g + 1)
                        for q in range(4):
                            s = g * 4 + q
                            nc.vector.tensor_scalar(oh[:, q, :], self.iota[:], dl[:, b % 2, q:q + 1], None,
                                                    ALU.is_equal).then_inc(hot, 1)
                            if ahead:
                                last_compare = compare(i, b + 1, q)
                            if ahead and q == 2:
                                factor(i, b + 1)
                            if ahead and q == 3:
                                cells(i, b + 1, last_compare)
                            if not (first and b == 0 and q == 0):
                                add(s - 1, (q - 1) % 2)

                factor(0, 0)
                for q in range(4):
                    last_compare = compare(0, 0, q)
                cells(0, 0, last_compare)
                body(0, first=True)
                with dve.Fori(1, ITERS - 1) as i:
                    body(i)
                body(ITERS - 1, last=True)
                add(STEPS - 1, 1)

    def norm_end(self, ctx, tag, Y):
        nc = self.nc
        st = self.sb(ctx, tag + "_st", [P, W, 6])
        mv = self.sb(ctx, tag + "_mv", [P, W, 2])
        std = self.sb(ctx, tag + "_std", [P, W])
        epsc = self.sb(ctx, tag + "_eps", [P, 1])
        var_ready, std_ready = self.sem(tag + "_var"), self.sem(tag + "_stdr")
        rec_ready, written = self.sem(tag + "_rec"), self.sem(tag + "_norm")
        stats_ready = self.sem(tag + "_stats")

        def scalar_part(act):
            act.wait_ge(var_ready, 1)
            nc.scalar.activation(std[:], mv[:, :, 1], ACT.Sqrt, bias=epsc[:]).then_inc(std_ready, 1)

        def vector_begin(dve):
            nc.vector.memset(epsc[:], 1.0e-5).then_inc(rec_ready, 1)
            dve.wait_ge(rec_ready, 1)

        def vector_part(dve, summed, count):
            dve.wait_ge(summed, count)
            dve.sem_inc(stats_ready, 1)
            with dve.Fori(0, W) as w:
                nc.vector.bn_stats(window(st, w), window(Y, w)).then_inc(stats_ready, 1)
            dve.wait_ge(stats_ready, W + 1)
            for w in range(W):
                last = nc.vector.bn_aggr(mv[:, w, :], st[:, w, :])
            last.then_inc(var_ready, 1)
            dve.wait_ge(std_ready, 1)
            nc.vector.reciprocal(std[:], std[:]).then_inc(rec_ready, 1)
            dve.wait_ge(rec_ready, 2)

            with dve.Fori(0, W) as w:
                nc.vector.tensor_scalar(window(self.X, w), window(Y, w),
                                        mv[:, bass.ds(w, 1), 0:1].rearrange("p w d -> p (w d)"),
                                        std[:, bass.ds(w, 1)], ALU.subtract, ALU.mult).then_inc(written, 1)

        return scalar_part, vector_begin, vector_part, written

    def layer0_nodes(self, ACC):
        nc, io, ps = self.nc, self.io, self.ps
        loaded, scaled = self.sem("b_loaded"), self.sem("b_scaled")
        turned, moved, mixed, resid = self.sem("b_turned"), self.sem("b_moved"), self.sem("b_mixed"), self.sem("b_resid")
        staged, vsums = self.sem("b_staged"), self.sem("b_vsums")
        scale = 1.679177 / (math.sqrt(2.0 * MUL) * math.sqrt(64.0) * math.sqrt(16.0))
        with ExitStack() as ctx:
            wgt = self.sb(ctx, "wgt", [P, 2, MUL])
            stage = self.sb(ctx, "stage", [P, 2, 512])
            vsum = self.sb(ctx, "vsum", [P, 2, MUL])
            turn = self.sb(ctx, "turn", [P, 2, 512])
            Y = self.sb(ctx, "Yb", [P, W, D])
            scalar_part, vector_begin, vector_part, _ = self.norm_end(ctx, "bn", Y)
            block = ctx.enter_context(nc.Block())

            @block.sync
            def _(sp):
                sp.dma_start(wgt[0:MUL, 0, :], io["w_00_0"]).then_inc(loaded, 16)
                sp.dma_start(wgt[MUL:P, 0, :], io["w_11_0"]).then_inc(loaded, 16)
                sp.dma_start(wgt[0:MUL, 1, :], io["w_01_1"]).then_inc(loaded, 16)
                sp.dma_start(wgt[MUL:P, 1, :], io["w_10_1"]).then_inc(loaded, 16)

            @block.gpsimd
            def _(pool):
                def arrange(w, k):
                    a = ACC[:, bass.ds(w * ACW, ACW)].rearrange("p (c i) -> p c i", i=MUL)
                    s_ = stage[:, k, :].rearrange("p (c h i) -> p c h i", c=4, h=2)
                    wait_pos(pool, turned, w - 1)
                    nc.gpsimd.tensor_copy(s_[:, 0, 0, :], a[:, 0, :])
                    nc.gpsimd.tensor_copy(s_[:, 1:4, 1, :], a[:, 1:4, :])
                    nc.gpsimd.tensor_copy(s_[:, 1:4, 0, :], a[:, 4:10:2, :])
                    nc.gpsimd.tensor_tensor(vsum[:, k, :], a[:, 5, :], a[:, 7, :], ALU.add).then_inc(vsums, 1)
                    pool.wait_ge(vsums, w + 1)
                    nc.gpsimd.tensor_tensor(s_[:, 0, 1, :], vsum[:, k, :], a[:, 9, :], ALU.add).then_inc(staged, 1)

                for_pairs(pool, arrange)
                arrange(W - 1, 0)

            @block.tensor
            def _(pe):
                pe.wait_ge(scaled, 1)

                def turn_window(w, k):
                    pe.wait_ge(staged, w + 1)
                    wait_pos(pe, moved, w - 1)
                    for c in range(4):
                        last = nc.tensor.transpose(ps[:, k, c * P:(c + 1) * P], stage[:, k, c * P:(c + 1) * P],
                                                   self.ident[:])
                    last.then_inc(turned, 1)

                def mix_window(w, k):
                    pe.wait_ge(moved, w + 1)
                    wait_pos(pe, resid, w - 1)
                    for c in range(4):
                        last = nc.tensor.matmul(ps[:, 2 + k, c * MUL:(c + 1) * MUL], turn[:, k, c * P:(c + 1) * P],
                                                wgt[:, min(c, 1), :], start=True, stop=True)
                    last.then_inc(mixed, 1)

                turn_window(0, 0)
                for_pairs(pe, lambda w, k: (turn_window(w + 1, 1 - k), mix_window(w, k)))
                mix_window(W - 1, 0)

            @block.scalar
            def _(act):
                act.wait_ge(loaded, 64)
                nc.scalar.mul(wgt[MUL:P, 0, :], wgt[MUL:P, 0, :], 1.0 / math.sqrt(3.0)).then_inc(scaled, 1)

                def move(w, k):
                    act.wait_ge(turned, w + 1)
                    wait_pos(act, mixed, w - 1)
                    nc.scalar.copy(turn[:, k, :], ps[:, k, :]).then_inc(moved, 1)

                for_pairs(act, move)
                move(W - 1, 0)
                scalar_part(act)

            @block.vector
            def _(dve):
                vector_begin(dve)

                def residual(w, k):
                    dve.wait_ge(mixed, w + 1)
                    y, x = window(Y, w), window(self.X, w)
                    nc.vector.scalar_tensor_tensor(y[:, 0:MUL], ps[:, 2 + k, 0:MUL], scale, x[:, 0:MUL], ALU.mult,
                                                   ALU.add)
                    ins = nc.vector.scalar_tensor_tensor(
                        y[:, MUL:D].rearrange("p (o m) -> p m o", m=3),
                        ps[:, 2 + k, MUL:D].rearrange("p (m o) -> p m o", m=3), scale,
                        x[:, MUL:D].rearrange("p (o m) -> p m o", m=3), ALU.mult, ALU.add)
                    ins.then_inc(resid, 1)

                for_pairs(dve, residual)
                residual(W - 1, 0)
                vector_part(dve, resid, W)

    def log_counts(self):
        nc, io = self.nc, self.io
        HALF = NPAD // 2
        cin = [self.sem(f"c_in{k}") for k in range(2)]
        cout = [self.sem(f"c_out{k}") for k in range(2)]
        clipped, logged, summed = self.sem("c_clipped"), self.sem("c_logged"), self.sem("c_summed")
        with ExitStack() as ctx:
            c = self.sb(ctx, "c_cnt", [P, 2, HALF])
            one = self.sb(ctx, "c_one", [P, 2, HALF])
            none = self.sb(ctx, "c_none", [P, 2, HALF])
            res = self.sb(ctx, "c_res", [P, 2, HALF])
            table = io["counts"][0:CELLS, :].rearrange("(w p f) o -> w p (f o)", p=P, f=NPAD)
            block = ctx.enter_context(nc.Block())

            def piece(i, k):
                return table[bass.ds(i, 1), :, k * HALF:(k + 1) * HALF].rearrange("w p f -> p (w f)")

            def loop(eng, body):
                body(0)
                with eng.Fori(1, W) as i:
                    body(i)

            @block.sync
            def _(sp):
                def body(i):
                    for k in range(2):
                        wait_pos(sp, clipped, 2 * i + k - 1)
                        sp.dma_start(c[:, k, :], piece(i, k)).then_inc(cin[k], 16)
                loop(sp, body)

            @block.vector
            def _(dve):
                def body(i):
                    for k in range(2):
                        dve.wait_ge(cin[k], 16 * (i + 1))
                        wait_pos(dve, summed, 2 * i + k - 1)
                        nc.vector.tensor_scalar(none[:, k, :], c[:, k, :], 0.0, NO_EDGE, ALU.is_equal, ALU.mult)
                        nc.vector.tensor_scalar(one[:, k, :], c[:, k, :], 1.0, None, ALU.max).then_inc(clipped, 1)
                    for k in range(2):
                        dve.wait_ge(logged, 2 * i + k + 1)
                        wait_pos(dve, cout[k], 16 * i)
                        nc.vector.tensor_tensor(res[:, k, :], none[:, k, :], one[:, k, :],
                                                ALU.add).then_inc(summed, 1)
                loop(dve, body)

            @block.scalar
            def _(act):
                def body(i):
                    for k in range(2):
                        act.wait_ge(clipped, 2 * i + k + 1)
                        nc.scalar.activation(one[:, k, :], one[:, k, :], ACT.Ln).then_inc(logged, 1)
                loop(act, body)

            @block.gpsimd
            def _(pool):
                def body(i):
                    for k in range(2):
                        pool.wait_ge(summed, 2 * i + k + 1)
                        pool.dma_start(piece(i, k), res[:, k, :]).then_inc(cout[k], 16)
                loop(pool, body)
                for k in range(2):
                    pool.wait_ge(cout[k], 16 * W)

    def attention(self, layer, H, out, T, HS, betas):
        nc, ps = self.nc, self.ps
        n = f"l{layer}_"
        squared, eps_added, rooted, inverted = (self.sem(n + x) for x in ("sq", "eps", "root", "inv"))
        scaled, turned, t_high, t_low = (self.sem(n + x) for x in ("scaled", "turned", "thigh", "tlow"))
        h_high, h_low = self.sem(n + "hhigh"), self.sem(n + "hlow")
        with ExitStack() as ctx:
            ss = self.sb(ctx, n + "ss", [P, W])
            junk = self.sb(ctx, n + "junk", [P, 2, D])
            hn = self.sb(ctx, n + "hn", [P, 2, D])
            block = ctx.enter_context(nc.Block())

            @block.scalar
            def _(act):
                def square(w, k):
                    wait_pos(act, squared, w - 1)
                    nc.scalar.activation(junk[:, k, :], window(H, w), ACT.Square,
                                         accum_out=ss[:, bass.ds(w, 1)]).then_inc(squared, 1)
                for_pairs(act, square)
                square(W - 1, 0)
                act.wait_ge(eps_added, 1)
                nc.scalar.activation(ss[:], ss[:], ACT.Sqrt).then_inc(rooted, 1)

                def parts(w, k):
                    nc.scalar.copy(window(HS[0], w), window(H, w)).then_inc(h_high, 1)
                    act.wait_ge(turned, w + 1)
                    nc.scalar.activation(T[0][:, :, bass.ds(w * P, P)],
                                         ps[:, k, 0:D].rearrange("p (t n) -> p t n", t=2), ACT.Copy,
                                         scale=SN).then_inc(t_high, 1)
                for_pairs(act, parts)
                parts(W - 1, 0)

            @block.gpsimd
            def _(pool):
                def low(w, k):
                    pool.wait_ge(h_high, w + 1)
                    nc.gpsimd.tensor_tensor(window(HS[1], w), window(H, w), window(HS[0], w),
                                            ALU.subtract).then_inc(h_low, 1)
                for_pairs(pool, low)
                low(W - 1, 0)

            @block.vector
            def _(dve):
                dve.wait_ge(squared, W)
                nc.vector.tensor_scalar(ss[:], ss[:], 1.0e-16, None, ALU.add).then_inc(eps_added, 1)
                dve.wait_ge(rooted, 1)
                nc.vector.reciprocal(ss[:], ss[:]).then_inc(inverted, 1)
                dve.wait_ge(inverted, 1)

                def scale(w, k):
                    wait_pos(dve, turned, w - 1)
                    nc.vector.tensor_scalar(hn[:, k, :], window(H, w), ss[:, bass.ds(w, 1)], None,
                                            ALU.mult).then_inc(scaled, 1)

                def low(w, k):
                    dve.wait_ge(t_high, w + 1)
                    part = bass.ds(w * P, P)
                    nc.vector.scalar_tensor_tensor(T[1][:, :, part],
                                                   ps[:, k, 0:D].rearrange("p (t n) -> p t n", t=2), SN,
                                                   T[0][:, :, part], ALU.mult, ALU.subtract).then_inc(t_low, 1)
                scale(0, 0)
                for_pairs(dve, lambda w, k: (scale(w + 1, 1 - k), low(w, k)))
                low(W - 1, 0)

            @block.tensor
            def _(pe):
                def turn(w, k):
                    pe.wait_ge(scaled, w + 1)
                    wait_pos(pe, t_low, w - 1)
                    for t in range(2):
                        last = nc.tensor.transpose(ps[:, k, t * P:(t + 1) * P], hn[:, k, t * P:(t + 1) * P],
                                                   self.ident[:])
                    last.then_inc(turned, 1)
                for_pairs(pe, turn)
                turn(W - 1, 0)

        log_in, scored, logits = (self.sem(n + x) for x in ("log_in", "scored", "logits"))
        max_ready, exp_ready, e_high, e_low = (self.sem(n + x) for x in ("max", "exp", "ehigh", "elow"))
        e_turned, moved_a, moved_v = (self.sem(n + x) for x in ("eturned", "moved_a", "moved_v"))
        mixed, done, chain = (self.sem(n + x) for x in ("mixed", "done", "chain"))
        BY_ACT = [True, True, True, False, True, False, True]
        A_MOVES, V_MOVES = sum(BY_ACT), len(BY_ACT) - sum(BY_ACT)
        G = len(GROUPS)
        with ExitStack() as ctx:
            lc = self.sb(ctx, n + "lc", [P, NPAD])
            L = self.sb(ctx, n + "L", [P, NPAD])
            Ex = self.sb(ctx, n + "E", [P, NPAD])
            parts = [self.sb(ctx, n + f"e{x}", [P, 2, NPAD], F16) for x in ("hi", "lo")]
            PT = self.sb(ctx, n + "PT", [P, W, 2, P], F16)
            mx, neg, den, rden = (self.sb(ctx, n + x, [P, 2]) for x in ("mx", "neg", "den", "rden"))
            table = self.io["counts"][0:CELLS, :].rearrange("(w p f) o -> w p (f o)", p=P, f=NPAD)
            block = ctx.enter_context(nc.Block())

            def bank16(g):
                return ps[:, 4 + g % 2, :].bitcast(F16)

            @block.sync
            def _(sp):
                def load(w, k):
                    wait_pos(sp, logits, NSC * w)
                    sp.dma_start(lc[:], table[bass.ds(w, 1), :, :].rearrange("w p f -> p (w f)")).then_inc(log_in, 16)
                for_pairs(sp, load)
                load(W - 1, 0)

            @block.tensor
            def _(pe):
                def scores(w):
                    for c in range(NSC):
                        wait_pos(pe, logits, NSC * w + c - 3)
                        cols = slice(c * SC, (c + 1) * SC)
                        q = bass.ds(w * P, P)
                        for t in range(2):
                            for a, b in ((0, 0), (0, 1), (1, 0)):
                                last = nc.tensor.matmul(ps[:, c % 4, 0:SC], T[a][:, t, q], T[b][:, t, cols],
                                                        start=(t, a, b) == (0, 0, 0), stop=(t, a) == (1, 1))
                        last.then_inc(scored, 1)

                def turn(w, k, g):
                    t0, m = GROUPS[g]
                    for t in range(m):
                        for h in range(2):
                            last = nc.tensor.transpose(bank16(g)[:, (2 * t + h) * P:(2 * t + h + 1) * P],
                                                       parts[h][:, k, (t0 + t) * P:(t0 + t + 1) * P],
                                                       self.ident16[:])
                    last.then_inc(e_turned, 1)

                def mix(w, k):
                    pe.wait_ge(e_high, w + 1)
                    pe.wait_ge(e_low, w + 1)
                    wait_pos(pe, done, w - 1)
                    turn(w, k, 0)
                    for g, (t0, m) in enumerate(GROUPS):
                        if g + 1 < G:
                            turn(w, k, g + 1)
                        if BY_ACT[g]:
                            pe.wait_ge(moved_a, A_MOVES * w + sum(BY_ACT[:g + 1]))
                        else:
                            pe.wait_ge(moved_v, V_MOVES * w + g + 1 - sum(BY_ACT[:g + 1]))
                        for t in range(t0, t0 + m):
                            for a, b in ((0, 0), (0, 1), (1, 0)):
                                last = nc.tensor.matmul(ps[:, 6 + k, 0:D], PT[:, t, a, :], HS[b][:, t, :],
                                                        start=(t, a, b) == (0, 0, 0), stop=(t, a) == (W - 1, 1))
                    last.then_inc(mixed, 1)

                scores(0)
                for_pairs(pe, lambda w, k: (scores(w + 1), mix(w, k)))
                mix(W - 1, 0)

            def move(w, k, g):
                t0, m = GROUPS[g]
                return PT[:, t0:t0 + m, :, :].rearrange("p t h n -> p (t h n)"), bank16(g)[:, 0:m * 2 * P]

            @block.scalar
            def _(act):
                def moves(w, k, groups):
                    for g in groups:
                        act.wait_ge(e_turned, G * w + g + 1)
                        out_, in_ = move(w, k, g)
                        nc.scalar.copy(out_, in_).then_inc(moved_a, 1)

                def exps(w, k):
                    act.wait_ge(max_ready, w + 1)
                    wait_pos(act, e_low, w)
                    nc.scalar.activation(Ex[:], L[:], ACT.Exp, bias=neg[:, k:k + 1],
                                         accum_out=den[:, k:k + 1]).then_inc(exp_ready, 1)

                def high(w, k):
                    act.wait_ge(exp_ready, w + 1)
                    wait_pos(act, e_turned, G * (w - 1))
                    nc.scalar.copy(parts[0][:, k, :], Ex[:]).then_inc(e_high, 1)

                exps(0, 0)
                high(0, 0)
                for_pairs(act, lambda w, k: (moves(w, k, [0, 1, 2]), exps(w + 1, 1 - k), moves(w, k, [4]),
                                             high(w + 1, 1 - k), moves(w, k, [6])))
                moves(W - 1, 0, [0, 1, 2, 4, 6])

            @block.vector
            def _(dve):
                def logit(w, k):
                    dve.wait_ge(log_in, 16 * (w + 1))
                    wait_pos(dve, exp_ready, w)
                    for c in range(NSC):
                        cols = slice(c * SC, (c + 1) * SC)
                        dve.wait_ge(scored, NSC * w + c + 1)
                        nc.vector.scalar_tensor_tensor(L[:, cols], ps[:, c % 4, 0:SC], betas[:, layer:layer + 1],
                                                       lc[:, cols], ALU.mult, ALU.add).then_inc(logits, 1)
                    dve.wait_ge(logits, NSC * (w + 1))
                    t = Tally(chain, w * 3 - 2 if not isinstance(w, int) or w else 0)
                    t.link(dve, nc.vector.tensor_reduce(mx[:, k:k + 1], L[:], AX.X, ALU.max))
                    nc.vector.tensor_scalar(neg[:, k:k + 1], mx[:, k:k + 1], -1.0, None,
                                            ALU.mult).then_inc(max_ready, 1)

                def moves(w, k):
                    for g in (3, 5):
                        dve.wait_ge(e_turned, G * w + g + 1)
                        out_, in_ = move(w, k, g)
                        nc.vector.tensor_copy(out_, in_).then_inc(moved_v, 1)

                def low(w, k):
                    dve.wait_ge(e_high, w + 1)
                    wait_pos(dve, e_turned, G * (w - 1))
                    nc.vector.tensor_tensor(parts[1][:, k, :], Ex[:], parts[0][:, k, :],
                                            ALU.subtract).then_inc(e_low, 1)

                def finish(w, k):
                    t = Tally(chain, w * 3 + (1 if isinstance(w, int) and w == W - 1 else 2))
                    t.link(dve, nc.vector.reciprocal(rden[:, k:k + 1], den[:, k:k + 1]))
                    t.link(dve, nc.vector.scalar_tensor_tensor(rden[:, k:k + 1], mx[:, k:k + 1], 0.1 * NO_EDGE,
                                                               rden[:, k:k + 1], ALU.is_gt, ALU.mult))
                    dve.wait_ge(mixed, w + 1)
                    nc.vector.tensor_scalar(window(out, w), ps[:, 6 + k, 0:D], rden[:, k:k + 1], 0.0, ALU.mult,
                                            ALU.max).then_inc(done, 1)

                logit(0, 0)
                low(0, 0)
                for_pairs(dve, lambda w, k: (logit(w + 1, 1 - k), moves(w, k), low(w + 1, 1 - k), finish(w, k)))
                moves(W - 1, 0)
                finish(W - 1, 0)

    def load_betas(self, betas):
        nc = self.nc
        loaded, scaled = self.sem("beta_in"), self.sem("beta_scaled")
        with nc.Block() as block:
            @block.sync
            def _(sp):
                sp.dma_start(betas[:], self.io["betas"].to_broadcast([P, 4])).then_inc(loaded, 16)

            @block.vector
            def _(dve):
                dve.wait_ge(loaded, 16)
                nc.vector.tensor_scalar(betas[:], betas[:], 1.0 / (SN * SN), None, ALU.mult).then_inc(scaled, 1)

    def add_norm(self, tag, Z):
        nc = self.nc
        summed = self.sem(tag + "_summed")
        with ExitStack() as ctx:
            Y = self.sb(ctx, tag + "_Y", [P, W, D])
            scalar_part, vector_begin, vector_part, _ = self.norm_end(ctx, tag, Y)
            block = ctx.enter_context(nc.Block())

            @block.scalar
            def _(act):
                scalar_part(act)

            @block.vector
            def _(dve):
                vector_begin(dve)

                nc.vector.tensor_tensor(Y[:], self.X[:], Z[:], ALU.add).then_inc(summed, 1)
                vector_part(dve, summed, 1)

    def attribute_sums(self):
        nc, io, ps = self.nc, self.io, self.ps
        C = MUL + 1
        SRING, SUNROLL = 4, 8
        SITERS = STEPS // SUNROLL
        lda = [self.sem(f"s_attr_in{k}") for k in range(SRING)]
        ldi = [self.sem(f"s_ids_in{c}") for c in range(2)]
        tab = [self.sem(f"s_table{k}") for k in range(TABLES)]
        once, consts, spared = self.sem("s_once"), self.sem("s_consts"), self.sem("s_spared")
        equal, merged, copied = self.sem("s_equal"), self.sem("s_merged"), self.sem("s_copied")
        placed, chain, tick, ids_used = self.sem("s_placed"), self.sem("s_chain"), self.sem("s_tick"), self.sem("s_used")
        with ExitStack() as ctx:
            sb = lambda name, shape, dt=F32: self.sb(ctx, name, shape, dt)
            attr = sb("s_attr", [P, SRING, C])
            ids = sb("s_ids", [P, 2, 4 * P], I32)
            idf = sb("s_idf", [P, 2, 4 * P])
            src_i = sb("s_src_i", [P, STEPS], I32)
            srcf = sb("s_srcf", [P, STEPS])
            spare = sb("s_spare", [P, STEPS])
            base = sb("s_base", [P, TABLES])
            dump = sb("s_dump", [P, TABLES])
            home = sb("s_home", [P, 2, 4])
            same = sb("s_same", [P, SRING, P])
            junk = sb("s_junk", [P, SRING, P])
            earlier = sb("s_earlier", [P, 2, 4])
            skip = sb("s_skip", [P, 2, 4])
            keep = sb("s_keep", [P, 2, 4])
            spot = sb("s_spot", [P, 2, 4])
            place = sb("s_place", [P, 2, 4], I32)
            total = sb("s_total", [P, SRING, C])
            block = ctx.enter_context(nc.Block())

            def loop(eng, body):
                body(0)
                with eng.Fori(1, SITERS) as i:
                    body(i)

            @block.sync
            def _(sp):
                sp.dma_start(src_i[:], io["src_t"]).then_inc(once, 16)

                def body(i):
                    for j in range(SUNROLL):
                        s, k = i * SUNROLL + j, j % SRING
                        if j % 4 == 0:
                            c = j // 4
                            wait_pos(sp, ids_used, i * 2 + c - 1)
                            sp.dma_start(ids[:, c, :], io["ids"][0:1, bass.ds((i * 2 + c) * 4 * P, 4 * P)]
                                         .to_broadcast([P, 4 * P])).then_inc(ldi[c], 16)
                        wait_pos(sp, merged, s - SRING + 1)
                        sp.dma_start(attr[:, k, 0:MUL],
                                     io["attr64"][bass.ds(s * P, P), :]).then_inc(lda[k], 16)
                loop(sp, body)

            @block.gpsimd
            def _(pool):
                nc.gpsimd.memset(attr[:, :, MUL:C], 1.0).then_inc(consts, 1)
                nc.gpsimd.iota(base[:], [[TROWS, TABLES]], base=0, channel_multiplier=0,
                               allow_small_or_imprecise_dtypes=True)
                nc.gpsimd.iota(dump[:], [[TROWS, TABLES]], base=NPAD, channel_multiplier=1,
                               allow_small_or_imprecise_dtypes=True).then_inc(consts, 1)

                def body(i):
                    for j in range(SUNROLL):
                        s, k, c, t = i * SUNROLL + j, j % SRING, j // 4, j % 4
                        pool.wait_ge(copied, s + 1)
                        pool.sem_inc(tick, 1)
                        if t == 0:
                            pool.wait_ge(placed, i * 2 + c + 1)
                            pool.sem_inc(tick, 1)
                        if not (isinstance(i, int) and j < TABLES):
                            pool.wait_ge(tab[k], 16 * (i * 2 + c))
                            pool.sem_inc(tick, 1)
                        pool.indirect_dma_start(
                            out=io["sums"], out_offset=bass.IndirectOffsetOnAxis(ap=place[:, c, t:t + 1], axis=0),
                            in_=total[:, k, :], in_offset=None, compute_op=ALU.add).then_inc(tab[k], 16)
                loop(pool, body)
                for k in range(TABLES):
                    pool.wait_ge(tab[k], 16 * (STEPS // TABLES))

            @block.vector
            def _(dve):
                dve.wait_ge(once, 16)
                dve.wait_ge(consts, 2)
                nc.vector.tensor_copy(srcf[:], src_i[:]).then_inc(spared, 1)
                dve.wait_ge(spared, 1)
                nc.vector.tensor_scalar(spare[:], srcf[:], float(N), None, ALU.is_ge).then_inc(spared, 1)
                dve.wait_ge(spared, 2)
                LINKS = 2 * 3

                def body(i):
                    t = Tally(chain, i * LINKS)
                    for c in range(2):
                        dve.wait_ge(ldi[c], 16 * (i + 1))
                        nc.vector.tensor_copy(idf[:, c, :], ids[:, c, :]).then_inc(ids_used, 1)
                        dve.wait_ge(ids_used, i * 2 + c + 1)
                        for q in range(4):
                            mine = srcf[:, bass.ds(i * SUNROLL + 4 * c + q, 1)]
                            row = idf[:, c, q * P:(q + 1) * P]
                            wait_pos(dve, merged, i * SUNROLL + 4 * c + q - SRING + 1)
                            nc.vector.tensor_scalar(same[:, q, :], row, mine, None, ALU.is_equal).then_inc(equal, 1)
                            last = nc.vector.scalar_tensor_tensor(junk[:, q, :], row, mine, self.lower[:],
                                                                  ALU.is_equal, ALU.mult,
                                                                  accum_out=earlier[:, c, q:q + 1])
                        t.link(dve, last)
                        cols = bass.ds(i * SUNROLL + 4 * c, 4)
                        nc.vector.scalar_tensor_tensor(home[:, c, :], srcf[:, cols], 0.0, base[:], ALU.add, ALU.add)
                        t.link(dve, nc.vector.scalar_tensor_tensor(skip[:, c, :], earlier[:, c, :], 0.5,
                                                                   spare[:, cols], ALU.is_gt, ALU.max))
                        nc.vector.scalar_tensor_tensor(keep[:, c, :], skip[:, c, :], 0.0, home[:, c, :],
                                                       ALU.is_equal, ALU.mult)
                        t.link(dve, nc.vector.tensor_tensor(spot[:, c, :], skip[:, c, :], dump[:], ALU.mult))
                        if not (isinstance(i, int) and i == 0):
                            for k in range(TABLES):
                                dve.wait_ge(tab[k], 16 * (2 * i + c - 1))
                        nc.vector.tensor_tensor(place[:, c, :], spot[:, c, :], keep[:, c, :],
                                                ALU.add).then_inc(placed, 1)
                loop(dve, body)

            @block.tensor
            def _(pe):
                def body(i):
                    for j in range(SUNROLL):
                        s, k = i * SUNROLL + j, j % SRING
                        pe.wait_ge(equal, s + 1)
                        pe.wait_ge(lda[k], 16 * (i * 2 + j // 4 + 1))
                        wait_pos(pe, copied, s - 1)
                        nc.tensor.matmul(ps[:, j % 2, 0:C], same[:, k, :], attr[:, k, :], start=True,
                                         stop=True).then_inc(merged, 1)
                loop(pe, body)

            @block.scalar
            def _(act):
                def body(i):
                    for j in range(SUNROLL):
                        s, k = i * SUNROLL + j, j % SRING
                        act.wait_ge(merged, s + 1)
                        if not (isinstance(i, int) and j < SRING):
                            act.wait_ge(tab[k], 16 * (i * 2 + j // 4))
                        nc.scalar.copy(total[:, k, :], ps[:, j % 2, 0:C]).then_inc(copied, 1)
                loop(act, body)

    def layer2_nodes(self):
        nc, io, ps = self.nc, self.io, self.ps
        C = MUL + 1
        KH = HID // P
        loaded, u_ready, bias_sum, bias_ready = (self.sem("g_" + x) for x in ("loaded", "u", "bsum", "bias"))
        tab_in, mean_ready, turned, moved = (self.sem("g_" + x) for x in ("tab", "mean", "turned", "moved"))
        hid_ready, hid_moved, o_ready, resid, chain, consts, staged = (self.sem("g_" + x) for x in (
            "hid", "hmoved", "o", "resid", "chain", "consts", "staged"))
        with ExitStack() as ctx:
            sb = lambda name, shape, dt=F32: self.sb(ctx, name, shape, dt)
            W1x = sb("W1x", [P, 2, HID])
            W1a = sb("W1a", [MUL, HID])
            W1u = sb("W1u", [P, HID])
            W2 = sb("W2", [P, KH, D])
            ucol = sb("ucol", [P, 1])
            b1 = sb("b1", [P, KH])
            bias = sb("bias", [P, KH])
            b2 = sb("b2", [1, D])
            ones = sb("g_ones", [1, P])
            tabs = sb("tabs", [P, 4, TABLES, C])
            pair = sb("g_pair", [P, 4, 2, C])
            summ = sb("g_sum", [P, 4, C])
            inv = sb("g_inv", [P, 4])
            mean = sb("g_mean", [P, 4, P])
            stage = sb("g_stage", [P, 4, D])
            xT = sb("xT", [P, 3, 4 * P])
            hid = sb("g_hidT", [P, KH, 4 * P])
            Y = sb("Yg", [P, W, D])
            scalar_part, vector_begin, vector_part, _ = self.norm_end(ctx, "gn", Y)
            sums = io["sums"].rearrange("(t r) c -> t r c", t=TABLES)
            block = ctx.enter_context(nc.Block())

            def loop(eng, body):
                body(0, 4)
                with eng.Fori(1, W // 4) as i:
                    body(i, 4)
                body(W // 4, W % 4)

            @block.sync
            def _(sp):
                sp.dma_start(W1x[:], io["W1"][0:D, :].rearrange("(t p) n -> p t n", p=P)).then_inc(loaded, 16)
                sp.dma_start(W1a[:], io["W1"][D:D + MUL, :]).then_inc(loaded, 16)
                sp.dma_start(W1u[:], io["W1"][D + MUL:D + MUL + P, :]).then_inc(loaded, 16)
                sp.dma_start(W2[:], io["W2"].rearrange("(t p) n -> p t n", p=P)).then_inc(loaded, 16)
                sp.dma_start(ucol[:], io["u"][0:1, :].rearrange("o p -> p o"),
                             allow_slow_non_contiguous=True).then_inc(loaded, 16)
                sp.dma_start(b1[:], io["b1"]).then_inc(loaded, 16)
                sp.dma_start(b2[:], io["b2"]).then_inc(loaded, 16)

                def body(i, m):
                    wait_pos(sp, mean_ready, i)
                    for w in range(m):
                        sp.dma_start(tabs[:, w, :, :],
                                     sums[:, bass.ds((i * 4 + w) * P, P), :].rearrange("t p c -> p t c")
                                     ).then_inc(tab_in, 16)
                loop(sp, body)

            @block.gpsimd
            def _(pool):
                def body(i, m):
                    wait_pos(pool, turned, 3 * i)
                    nc.gpsimd.tensor_copy(stage[:, 0:m, :], self.X[:, bass.ds(i * 4, m), :]).then_inc(staged, 1)
                loop(pool, body)

            @block.vector
            def _(dve):
                vector_begin(dve)
                nc.vector.memset(mean[:], 0.0)
                nc.vector.memset(ones[:], 1.0).then_inc(consts, 1)
                dve.wait_ge(consts, 1)
                dve.wait_ge(loaded, 112)
                dve.wait_ge(bias_sum, 1)
                nc.vector.tensor_tensor(bias[:], ps[:, 7, 0:KH], b1[:], ALU.add).then_inc(bias_ready, 1)

                def means(t, i, m):
                    dve.wait_ge(tab_in, 64 * i + 16 * m)
                    t.link(dve, nc.vector.tensor_tensor(pair[:, 0:m], tabs[:, 0:m, 0:2, :], tabs[:, 0:m, 2:4, :],
                                                        ALU.add))
                    t.link(dve, nc.vector.tensor_tensor(summ[:, 0:m], pair[:, 0:m, 0, :], pair[:, 0:m, 1, :],
                                                        ALU.add))
                    t.link(dve, nc.vector.tensor_scalar(inv[:, 0:m], summ[:, 0:m, MUL], 1.0, None, ALU.max))
                    t.link(dve, nc.vector.reciprocal(inv[:, 0:m], inv[:, 0:m]))
                    wait_pos(dve, moved, 3 * i)
                    for w in range(m):
                        last = nc.vector.tensor_scalar(mean[:, w, 0:MUL], summ[:, w, 0:MUL], inv[:, w:w + 1], None,
                                                       ALU.mult)
                    last.then_inc(mean_ready, 1)

                def body(i, m):
                    t = Tally(chain, i * 4)
                    means(t, i, m)
                    for w in range(m):
                        dve.wait_ge(o_ready, 4 * i + w + 1)
                        y = window(Y, 4 * i + w)
                        nc.vector.tensor_tensor(y, ps[:, 5 + w % 2, 0:D], window(self.X, 4 * i + w),
                                                ALU.add).then_inc(resid, 1)
                loop(dve, body)
                vector_part(dve, resid, W)

            @block.tensor
            def _(pe):
                pe.wait_ge(loaded, 112)
                pe.wait_ge(consts, 1)
                for t in range(KH):
                    last = nc.tensor.matmul(ps[:, 7, t:t + 1], W1u[:, t * P:(t + 1) * P], ucol[:], start=True,
                                            stop=True)
                last.then_inc(bias_sum, 1)

                def body(i, m):
                    n = m * P
                    pe.wait_ge(staged, i + 1)
                    for t in range(2):
                        for w in range(m):
                            last = nc.tensor.transpose(ps[:, t, w * P:(w + 1) * P],
                                                       stage[:, w, t * P:(t + 1) * P], self.ident[:])
                        last.then_inc(turned, 1)
                    pe.wait_ge(mean_ready, i + 1)
                    for w in range(m):
                        last = nc.tensor.transpose(ps[:, 2, w * P:(w + 1) * P], mean[:, w, :], self.ident[:])
                    last.then_inc(turned, 1)
                    pe.wait_ge(moved, 3 * i + 3)
                    for h in range(KH):
                        if h >= 2:
                            pe.wait_ge(hid_moved, KH * i + h - 1)
                        cols = slice(h * P, (h + 1) * P)
                        out = ps[:, 3 + h % 2, 0:n]
                        nc.tensor.matmul(out, W1x[:, 0, cols], xT[:, 0, 0:n], start=True, stop=False)
                        nc.tensor.matmul(out, W1x[:, 1, cols], xT[:, 1, 0:n], start=False, stop=False)
                        nc.tensor.matmul(out, W1a[:, cols], xT[0:MUL, 2, 0:n], start=False,
                                         stop=True).then_inc(hid_ready, 1)
                    pe.wait_ge(hid_moved, KH * (i + 1))
                    for w in range(m):
                        wait_pos(pe, resid, 4 * i + w - 1)
                        out = ps[:, 5 + w % 2, 0:D]
                        for h in range(KH):
                            nc.tensor.matmul(out, hid[:, h, w * P:(w + 1) * P], W2[:, h, :], start=h == 0, stop=False)
                        nc.tensor.matmul(out, ones[:], b2[:], start=False, stop=True).then_inc(o_ready, 1)
                loop(pe, body)

            @block.scalar
            def _(act):
                act.wait_ge(bias_ready, 1)

                def body(i, m):
                    n = m * P
                    wait_pos(act, o_ready, 4 * i)
                    for t in range(3):
                        rows = P if t < 2 else MUL
                        act.wait_ge(turned, 3 * i + t + 1)
                        nc.scalar.copy(xT[0:rows, t, 0:n], ps[0:rows, t, 0:n]).then_inc(moved, 1)
                    for h in range(KH):
                        act.wait_ge(hid_ready, KH * i + h + 1)
                        nc.scalar.activation(hid[:, h, 0:n], ps[:, 3 + h % 2, 0:n], ACT.Relu,
                                             bias=bias[:, h:h + 1]).then_inc(hid_moved, 1)
                loop(act, body)
                scalar_part(act)

    def layer3_edges(self, AGG):
        nc, io, ps = self.nc, self.io, self.ps
        ld = [self.sem(f"h_edges_in{k}") for k in range(RING)]
        xg = [self.sem(f"h_rows_in{k}") for k in range(RING)]
        once, biased, stored, zeroed = (self.sem("h_" + x) for x in ("once", "biased", "stored", "zeroed"))
        edge_ready, pre_ready, msg_ready, hot = (self.sem("h_" + x) for x in ("edge", "pre", "msg", "hot"))
        summed, added, locals_ready, tick = (self.sem("h_" + x) for x in ("summed", "added", "locals", "tick"))
        with ExitStack() as ctx:
            sb = lambda name, shape, dt=F32: self.sb(ctx, name, shape, dt)
            We = sb("We", [P, D])
            be = sb("be", [P, D])
            XB = sb("XB", [P, W, D])
            sd = sb("h_sd", [P, RING, 2], I32)
            attr = sb("h_attr", [P, RING, P])
            rows = sb("h_rows", [P, RING, D])
            pre = sb("h_pre", [P, 2, D])
            msg = sb("h_msg", [P, 4, D])
            dl = sb("h_dl", [P, 2, 4])
            oh = sb("h_oh", [P, 4, P])
            block = ctx.enter_context(nc.Block())

            @block.sync
            def _(sp):
                sp.dma_start(We[:], io["W_edge"]).then_inc(once, 16)
                sp.dma_start(be[:], io["b_edge"].to_broadcast([P, D])).then_inc(once, 16)
                sp.wait_ge(biased, W)
                sp.dma_start(io["rows3"].rearrange("(w p) d -> p w d", p=P), XB[:]).then_inc(stored, 16)

                def body(i):
                    for k in range(UNROLL):
                        s = i * UNROLL + k
                        wait_pos(sp, summed, s - RING + 1)
                        o = sp.value_load(self.off[0:1, bass.ds(s, 1)], min_val=0, max_val=EP - P)
                        sp.dma_start(sd[:, k, :], io["sd"][bass.ds(o, P), :]).then_inc(ld[k], 16)
                        sp.dma_start(attr[:, k, :], io["attr128"][:, bass.ds(o, P)]).then_inc(ld[k], 16)
                body(0)
                with sp.Fori(1, ITERS) as i:
                    body(i)

            @block.gpsimd
            def _(pool):
                pool.wait_ge(stored, 16)
                pool.sem_inc(tick, 1)

                def body(i):
                    for k in range(UNROLL):
                        pool.wait_ge(ld[k], 32 * (i + 1))
                        pool.sem_inc(tick, 1)
                        pool.indirect_dma_start(
                            out=rows[:, k, :], out_offset=None, in_=io["rows3"],
                            in_offset=bass.IndirectOffsetOnAxis(ap=sd[:, k, 0:1], axis=0)).then_inc(xg[k], 16)
                body(0)
                with pool.Fori(1, ITERS) as i:
                    body(i)

            @block.tensor
            def _(pe):
                pe.wait_ge(once, 32)

                def edge(i, k):
                    s = i * UNROLL + k
                    pe.wait_ge(ld[k], 32 * (i + 1))
                    wait_pos(pe, pre_ready, s - 1)
                    nc.tensor.matmul(ps[:, k % 2, 0:D], attr[:, k, :], We[:], start=True,
                                     stop=True).then_inc(edge_ready, 1)

                def body(i, last=False):
                    for k in range(UNROLL):
                        s = i * UNROLL + k
                        if not (last and k + 1 == UNROLL):
                            edge(*((i, k + 1) if k + 1 < UNROLL else (i + 1, 0)))
                        pe.wait_ge(msg_ready, s + 1)
                        pe.wait_ge(hot, s + 1)
                        wait_pos(pe, added, s - 1)
                        nc.tensor.matmul(ps[:, 2 + k % 2, 0:D], oh[:, k % 4, :], msg[:, k % 4, :], start=True,
                                         stop=True).then_inc(summed, 1)
                edge(0, 0)
                body(0)
                with pe.Fori(1, ITERS - 1) as i:
                    body(i)
                body(ITERS - 1, last=True)

            @block.scalar
            def _(act):
                def body(i):
                    for k in range(UNROLL):
                        s = i * UNROLL + k
                        act.wait_ge(pre_ready, s + 1)
                        wait_pos(act, summed, s - 3)
                        nc.scalar.activation(msg[:, k % 4, :], pre[:, k % 2, :], ACT.Relu).then_inc(msg_ready, 1)
                body(0)
                with act.Fori(1, ITERS) as i:
                    body(i)

            @block.vector
            def _(dve):
                dve.wait_ge(once, 32)
                nc.vector.memset(AGG[:], 0.0).then_inc(zeroed, 1)
                with dve.Fori(0, W) as w:
                    nc.vector.tensor_tensor(window(XB, w), window(self.X, w), be[:], ALU.add).then_inc(biased, 1)
                dve.wait_ge(zeroed, 1)

                def local(i, b):
                    g, k0, it = i * GB + b, (4 * b) % RING, i + b // GB
                    for k in range(k0, k0 + 4):
                        dve.wait_ge(ld[k], 32 * (it + 1))
                    nc.vector.tensor_tensor(dl[:, b % 2, :], sd[:, k0:k0 + 4, 1],
                                            self.win_col[:, bass.ds(g * 4, 4)],
                                            ALU.subtract).then_inc(locals_ready, 1)

                def add(s, p):
                    w = dve.value_load(self.win[0:1, bass.ds(s, 1)], min_val=0, max_val=W - 1)
                    dve.wait_ge(summed, s + 1)
                    wait_pos(dve, added, s)
                    a = window(AGG, w)
                    nc.vector.tensor_tensor(a, a, ps[:, 2 + p, 0:D], ALU.add).then_inc(added, 1)

                def body(i, first=False, last=False):
                    for k in range(UNROLL):
                        s, b, q = i * UNROLL + k, k // 4, k % 4
                        if q == 0:
                            dve.wait_ge(locals_ready, i * GB + b + 1)
                        nc.vector.tensor_scalar(oh[:, q, :], self.iota[:], dl[:, b % 2, q:q + 1], None,
                                                ALU.is_equal).then_inc(hot, 1)
                        if q == 2 and not (last and b + 1 == GB):
                            local(i, b + 1)
                        dve.wait_ge(xg[k], 16 * (i + 1))
                        dve.wait_ge(edge_ready, s + 1)
                        wait_pos(dve, msg_ready, s - 1)
                        nc.vector.tensor_tensor(pre[:, k % 2, :], ps[:, k % 2, 0:D], rows[:, k, :],
                                                ALU.add).then_inc(pre_ready, 1)
                        if not (first and k == 0):
                            add(s - 1, (k - 1) % 2)
                local(0, 0)
                body(0, first=True)
                with dve.Fori(1, ITERS - 1) as i:
                    body(i)
                body(ITERS - 1, last=True)
                add(STEPS - 1, 1)

    def layer3_nodes(self, AGG):
        nc, io, ps = self.nc, self.io, self.ps
        loaded, eps1, h_ready, turned, moved = (self.sem("i_" + x) for x in ("loaded", "eps1", "h", "turned", "moved"))
        z1, r1, z2, r2 = (self.sem("i_" + x) for x in ("z1", "r1", "z2", "r2"))
        chain, bvar, bstd, coef, act_done, back, resid = (self.sem("i_" + x) for x in (
            "chain", "bvar", "bstd", "coef", "act", "back", "resid"))
        stored, bn_eps = self.sem("i_stored"), self.sem("i_bneps")
        CH = [(c, min(512, N - c)) for c in range(0, N, 512)]
        with ExitStack() as ctx:
            sb = lambda name, shape, dt=F32: self.sb(ctx, name, shape, dt)
            V1, V2 = sb("V1", [P, 2, D]), sb("V2", [P, 2, D])
            c1, c2, gamma, beta = (sb("i_" + x, [P, 2]) for x in ("c1", "c2", "gamma", "beta"))
            eps = sb("i_eps", [P, 1])
            beps = sb("i_beps", [P, 1])
            stage = sb("i_stage", [P, 4 * D])
            zr = sb("zr", [P, 2, 2, P])
            hT = sb("hT", [P, 2, 512])
            gT = sb("gT", [P, 2, 512])
            Z = sb("Zi", [P, 2, NPAD])
            bst = sb("i_bst", [P, 2, len(CH), 6])
            bmv = sb("i_bmv", [P, 2, 2])
            bsd = sb("i_bsd", [P, 2])
            mul, shf = sb("i_mul", [P, 2]), sb("i_shf", [P, 2])
            Y = sb("Yi", [P, W, D])
            scalar_part, vector_begin, vector_part, written = self.norm_end(ctx, "last", Y)
            block = ctx.enter_context(nc.Block())

            def loop(eng, body):
                body(0, 4)
                with eng.Fori(1, W // 4) as i:
                    body(i, 4)
                body(W // 4, W % 4)

            @block.sync
            def _(sp):
                for name, tile in (("V1", V1), ("V2", V2)):
                    sp.dma_start(tile[:], io[name].rearrange("(t p) n -> p t n", p=P)).then_inc(loaded, 16)
                for name, tile in (("c1", c1), ("c2", c2), ("gamma", gamma), ("beta", beta)):
                    sp.dma_start(tile[:], io[name]).then_inc(loaded, 16)
                sp.dma_start(eps[:], io["eps"].to_broadcast([P, 1])).then_inc(loaded, 16)
                sp.wait_ge(written, W)
                sp.dma_start(io["out"][0:(W - 1) * P, :].rearrange("(w p) d -> p w d", p=P),
                             self.X[:, 0:W - 1, :]).then_inc(stored, 16)
                sp.dma_start(io["out"][(W - 1) * P:N, :], self.X[0:TAIL, W - 1, :]).then_inc(stored, 16)
                sp.wait_ge(stored, 32)

            @block.vector
            def _(dve):
                vector_begin(dve)
                dve.wait_ge(loaded, 112)
                nc.vector.memset(beps[:], 1.0e-5).then_inc(bn_eps, 1)
                nc.vector.tensor_scalar(eps[:], eps[:], 1.0, None, ALU.add).then_inc(eps1, 1)
                dve.wait_ge(eps1, 1)

                def update(i, m):
                    wait_pos(dve, turned, 2 * i)
                    group = lambda x: x[:, bass.ds(i * 4, m), :].rearrange("p w d -> p (w d)")
                    nc.vector.scalar_tensor_tensor(stage[:, 0:m * D], group(self.X), eps[:], group(AGG),
                                                   ALU.mult, ALU.add).then_inc(h_ready, 1)
                loop(dve, update)
                t = Tally(chain, 0)
                dve.wait_ge(r2, 2 * (W // 4 + 1))
                for h in range(2):
                    for c, (lo, m) in enumerate(CH):
                        nc.vector.bn_stats(bst[:, h, c, :], Z[:, h, lo:lo + m])
                t.link(dve, nc.vector.engine_nop())
                for h in range(2):
                    nc.vector.bn_aggr(bmv[:, h, :], bst[:, h, :, :].rearrange("p c s -> p (c s)"))
                nc.vector.engine_nop().then_inc(bvar, 1)
                dve.wait_ge(bstd, 1)
                t.link(dve, nc.vector.reciprocal(bsd[:], bsd[:]))
                t.link(dve, nc.vector.tensor_tensor(mul[:], gamma[:], bsd[:], ALU.mult))
                t.link(dve, nc.vector.tensor_tensor(shf[:], bmv[:, :, 0], mul[:], ALU.mult))
                nc.vector.tensor_tensor(shf[:], beta[:], shf[:], ALU.subtract).then_inc(coef, 1)

                def residual(w, k):
                    dve.wait_ge(back, w + 1)
                    nc.vector.tensor_tensor(window(Y, w), ps[:, k, 0:D], window(self.X, w), ALU.add).then_inc(resid, 1)
                for_pairs(dve, residual)
                residual(W - 1, 0)
                vector_part(dve, resid, W)

            @block.tensor
            def _(pe):
                pe.wait_ge(loaded, 112)

                def body(i, m):
                    n = m * P
                    pe.wait_ge(h_ready, i + 1)
                    for t in range(2):
                        for w in range(m):
                            last = nc.tensor.transpose(ps[:, t, w * P:(w + 1) * P],
                                                       stage[:, w * D + t * P:w * D + (t + 1) * P], self.ident[:])
                        last.then_inc(turned, 1)
                    pe.wait_ge(moved, 2 * i + 2)
                    for h in range(2):
                        out = ps[:, 2 + h, 0:n]
                        for t in range(2):
                            last = nc.tensor.matmul(out, V1[:, t, h * P:(h + 1) * P], hT[:, t, 0:n], start=t == 0,
                                                    stop=t == 1)
                        last.then_inc(z1, 1)
                    pe.wait_ge(r1, 2 * i + 2)
                    for h in range(2):
                        wait_pos(pe, r2, 2 * i)
                        out = ps[:, 4 + h, 0:n]
                        for t in range(2):
                            last = nc.tensor.matmul(out, V2[:, t, h * P:(h + 1) * P], gT[:, t, 0:n], start=t == 0,
                                                    stop=t == 1)
                        last.then_inc(z2, 1)
                loop(pe, body)

                def turn(w, k):
                    pe.wait_ge(act_done, 2 * w + 2)
                    wait_pos(pe, resid, w - 1)
                    for h in range(2):
                        last = nc.tensor.transpose(ps[:, k, h * P:(h + 1) * P], zr[:, k, h, :], self.ident[:])
                    last.then_inc(back, 1)
                for_pairs(pe, turn)
                turn(W - 1, 0)

            @block.scalar
            def _(act):
                act.wait_ge(loaded, 112)

                def body(i, m):
                    n = m * P
                    wait_pos(act, z1, 2 * i)
                    for t in range(2):
                        act.wait_ge(turned, 2 * i + t + 1)
                        nc.scalar.copy(hT[:, t, 0:n], ps[:, t, 0:n]).then_inc(moved, 1)
                    wait_pos(act, z2, 2 * i)
                    for h in range(2):
                        act.wait_ge(z1, 2 * i + h + 1)
                        nc.scalar.activation(gT[:, h, 0:n], ps[:, 2 + h, 0:n], ACT.Relu,
                                             bias=c1[:, h:h + 1]).then_inc(r1, 1)
                    for h in range(2):
                        act.wait_ge(z2, 2 * i + h + 1)
                        nc.scalar.activation(Z[:, h, bass.ds(i * 512, n)], ps[:, 4 + h, 0:n], ACT.Identity,
                                             bias=c2[:, h:h + 1]).then_inc(r2, 1)
                loop(act, body)
                act.wait_ge(bvar, 1)
                act.wait_ge(bn_eps, 1)
                nc.scalar.activation(bsd[:], bmv[:, :, 1], ACT.Sqrt, bias=beps[:]).then_inc(bstd, 1)
                act.wait_ge(coef, 1)

                def relu(w, k):
                    wait_pos(act, back, w - 1)
                    for h in range(2):
                        nc.scalar.activation(zr[:, k, h, :], Z[:, h, bass.ds(w * P, P)], ACT.Relu,
                                             bias=shf[:, h:h + 1], scale=mul[:, h:h + 1]).then_inc(act_done, 1)
                for_pairs(act, relu)
                relu(W - 1, 0)
                scalar_part(act)


def gnn_stack(nc, io):
    with ExitStack() as ctx:
        prog = Program(nc, ctx, io)
        with ExitStack() as inner:
            prog.zeros = prog.sb(inner, "zeros", [P, NPAD])
            prog.setup()
            prog.end_stage()
            ACC = prog.sb(inner, "ACC", [P, W * ACW])
            prog.layer0_edges(ACC)
            prog.end_stage()
            prog.layer0_nodes(ACC)
            prog.end_stage()
        prog.log_counts()
        prog.end_stage()
        with ExitStack() as inner:
            H = prog.sb(inner, "H", [P, W, D])
            with ExitStack() as deep:
                T = [prog.sb(deep, f"T{x}", [P, 2, NPAD], F16) for x in ("hi", "lo")]
                HS = [prog.sb(deep, f"H{x}", [P, W, D], F16) for x in ("hi", "lo")]
                betas = prog.sb(deep, "betas", [P, 4])
                prog.load_betas(betas)
                prog.end_stage()
                for layer in range(4):
                    prog.attention(layer, H if layer else prog.X, H, T, HS, betas)
                    prog.end_stage()
            prog.add_norm("e", H)
            prog.end_stage()
        prog.attribute_sums()
        prog.end_stage()
        prog.layer2_nodes()
        prog.end_stage()
        with ExitStack() as inner:
            AGG = prog.sb(inner, "AGG", [P, W, D])
            prog.layer3_edges(AGG)
            prog.end_stage()
            prog.layer3_nodes(AGG)


def kernel(**inputs):
    import numpy as np
    import concourse.bacc as bacc
    from concourse.bass_utils import run_bass_kernel_spmd

    nc = bacc.Bacc("TRN2", target_bir_lowering=False, num_devices=1)
    a = {name: np.asarray(value) for name, value in inputs.items()}
    src, dst = a["src"], a["dst"]
    spare = EP - E
    src_in = np.concatenate([src, np.zeros(spare, src.dtype)])
    src_id = np.concatenate([src, np.full(spare, PAD_ID, src.dtype)])
    dst_id = np.concatenate([dst, np.full(spare, PAD_ID, dst.dtype)])
    rows = lambda v: np.concatenate([v, np.zeros((spare, v.shape[1]), v.dtype)])
    arrays = {
        "x": a["x"],
        "x_blocks": np.concatenate([a["x"][:, :MUL]] + [a["x"][:, MUL + m::3] for m in range(3)], axis=1),
        "sd": np.stack([src_in, dst_id], axis=1),
        "ids": np.stack([src_id, dst_id]),
        "src_t": src_id.reshape(STEPS, P).T,
        "dst_t": dst_id.reshape(STEPS, P).T,
        "attr4": rows(a["edge_attr_4"]),
        "emb": rows(a["edge_attr_10"]).T,
        "attr64": rows(a["edge_attr_64"]),
        "attr128": rows(a["edge_attr_128"]).T,
        "w_00_0": a["L0_gnn_w_00_0"], "w_11_0": a["L0_gnn_w_11_0"],
        "w_01_1": a["L0_gnn_w_01_1"], "w_10_1": a["L0_gnn_w_10_1"],
        "fc_w1": a["L0_gnn_fc_w1"], "fc_w2": a["L0_gnn_fc_w2"],
        "betas": a["L1_gnn_betas"].reshape(1, 4),
        "u": a["L2_gnn_u"], "W1": a["L2_gnn_W1"], "b1": a["L2_gnn_b1"].reshape(4, P).T,
        "W2": a["L2_gnn_W2"], "b2": a["L2_gnn_b2"].reshape(1, D),
        "W_edge": a["L3_gnn_W_edge"], "b_edge": a["L3_gnn_b_edge"].reshape(1, D),
        "V1": a["L3_gnn_W1"], "c1": a["L3_gnn_b1"].reshape(2, P).T,
        "V2": a["L3_gnn_W2"], "c2": a["L3_gnn_b2"].reshape(2, P).T,
        "eps": a["L3_gnn_eps"].reshape(1, 1),
        "gamma": a["L3_gnn_gamma"].reshape(2, P).T, "beta": a["L3_gnn_beta"].reshape(2, P).T,
    }
    arrays = {f"in_{name}": np.ascontiguousarray(value) for name, value in arrays.items()}
    io = {name[3:]: nc.dram_tensor(name, v.shape, mybir.dt.from_np(v.dtype), kind="ExternalInput").ap()
          for name, v in arrays.items()}
    io["counts"] = nc.dram_tensor("counts", (CELLS + 4 * P, 1), F32, kind="Internal").ap()
    io["sums"] = nc.dram_tensor("sums", (TABLES * TROWS, 65), F32, kind="Internal").ap()
    io["rows3"] = nc.dram_tensor("rows3", (NPAD, D), F32, kind="Internal").ap()
    io["out"] = nc.dram_tensor("out", (N, D), F32, kind="ExternalOutput").ap()
    gnn_stack(nc, io)
    result = run_bass_kernel_spmd(nc, [arrays], core_ids=[0])
    return result.results[0]["out"]
```

```python
import math
from contextlib import ExitStack

import concourse.bass as bass
from concourse import mybir

F32 = mybir.dt.float32
F16 = mybir.dt.float16
I32 = mybir.dt.int32
ALU = mybir.AluOpType
ACT = mybir.ActivationFunctionType
AX = mybir.AxisListType

P = 128
N = 3125
E = 50000
D = 256
MUL = 64
W = -(-N // P)
NPAD = W * P
TAIL = N - (W - 1) * P
SE = 2 * P
UNROLL = 8
ZEROED_FIRST = 12
LEAD = 4
STEPS = -(-((E + W * (SE - 1)) // SE) // UNROLL) * UNROLL
ITERS = STEPS // UNROLL
EP = STEPS * SE
PAIR_ITERS = -(-E // (SE * UNROLL))
PAIR_STEPS = PAIR_ITERS * UNROLL
PAIR_LAG = STEPS - PAIR_STEPS
PAIR_TILES = 2 * PAIR_STEPS
PAD_ID = 16384
CELLS = NPAD * NPAD
TROWS = NPAD + P
TABLES = 4
ACW = 640
NO_EDGE = -1.0e29
FLOOR = 1.0e-12
SC = 400
NSC = NPAD // SC
SN = 1024.0
GROUPS = [(g, min(4, W - g)) for g in range(0, W, 4)]
HID = 512


class Tally:

    def __init__(self, sem, base):
        self.sem, self.n = sem, base

    def link(self, eng, ins):
        ins.then_inc(self.sem, 1)
        self.n = self.n + 1
        eng.wait_ge(self.sem, self.n)


def wait_pos(eng, sem, value):
    if not (isinstance(value, int) and value <= 0):
        eng.wait_ge(sem, value)


def window(t, w):
    return t[:, bass.ds(w, 1), :].rearrange("p w d -> p (w d)")


def for_pairs(eng, body, n=W - 1):
    body(0, 0)
    body(1, 1)
    with eng.Fori(1, n // 2) as i:
        body(i * 2, 0)
        body(i * 2 + 1, 1)


def for_fives(eng, step):
    assert W % 5 == 0
    with eng.Fori(0, W // 5) as i:
        for k in range(5):
            step(i * 5 + k)


class Program:
    def __init__(self, nc, ctx, io):
        self.nc, self.ctx, self.io = nc, ctx, io
        self.sems = []
        self.ps = ctx.enter_context(nc.psum_tensor("ps", [P, 8, 512], F32))
        self.zeroed = nc.alloc_semaphore(name="zeroed")
        self.zero_count = 16 * (W + -(-TABLES * TROWS * 65 // (P * NPAD)))
        self.kept = nc.alloc_semaphore(name="kept")
        self.count_rows = io["counts"][0:CELLS, :].rearrange("(w p f) o -> w p (f o)", p=P, f=NPAD)
        self.X = self.sb(ctx, "X", [P, W, D])
        self.iota = self.sb(ctx, "iota", [P, P])
        self.lower = self.sb(ctx, "lower", [P, P])
        self.ident = self.sb(ctx, "ident", [P, P])
        self.ident16 = self.sb(ctx, "ident16", [P, P], F16)
        self.part = self.sb(ctx, "part", [P, 1])
        self.win_col = self.sb(ctx, "win_col", [P, STEPS])
        self.win = self.sb(ctx, "win", [P, STEPS], I32)
        self.off = self.sb(ctx, "off", [P, STEPS], I32)

    def sb(self, ctx, name, shape, dt=F32):
        return ctx.enter_context(self.nc.sbuf_tensor(name, shape, dt))

    def sem(self, name):
        self.sems.append(self.nc.alloc_semaphore(name=name))
        return self.sems[-1]

    def end_stage(self):
        self.nc.clear_and_free_semaphores(self.sems)
        self.sems = []
        self.nc.all_engine_barrier()

    def setup(self):
        nc, io = self.nc, self.io
        dst_in, x_in = self.sem("su_dst_in"), self.sem("su_x_in")
        consts, chain, sums, zero_ready = self.sem("su_consts"), self.sem("su_chain"), self.sem("su_sums"), self.sem("su_zero_ready")
        part_ready, xpad = self.sem("su_part"), self.sem("su_xpad")
        pchain = self.sem("su_pchain")
        with ExitStack() as ctx:
            sb = lambda name, shape, dt=F32: self.sb(ctx, name, shape, dt)
            zeros = self.zeros
            ones = sb("ones", [P, P])
            dst_all = sb("dst_all", [P, PAIR_TILES], I32)
            dstf = sb("dstf", [P, PAIR_TILES])
            junk = sb("junk", [P, 5, PAIR_TILES])
            late = sb("late", [P, 2, STEPS])
            step_no = sb("step_no", [P, STEPS])
            below = sb("below", [P, W + 1])
            start = sb("start", [P, W + 1])
            edges = sb("edges", [P, W])
            tiles_i = sb("tiles_i", [P, W], I32)
            tiles = sb("tiles", [P, W])
            first_step = sb("first_step", [P, W + 1])
            zero_w = sb("zero_w", [P, W])
            shift = sb("shift", [P, W])
            jump = sb("jump", [P, W])
            wsum = sb("wsum", [P, STEPS])
            osum = sb("osum", [P, STEPS])
            block = ctx.enter_context(nc.Block())

            @block.sync
            def _(sp):
                sp.dma_start(dst_all[:, :], io["dst_t"]).then_inc(dst_in, 16)
                sp.wait_ge(xpad, 1)
                sp.dma_start(self.X[:, 0:W - 1, :],
                             io["x"][0:(W - 1) * P, :].rearrange("(w p) d -> p w d", p=P)).then_inc(x_in, 16)
                sp.dma_start(self.X[0:TAIL, W - 1, :], io["x"][(W - 1) * P:N, :]).then_inc(x_in, 16)
                sp.wait_ge(zero_ready, 1)
                for w in range(ZEROED_FIRST):
                    sp.dma_start(self.count_rows[w], zeros[:]).then_inc(self.zeroed, 16)
                sp.wait_ge(x_in, 32)

            @block.gpsimd
            def _(pool):
                nc.gpsimd.memset(zeros[:], 0.0).then_inc(zero_ready, 1)
                nc.gpsimd.iota(self.iota[:], [[1, P]], base=0, channel_multiplier=0,
                               allow_small_or_imprecise_dtypes=True)
                nc.gpsimd.iota(step_no[:], [[1, STEPS]], base=0, channel_multiplier=0,
                               allow_small_or_imprecise_dtypes=True)
                nc.gpsimd.iota(self.part[:], [[1, 1]], base=0, channel_multiplier=1,
                               allow_small_or_imprecise_dtypes=True)
                nc.gpsimd.memset(ones[:], 1.0).then_inc(pchain, 1)
                pool.wait_ge(pchain, 1)
                nc.gpsimd.affine_select(self.lower[:], ones[:], [[-1, P]], ALU.is_gt, 0.0, base=0,
                                        channel_multiplier=1)
                nc.gpsimd.affine_select(self.ident[:], ones[:], [[-1, P]], ALU.is_equal, 0.0, base=0,
                                        channel_multiplier=1).then_inc(pchain, 1)
                pool.wait_ge(pchain, 2)
                nc.gpsimd.tensor_copy(self.ident16[:], self.ident[:]).then_inc(consts, 1)

            @block.vector
            def _(dve):
                t = Tally(chain, 0)
                nc.vector.memset(self.X[:, W - 1, :], 0.0).then_inc(xpad, 1)
                nc.vector.memset(below[:, 0:1], 0.0)
                nc.vector.memset(zero_w[:], 0.0)
                dve.wait_ge(dst_in, 16)
                t.link(dve, nc.vector.tensor_copy(dstf[:], dst_all[:]))
                for w in range(1, W + 1):
                    last = nc.vector.tensor_scalar(junk[:, w % 5, :], dstf[:], float(w * P), 0.0, ALU.is_lt,
                                                   ALU.add, accum_out=below[:, w:w + 1])
                    if w % 5 == 0:
                        t.link(dve, last)
                dve.sem_inc(part_ready, 1)
                dve.wait_ge(sums, 1)
                t.link(dve, nc.vector.tensor_copy(start[:], self.ps[:, 0, 0:W + 1]))
                t.link(dve, nc.vector.tensor_tensor(edges[:], start[:, 1:W + 1], start[:, 0:W], ALU.subtract))
                t.link(dve, nc.vector.tensor_scalar(tiles_i[:], edges[:], float(SE - 1), None, ALU.add))
                t.link(dve, nc.vector.tensor_scalar(tiles_i[:], tiles_i[:], 8, None, ALU.arith_shift_right))
                t.link(dve, nc.vector.tensor_copy(tiles[:], tiles_i[:]))
                t.link(dve, nc.vector.memset(first_step[:, 0:1], 0.0))
                t.link(dve, nc.vector.tensor_tensor_scan(first_step[:, 1:W + 1], zero_w[:], tiles[:], 0.0,
                                                         ALU.add, ALU.add))
                t.link(dve, nc.vector.scalar_tensor_tensor(shift[:], first_step[:, 0:W], -float(SE), start[:, 0:W],
                                                           ALU.mult, ALU.add))
                t.link(dve, nc.vector.tensor_tensor(jump[:, 1:W], shift[:, 1:W], shift[:, 0:W - 1], ALU.subtract))
                dve.wait_ge(consts, 1)
                nc.vector.memset(wsum[:], 0.0)
                t.link(dve, nc.vector.tensor_scalar(osum[:], step_no[:], float(SE), None, ALU.mult))
                for w in range(1, W + 1):
                    if w > 1:
                        last = nc.vector.tensor_tensor(osum[:], osum[:], late[:, (w - 1) % 2, :], ALU.add)
                    if w < W:
                        nc.vector.scalar_tensor_tensor(wsum[:], step_no[:], first_step[:, w:w + 1], wsum[:],
                                                       ALU.is_ge, ALU.add)
                        last = nc.vector.tensor_scalar(late[:, w % 2, :], step_no[:], first_step[:, w:w + 1],
                                                       jump[:, w:w + 1], ALU.is_ge, ALU.mult)
                    t.link(dve, last)
                nc.vector.tensor_copy(self.win[:], wsum[:])
                nc.vector.tensor_copy(self.off[:], osum[:])
                nc.vector.tensor_scalar(self.win_col[:], wsum[:], float(P), None, ALU.mult)

            @block.tensor
            def _(pe):
                pe.wait_ge(consts, 1)
                pe.wait_ge(part_ready, 1)
                nc.tensor.matmul(self.ps[:, 0, 0:W + 1], ones[:], below[:], start=True,
                                 stop=True).then_inc(sums, 1)

    def layer0_edges(self, ACC):
        nc, io, ps = self.nc, self.io, self.ps
        ld = [self.sem(f"a_edges_in{k}") for k in range(UNROLL)]
        xg = [self.sem(f"a_rows_in{k}") for k in range(UNROLL)]
        once = self.sem("a_once")
        hid_ready, silu_ready, rad_ready = self.sem("a_hid"), self.sem("a_silu"), self.sem("a_rad")
        factors, scaled, hot = self.sem("a_factors"), self.sem("a_scaled"), self.sem("a_hot")
        summed, added = self.sem("a_summed"), self.sem("a_added")
        own_ready, row_ready, compared = self.sem("a_own"), self.sem("a_row"), self.sem("a_compared")
        pairs_ready, pairs_done = self.sem("a_pairs_ready"), self.sem("a_pairs_done")
        chain, keys, tick = self.sem("a_chain"), self.sem("a_keys"), self.sem("a_tick")
        with ExitStack() as ctx:
            sb = lambda name, shape, dt=F32: self.sb(ctx, name, shape, dt)
            sd = sb("sd", [P, UNROLL, 2, 2], I32)
            attr = sb("attr", [P, UNROLL, 2, 4])
            emb = sb("emb", [10, UNROLL, SE])
            rows = sb("rows", [P, UNROLL, 2, D])
            fc1, fc2 = sb("fc1", [10, 64]), sb("fc2", [64, 1])
            hid = sb("hid", [64, 2, SE])
            dl = sb("dl", [P, 4, 2])
            ra = sb("ra", [P, 4, 2, 4])
            prod = sb("prod", [P, 4, ACW])
            oh = sb("oh", [P, 4, P])
            key = sb("key", [P, PAIR_TILES])
            spare = sb("spare", [P, PAIR_TILES])
            kt = sb("kt", [P, 2, PAIR_TILES], I32)
            own = sb("own", [P, 2, 2])
            junk = sb("junk_a", [P, 2, 2 * SE])
            before = sb("before", [P, SE])
            cnt = sb("cnt", [P, 2, 2])
            earlier = sb("earlier", [P, 2, 2])
            skip = sb("skip", [P, 2, 2])
            cellf = sb("cellf", [P, 2, 2])
            spot = sb("a_spot", [P, 2, 2])
            dump = sb("dump", [P, 2])
            cell = sb("cell", [P, 2, 2], I32)
            block = ctx.enter_context(nc.Block())

            def acc_ps(p):
                return ps[:, 2 + 2 * p:4 + 2 * p, :].rearrange("p b n -> p (b n)")[:, 0:ACW]

            def key_row(c, q, n=1):
                return ps[:, 6 + c, q * P:(q + n) * P]

            def step(i, b):
                return i * UNROLL + b, b % UNROLL, i + b // UNROLL

            def counted(s):
                return PAIR_LAG <= s < STEPS if isinstance(s, int) else True

            def loop(eng, body):
                for i in range(PAIR_LAG // UNROLL + 1):
                    body(i)
                with eng.Fori(PAIR_LAG // UNROLL + 1, ITERS - 1) as i:
                    body(i)
                body(ITERS - 1)

            @block.sync
            def _(sp):
                sp.dma_start(fc1[:], io["fc_w1"]).then_inc(once, 16)
                sp.dma_start(fc2[:], io["fc_w2"]).then_inc(once, 16)
                sp.dma_start(kt[:, 0, :], io["src_t"]).then_inc(once, 16)
                sp.dma_start(kt[:, 1, :], io["dst_t"]).then_inc(once, 16)

                def body(i):
                    for b in range(UNROLL):
                        s, k, _ = step(i, b)
                        if isinstance(i, int) and i * UNROLL + b in zeroing:
                            piece, zero = zeroing[i * UNROLL + b]
                            sp.dma_start(piece, zero).then_inc(self.zeroed, 16)
                        wait_pos(sp, summed, 2 * (s - UNROLL + 1))
                        o = sp.value_load(self.off[0:1, bass.ds(s, 1)], min_val=0, max_val=EP - SE)
                        sp.dma_start(sd[:, k, :, :], io["sd"][bass.ds(o, SE), :]
                                     .rearrange("(p t) c -> p t c", t=2)).then_inc(ld[k], 16)
                        sp.dma_start(emb[:, k, :], io["emb"][:, bass.ds(o, SE)]).then_inc(ld[k], 16)
                        sp.dma_start(attr[:, k, :, :], io["attr4"][bass.ds(o, SE), :]
                                     .rearrange("(p t) c -> p t c", t=2)).then_inc(ld[k], 16)

                sums = io["sums"].rearrange("(p r) c -> p (r c)", p=P)
                width = TABLES * TROWS * 65 // P
                pieces = [(self.count_rows[w], self.zeros[:]) for w in range(ZEROED_FIRST, W)]
                pieces += [(sums[:, lo:min(lo + NPAD, width)], self.zeros[:, 0:min(NPAD, width - lo)])
                           for lo in range(0, width, NPAD)]
                zeroing = dict(enumerate(pieces, start=2))
                peeled = -(-max(zeroing) // UNROLL) + 1
                for i in range(peeled):
                    body(i)
                with sp.Fori(peeled, ITERS) as i:
                    body(i)

            @block.gpsimd
            def _(pool):
                def gather(i, b):
                    _, k, it = step(i, b)
                    pool.wait_ge(ld[k], 48 * (it + 1))
                    pool.sem_inc(tick, 1)
                    for q in range(2):
                        pool.indirect_dma_start(
                            out=rows[:, k, q, :], out_offset=None, in_=io["x_blocks"],
                            in_offset=bass.IndirectOffsetOnAxis(ap=sd[:, k, q, 0:1], axis=0)).then_inc(xg[k], 16)

                def scatter(i, b):
                    g = i * UNROLL + b - PAIR_LAG
                    if isinstance(g, int) and g == 0:
                        pool.wait_ge(self.zeroed, self.zero_count)
                        pool.sem_inc(tick, 1)
                    pool.wait_ge(pairs_ready, g + 1)
                    pool.sem_inc(tick, 1)
                    if not (isinstance(g, int) and g == 0):
                        pool.wait_ge(pairs_done, g * 32)
                        pool.sem_inc(tick, 1)
                    for q in range(2):
                        pool.indirect_dma_start(
                            out=io["counts"],
                            out_offset=bass.IndirectOffsetOnAxis(ap=cell[:, b % 2, q:q + 1], axis=0),
                            in_=cnt[:, b % 2, q:q + 1], in_offset=None,
                            compute_op=ALU.add).then_inc(pairs_done, 16)

                def body(i):
                    for b in range(UNROLL):
                        s = i * UNROLL + b
                        if not (isinstance(s, int) and s + LEAD >= STEPS):
                            gather(i, b + LEAD)
                        if counted(s):
                            scatter(i, b)

                for b in range(LEAD):
                    gather(0, b)
                loop(pool, body)
                pool.wait_ge(pairs_done, 16 * PAIR_TILES)

            @block.scalar
            def _(act):
                def silu(i, b):
                    s, _, _ = step(i, b)
                    act.wait_ge(hid_ready, s + 1)
                    wait_pos(act, rad_ready, s - 1)
                    nc.scalar.activation(hid[:, b % 2, :], ps[0:64, 0, 0:SE], ACT.Silu,
                                         scale=1.0 / math.sqrt(10.0)).then_inc(silu_ready, 1)

                def body(i):
                    for b in range(UNROLL):
                        s, k, it = step(i, b)
                        if not (isinstance(s, int) and s + 2 >= STEPS):
                            silu(i, b + 2)
                        act.wait_ge(factors, s + 1)
                        act.wait_ge(xg[k], 32 * (it + 1))
                        for q in range(2):
                            r = (2 * b + q) % 4
                            wait_pos(act, summed, 2 * s + q - 3)
                            nc.scalar.activation(prod[:, r, 0:D], rows[:, k, q, :], ACT.Copy,
                                                 scale=ra[:, b % 4, q, 0:1])
                            for m in range(1, 4):
                                both = rows[:, k, q, :].rearrange("p (c i) -> p c i", c=4)[:, 0:m + 1:m, :]
                                last_op = nc.scalar.activation(
                                    prod[:, r, D + (m - 1) * P:D + m * P].rearrange("p (c i) -> p c i", c=2),
                                    both, ACT.Copy, scale=ra[:, b % 4, q, m:m + 1])
                            last_op.then_inc(scaled, 1)

                silu(0, 0)
                silu(0, 1)
                body(0)
                with act.Fori(1, ITERS - 1) as i:
                    body(i)
                body(ITERS - 1)

            @block.tensor
            def _(pe):
                pe.wait_ge(once, 64)

                def hidden(i, b):
                    s, k, it = step(i, b)
                    pe.wait_ge(ld[k], 48 * (it + 1))
                    wait_pos(pe, silu_ready, s)
                    nc.tensor.matmul(ps[0:64, 0, 0:SE], fc1[:], emb[:, k, :], start=True,
                                     stop=True).then_inc(hid_ready, 1)

                def radial(i, b):
                    s, _, _ = step(i, b)
                    pe.wait_ge(silu_ready, s + 1)
                    wait_pos(pe, factors, s)
                    by_tile = hid[:, b % 2, :].rearrange("h (p t) -> h t p", t=2)
                    for q in range(2):
                        c = (b % 2) * 2 + q
                        last = nc.tensor.matmul(ps[:, 1, c:c + 1], by_tile[:, q, :], fc2[:], start=True, stop=True)
                    last.then_inc(rad_ready, 1)

                def spread(i, b):
                    g = i * UNROLL + b - PAIR_LAG
                    pe.wait_ge(own_ready, g + 1)
                    wait_pos(pe, compared, g - 1)
                    for q in range(2):
                        last = nc.tensor.transpose(key_row(b % 2, q), own[:, b % 2, q:q + 1].to_broadcast([P, P]),
                                                   self.ident[:])
                    last.then_inc(row_ready, 1)

                def body(i):
                    for b in range(UNROLL):
                        s = i * UNROLL + b
                        if not (isinstance(s, int) and s + 2 >= STEPS):
                            radial(i, b + 2)
                        if not (isinstance(s, int) and s + 3 >= STEPS):
                            hidden(i, b + 3)
                        wait_pos(pe, added, s - 1)
                        out = acc_ps(b % 2)
                        for q in range(2):
                            r = (2 * b + q) % 4
                            pe.wait_ge(hot, 2 * s + q + 1)
                            pe.wait_ge(scaled, 2 * s + q + 1)
                            nc.tensor.matmul(out[:, 0:512], oh[:, r, :], prod[:, r, 0:512], start=q == 0,
                                             stop=q == 1)
                            nc.tensor.matmul(out[:, 512:ACW], oh[:, r, :], prod[:, r, 512:ACW], start=q == 0,
                                             stop=q == 1).then_inc(summed, 1)
                        if counted(s + 2):
                            spread(i, b + 2)

                for b in range(2):
                    hidden(0, b)
                    radial(0, b)
                hidden(0, 2)
                loop(pe, body)

            @block.vector
            def _(dve):
                nc.vector.memset(ACC[:], 0.0)
                nc.vector.memset(before[:, 0:P], 1.0)
                nc.vector.tensor_copy(before[:, P:SE], self.lower[:]).then_inc(keys, 1)
                dve.wait_ge(once, 64)
                nc.vector.scalar_tensor_tensor(key[:], kt[:, 1, :], float(NPAD), kt[:, 0, :], ALU.mult,
                                               ALU.add).then_inc(keys, 1)
                dve.wait_ge(keys, 2)
                nc.vector.tensor_scalar(spare[:], key[:], float(CELLS), None, ALU.is_ge).then_inc(keys, 1)
                for q in range(2):
                    last = nc.vector.tensor_scalar(dump[:, q:q + 1], self.part[:], float(CELLS + q * P), None, ALU.add)
                last.then_inc(keys, 1)
                dve.wait_ge(keys, 4)

                def take(i, b):
                    g = i * UNROLL + b - PAIR_LAG
                    nc.vector.tensor_copy(own[:, b % 2, :], key[:, bass.ds(g * 2, 2)]).then_inc(own_ready, 1)

                def compare(i, b):
                    g, c = i * UNROLL + b - PAIR_LAG, b % 2
                    dve.wait_ge(row_ready, g + 1)
                    if not (isinstance(g, int) and g < 2):
                        dve.wait_ge(pairs_done, 32 * (g - 1))
                    for q in range(2):
                        mine = own[:, c, q:q + 1]
                        nc.vector.tensor_scalar(junk[:, q, 0:SE], key_row(c, 0, 2), mine, 0.0, ALU.is_equal, ALU.add,
                                                accum_out=cnt[:, c, q:q + 1])
                        mask = before[:, 0:SE] if q else self.lower[:]
                        last = nc.vector.scalar_tensor_tensor(junk[:, q, SE:SE + (q + 1) * P], key_row(c, 0, q + 1),
                                                              mine, mask, ALU.is_equal, ALU.mult,
                                                              accum_out=earlier[:, c, q:q + 1])
                    last.then_inc(compared, 1)

                def skips(i, b):
                    g, c = i * UNROLL + b - PAIR_LAG, b % 2
                    dve.wait_ge(compared, g + 1)
                    nc.vector.scalar_tensor_tensor(skip[:, c, :], earlier[:, c, :], 0.5,
                                                   spare[:, bass.ds(g * 2, 2)], ALU.is_gt, ALU.max).then_inc(chain, 1)

                def cells(i, b):
                    g, c = i * UNROLL + b - PAIR_LAG, b % 2
                    dve.wait_ge(chain, 2 * g + 1)
                    nc.vector.scalar_tensor_tensor(cellf[:, c, :], skip[:, c, :], 0.0, own[:, c, :], ALU.is_equal,
                                                   ALU.mult)
                    nc.vector.tensor_tensor(spot[:, c, :], skip[:, c, :], dump[:], ALU.mult).then_inc(chain, 1)
                    dve.wait_ge(chain, 2 * g + 2)
                    nc.vector.tensor_tensor(cell[:, c, :], spot[:, c, :], cellf[:, c, :],
                                            ALU.add).then_inc(pairs_ready, 1)

                def factor(i, b):
                    s, k, it = step(i, b)
                    c, f = b % 2, b % 4
                    dve.wait_ge(ld[k], 48 * (it + 1))
                    nc.vector.tensor_tensor(dl[:, f, :], sd[:, k, :, 1],
                                            self.win_col[:, bass.ds(s, 1)].to_broadcast([P, 2]), ALU.subtract)
                    dve.wait_ge(rad_ready, s + 1)
                    nc.vector.tensor_tensor(ra[:, f, :, :], attr[:, k, :, :],
                                            ps[:, 1, c * 2:c * 2 + 2].unsqueeze(2).to_broadcast([P, 2, 4]),
                                            ALU.mult).then_inc(factors, 1)

                def add(s, p):
                    w = dve.value_load(self.win[0:1, bass.ds(s, 1)], min_val=0, max_val=W - 1)
                    dve.wait_ge(summed, 2 * s + 2)
                    wait_pos(dve, added, s)
                    a = ACC[:, bass.ds(w * ACW, ACW)]
                    nc.vector.tensor_tensor(a, a, acc_ps(p), ALU.add).then_inc(added, 1)

                def body(i):
                    for b in range(UNROLL):
                        s = i * UNROLL + b
                        dve.wait_ge(factors, s + 1)
                        for q in range(2):
                            nc.vector.tensor_scalar(oh[:, (2 * b + q) % 4, :], self.iota[:], dl[:, b % 4, q:q + 1],
                                                    None, ALU.is_equal).then_inc(hot, 1)
                        if counted(s + 2):
                            take(i, b + 2)
                        if counted(s + 1):
                            compare(i, b + 1)
                        if not (isinstance(s, int) and s + 2 >= STEPS):
                            factor(i, b + 2)
                        if counted(s + 1):
                            skips(i, b + 1)
                        if not (isinstance(s, int) and s == 0):
                            add(s - 1, (b - 1) % 2)
                        if counted(s + 1):
                            cells(i, b + 1)

                factor(0, 0)
                factor(0, 1)
                loop(dve, body)
                add(STEPS - 1, (STEPS - 1) % 2)

    def norm_end(self, ctx, tag, Y):
        nc = self.nc
        st = self.sb(ctx, tag + "_st", [P, W, 6])
        mv = self.sb(ctx, tag + "_mv", [P, W, 2])
        std = self.sb(ctx, tag + "_std", [P, W])
        epsc = self.sb(ctx, tag + "_eps", [P, 1])
        var_ready, std_ready = self.sem(tag + "_var"), self.sem(tag + "_stdr")
        rec_ready, written = self.sem(tag + "_rec"), self.sem(tag + "_norm")
        stats_ready = self.sem(tag + "_stats")

        def scalar_part(act):
            act.wait_ge(var_ready, 1)
            nc.scalar.activation(std[:], mv[:, :, 1], ACT.Sqrt, bias=epsc[:]).then_inc(std_ready, 1)

        def vector_begin(dve):
            nc.vector.memset(epsc[:], 1.0e-5).then_inc(rec_ready, 1)
            dve.wait_ge(rec_ready, 1)

        def vector_part(dve, summed, count):
            dve.wait_ge(summed, count)
            dve.sem_inc(stats_ready, 1)
            for_fives(dve, lambda w: nc.vector.bn_stats(window(st, w), window(Y, w)).then_inc(stats_ready, 1))
            dve.wait_ge(stats_ready, W + 1)
            for w in range(W):
                last = nc.vector.bn_aggr(mv[:, w, :], st[:, w, :])
            last.then_inc(var_ready, 1)
            dve.wait_ge(std_ready, 1)
            nc.vector.reciprocal(std[:], std[:]).then_inc(rec_ready, 1)
            dve.wait_ge(rec_ready, 2)

            for_fives(dve, lambda w: nc.vector.tensor_scalar(
                window(self.X, w), window(Y, w), mv[:, bass.ds(w, 1), 0:1].rearrange("p w d -> p (w d)"),
                std[:, bass.ds(w, 1)], ALU.subtract, ALU.mult).then_inc(written, 1))

        return scalar_part, vector_begin, vector_part, written

    def layer0_nodes(self, ACC):
        nc, io, ps = self.nc, self.io, self.ps
        loaded, scaled = self.sem("b_loaded"), self.sem("b_scaled")
        turned, moved, mixed, resid = self.sem("b_turned"), self.sem("b_moved"), self.sem("b_mixed"), self.sem("b_resid")
        staged, vsums = self.sem("b_staged"), self.sem("b_vsums")
        scale = 1.679177 / (math.sqrt(2.0 * MUL) * math.sqrt(64.0) * math.sqrt(16.0))
        with ExitStack() as ctx:
            wgt = self.sb(ctx, "wgt", [P, 2, MUL])
            stage = self.sb(ctx, "stage", [P, 2, 512])
            vsum = self.sb(ctx, "vsum", [P, 2, MUL])
            turn = self.sb(ctx, "turn", [P, 2, 512])
            Y = self.sb(ctx, "Yb", [P, W, D])
            scalar_part, vector_begin, vector_part, _ = self.norm_end(ctx, "bn", Y)
            block = ctx.enter_context(nc.Block())

            @block.sync
            def _(sp):
                sp.dma_start(wgt[0:MUL, 0, :], io["w_00_0"]).then_inc(loaded, 16)
                sp.dma_start(wgt[MUL:P, 0, :], io["w_11_0"]).then_inc(loaded, 16)
                sp.dma_start(wgt[0:MUL, 1, :], io["w_01_1"]).then_inc(loaded, 16)
                sp.dma_start(wgt[MUL:P, 1, :], io["w_10_1"]).then_inc(loaded, 16)

            @block.gpsimd
            def _(pool):
                def arrange(w, k):
                    a = ACC[:, bass.ds(w * ACW, ACW)].rearrange("p (c i) -> p c i", i=MUL)
                    s_ = stage[:, k, :].rearrange("p (c h i) -> p c h i", c=4, h=2)
                    wait_pos(pool, turned, w - 1)
                    nc.gpsimd.tensor_copy(s_[:, 0, 0, :], a[:, 0, :])
                    nc.gpsimd.tensor_copy(s_[:, 1:4, 1, :], a[:, 1:4, :])
                    nc.gpsimd.tensor_copy(s_[:, 1:4, 0, :], a[:, 4:10:2, :])
                    nc.gpsimd.tensor_tensor(vsum[:, k, :], a[:, 5, :], a[:, 7, :], ALU.add).then_inc(vsums, 1)
                    pool.wait_ge(vsums, w + 1)
                    nc.gpsimd.tensor_tensor(s_[:, 0, 1, :], vsum[:, k, :], a[:, 9, :], ALU.add).then_inc(staged, 1)

                for_pairs(pool, arrange)
                arrange(W - 1, 0)

            @block.tensor
            def _(pe):
                pe.wait_ge(scaled, 1)

                def turn_window(w, k):
                    pe.wait_ge(staged, w + 1)
                    wait_pos(pe, moved, w - 1)
                    for c in range(4):
                        last = nc.tensor.transpose(ps[:, k, c * P:(c + 1) * P], stage[:, k, c * P:(c + 1) * P],
                                                   self.ident[:])
                    last.then_inc(turned, 1)

                def mix_window(w, k):
                    pe.wait_ge(moved, w + 1)
                    wait_pos(pe, resid, w - 1)
                    for c in range(4):
                        last = nc.tensor.matmul(ps[:, 2 + k, c * MUL:(c + 1) * MUL], turn[:, k, c * P:(c + 1) * P],
                                                wgt[:, min(c, 1), :], start=True, stop=True)
                    last.then_inc(mixed, 1)

                turn_window(0, 0)
                for_pairs(pe, lambda w, k: (turn_window(w + 1, 1 - k), mix_window(w, k)))
                mix_window(W - 1, 0)

            @block.scalar
            def _(act):
                act.wait_ge(loaded, 64)
                nc.scalar.mul(wgt[MUL:P, 0, :], wgt[MUL:P, 0, :], 1.0 / math.sqrt(3.0)).then_inc(scaled, 1)

                def move(w, k):
                    act.wait_ge(turned, w + 1)
                    wait_pos(act, mixed, w - 1)
                    nc.scalar.copy(turn[:, k, :], ps[:, k, :]).then_inc(moved, 1)

                for_pairs(act, move)
                move(W - 1, 0)
                scalar_part(act)

            @block.vector
            def _(dve):
                vector_begin(dve)

                def residual(w, k):
                    dve.wait_ge(mixed, w + 1)
                    y, x = window(Y, w), window(self.X, w)
                    nc.vector.scalar_tensor_tensor(y[:, 0:MUL], ps[:, 2 + k, 0:MUL], scale, x[:, 0:MUL], ALU.mult,
                                                   ALU.add)
                    ins = nc.vector.scalar_tensor_tensor(
                        y[:, MUL:D].rearrange("p (o m) -> p m o", m=3),
                        ps[:, 2 + k, MUL:D].rearrange("p (m o) -> p m o", m=3), scale,
                        x[:, MUL:D].rearrange("p (o m) -> p m o", m=3), ALU.mult, ALU.add)
                    ins.then_inc(resid, 1)

                for_pairs(dve, residual)
                residual(W - 1, 0)
                vector_part(dve, resid, W)

    def attention(self, layer, T, HS, betas, places, ss):
        nc, ps, H = self.nc, self.ps, self.X
        srcf, spare, home, away = places
        n = f"l{layer}_"
        squared, eps_added, rooted, inverted = (self.sem(n + x) for x in ("sq", "eps", "root", "inv"))
        scaled, turned, t_high, t_low = (self.sem(n + x) for x in ("scaled", "turned", "thigh", "tlow"))
        h_high, h_low = self.sem(n + "hhigh"), self.sem(n + "hlow")
        with ExitStack() as ctx:
            junk = self.sb(ctx, n + "junk", [P, 2, D])
            norm = self.sb(ctx, n + "norm", [P, W])
            hn = self.sb(ctx, n + "hn", [P, 2, D])
            block = ctx.enter_context(nc.Block())

            @block.scalar
            def _(act):
                def square(w, k):
                    wait_pos(act, squared, w - 1)
                    nc.scalar.activation(junk[:, k, :], window(H, w), ACT.Square,
                                         accum_out=ss[:, bass.ds(w, 1)]).then_inc(squared, 1)
                if layer == 0:
                    for_pairs(act, square)
                    square(W - 1, 0)
                act.wait_ge(eps_added, 1)
                nc.scalar.activation(norm[:], norm[:], ACT.Sqrt).then_inc(rooted, 1)

                def parts(w, k):
                    nc.scalar.copy(window(HS[0], w), window(H, w)).then_inc(h_high, 1)
                    act.wait_ge(turned, w + 1)
                    nc.scalar.activation(T[0][:, :, bass.ds(w * P, P)],
                                         ps[:, k, 0:D].rearrange("p (t n) -> p t n", t=2), ACT.Copy,
                                         scale=SN).then_inc(t_high, 1)
                for_pairs(act, parts)
                parts(W - 1, 0)

            @block.gpsimd
            def _(pool):
                def low(w, k):
                    pool.wait_ge(h_high, w + 1)
                    nc.gpsimd.tensor_tensor(window(HS[1], w), window(H, w), window(HS[0], w),
                                            ALU.subtract).then_inc(h_low, 1)
                for_pairs(pool, low)
                low(W - 1, 0)

            @block.vector
            def _(dve):
                if layer == 0:
                    dve.wait_ge(squared, W)
                nc.vector.tensor_scalar(norm[:], ss[:], 1.0e-16, None, ALU.add).then_inc(eps_added, 1)
                dve.wait_ge(rooted, 1)
                nc.vector.reciprocal(norm[:], norm[:]).then_inc(inverted, 1)
                dve.wait_ge(inverted, 1)

                def scale(w, k):
                    wait_pos(dve, turned, w - 1)
                    nc.vector.tensor_scalar(hn[:, k, :], window(H, w), norm[:, bass.ds(w, 1)], None,
                                            ALU.mult).then_inc(scaled, 1)

                def low(w, k):
                    dve.wait_ge(t_high, w + 1)
                    part = bass.ds(w * P, P)
                    nc.vector.scalar_tensor_tensor(T[1][:, :, part],
                                                   ps[:, k, 0:D].rearrange("p (t n) -> p t n", t=2), SN,
                                                   T[0][:, :, part], ALU.mult, ALU.subtract).then_inc(t_low, 1)
                scale(0, 0)
                for_pairs(dve, lambda w, k: (scale(w + 1, 1 - k), low(w, k)))
                low(W - 1, 0)

            @block.tensor
            def _(pe):
                def turn(w, k):
                    pe.wait_ge(scaled, w + 1)
                    wait_pos(pe, t_low, w - 1)
                    for t in range(2):
                        last = nc.tensor.transpose(ps[:, k, t * P:(t + 1) * P], hn[:, k, t * P:(t + 1) * P],
                                                   self.ident[:])
                    last.then_inc(turned, 1)
                for_pairs(pe, turn)
                turn(W - 1, 0)

        count_in, logged, masked = (self.sem(n + x) for x in ("count_in", "logged", "masked"))
        scored, logits = self.sem(n + "scored"), self.sem(n + "logits")
        attr_in, matched, placing, placed = (self.sem(n + x) for x in ("attr_in", "matched", "placing", "placed"))
        resquared, warmed = self.sem(n + "resquared"), self.sem(n + "warmed")
        spotted, stored, sp_tick = (self.sem(n + x) for x in ("spotted", "stored", "sp_tick"))
        totalled, landed, consts, tick = (self.sem(n + x) for x in ("totalled", "landed", "consts", "tick"))
        max_ready, exp_ready, e_high, e_low = (self.sem(n + x) for x in ("max", "exp", "ehigh", "elow"))
        e_turned, moved_a, moved_v = (self.sem(n + x) for x in ("eturned", "moved_a", "moved_v"))
        mixed, done, chain = (self.sem(n + x) for x in ("mixed", "done", "chain"))
        BY_ACT = [True, True, True, False, True, False, True]
        A_MOVES, V_MOVES = sum(BY_ACT), len(BY_ACT) - sum(BY_ACT)
        G = len(GROUPS)
        with ExitStack() as ctx:
            L = self.sb(ctx, n + "L", [P, 2, NPAD])
            floor, warm = self.sb(ctx, n + "floor", [P, 1]), self.sb(ctx, n + "warm", [P, 1])
            square_out = self.sb(ctx, n + "square_out", [P, 2, D])
            attr = self.sb(ctx, n + "attr", [P, 2, TABLES, MUL + 1])
            ids = self.sb(ctx, n + "ids", [P, 2, TABLES * P], I32)
            same = self.sb(ctx, n + "same", [P, 2, TABLES, P])
            first = self.sb(ctx, n + "first", [P, TABLES, P])
            total = self.sb(ctx, n + "total", [P, 2, TABLES, MUL + 1])
            earlier, skip, spot = (self.sb(ctx, n + x, [P, 2, TABLES]) for x in ("earlier", "skip", "spot"))
            place = self.sb(ctx, n + "place", [P, 2, TABLES], I32)
            Ex = self.sb(ctx, n + "E", [P, NPAD])
            parts = [self.sb(ctx, n + f"e{x}", [P, 2, NPAD], F16) for x in ("hi", "lo")]
            PT = self.sb(ctx, n + "PT", [P, W, 2, P], F16)
            mx, neg, den, rden = (self.sb(ctx, n + x, [P, 2]) for x in ("mx", "neg", "den", "rden"))
            table = self.io["counts"][0:CELLS, :].rearrange("(w p f) o -> w p (f o)", p=P, f=NPAD)
            block = ctx.enter_context(nc.Block())

            def bank16(g):
                return ps[:, 4 + g % 2, :].bitcast(F16)

            def totals_ps():
                assert GROUPS[-1][1] * P + TABLES * (MUL + 1) <= 512
                return ps[:, 4 + (G - 1) % 2, P:P + TABLES * (MUL + 1)].rearrange("p (q c) -> p q c", q=TABLES)

            def four(w):
                return (layer * W + w) * TABLES

            @block.sync
            def _(sp):
                def load_counts(w, k):
                    wait_pos(sp, exp_ready, w - 1)
                    sp.sem_inc(sp_tick, 1)
                    wait_pos(sp, count_in, 16 * w)
                    sp.sem_inc(sp_tick, 1)
                    sp.dma_start(L[:, k, :], table[bass.ds(w, 1), :, :]
                                 .rearrange("w p f -> p (w f)")).then_inc(count_in, 16)

                def load_edges(w, k):
                    wait_pos(sp, e_turned, G * (w - 1))
                    sp.sem_inc(sp_tick, 1)
                    wait_pos(sp, placing, 3 * (w - 1))
                    sp.sem_inc(sp_tick, 1)
                    wait_pos(sp, attr_in, 32 * w)
                    sp.sem_inc(sp_tick, 1)
                    e = four(w) * P
                    sp.dma_start(attr[:, k, :, 0:MUL], self.io["attr64"][bass.ds(e, TABLES * P), :]
                                 .rearrange("(q p) c -> p q c", p=P)).then_inc(attr_in, 16)
                    sp.dma_start(ids[:, k, :], self.io["ids"][0:1, bass.ds(e, TABLES * P)]
                                 .to_broadcast([P, TABLES * P])).then_inc(attr_in, 16)
                def window_part(w, k):
                    load_counts(w + 2, k)
                    load_edges(w + 1, 1 - k)

                load_counts(0, 0)
                load_counts(1, 1)
                load_edges(0, 0)
                for_pairs(sp, window_part, W - 3)
                window_part(W - 3, 0)
                load_edges(W - 1, 0)

            @block.tensor
            def _(pe):
                def scores(w):
                    for c in range(NSC):
                        wait_pos(pe, logits, NSC * w + c - 3)
                        cols = slice(c * SC, (c + 1) * SC)
                        q = bass.ds(w * P, P)
                        for t in range(2):
                            for a, b in ((0, 0), (0, 1), (1, 0)):
                                last = nc.tensor.matmul(ps[:, c % 4, 0:SC], T[a][:, t, q], T[b][:, t, cols],
                                                        start=(t, a, b) == (0, 0, 0), stop=(t, a) == (1, 1))
                        last.then_inc(scored, 1)

                def merge(w, k):
                    pe.wait_ge(matched, w + 1)
                    pe.wait_ge(attr_in, 32 * (w + 1))
                    for q in range(TABLES):
                        last = nc.tensor.matmul(totals_ps()[:, q, :], same[:, k, q, :], attr[:, k, q, :], start=True,
                                                stop=True)
                    return last

                def turn(w, k, g):
                    t0, m = GROUPS[g]
                    for t in range(m):
                        for h in range(2):
                            last = nc.tensor.transpose(bank16(g)[:, (2 * t + h) * P:(2 * t + h + 1) * P],
                                                       parts[h][:, k, (t0 + t) * P:(t0 + t + 1) * P],
                                                       self.ident16[:])
                    if g + 1 == G:
                        last = merge(w, k)
                    last.then_inc(e_turned, 1)

                def mix(w, k):
                    pe.wait_ge(e_high, w + 1)
                    pe.wait_ge(e_low, w + 1)
                    wait_pos(pe, done, w - 1)
                    turn(w, k, 0)
                    for g, (t0, m) in enumerate(GROUPS):
                        if g + 1 < G:
                            turn(w, k, g + 1)
                        if BY_ACT[g]:
                            pe.wait_ge(moved_a, A_MOVES * w + sum(BY_ACT[:g + 1]))
                        else:
                            pe.wait_ge(moved_v, V_MOVES * w + g + 1 - sum(BY_ACT[:g + 1]))
                        for t in range(t0, t0 + m):
                            for a, b in ((0, 0), (0, 1), (1, 0)):
                                last = nc.tensor.matmul(ps[:, 6 + k, 0:D], PT[:, t, a, :], HS[b][:, t, :],
                                                        start=(t, a, b) == (0, 0, 0), stop=(t, a) == (W - 1, 1))
                    last.then_inc(mixed, 1)

                pe.wait_ge(consts, 2)
                scores(0)
                for_pairs(pe, lambda w, k: (scores(w + 1), mix(w, k)))
                mix(W - 1, 0)

            def move(w, k, g):
                t0, m = GROUPS[g]
                return PT[:, t0:t0 + m, :, :].rearrange("p t h n -> p (t h n)"), bank16(g)[:, 0:m * 2 * P]

            @block.scalar
            def _(act):
                def moves(w, k, groups):
                    for g in groups:
                        act.wait_ge(e_turned, G * w + g + 1)
                        out_, in_ = move(w, k, g)
                        nc.scalar.copy(out_, in_).then_inc(moved_a, 1)

                def exps(w, k):
                    act.wait_ge(max_ready, w + 1)
                    wait_pos(act, e_low, w)
                    nc.scalar.activation(Ex[:], L[:, k, :], ACT.Exp, bias=neg[:, k:k + 1],
                                         accum_out=den[:, k:k + 1]).then_inc(exp_ready, 1)

                def high(w, k):
                    act.wait_ge(exp_ready, w + 1)
                    wait_pos(act, e_turned, G * (w - 1))
                    nc.scalar.copy(parts[0][:, k, :], Ex[:]).then_inc(e_high, 1)

                def logs(w, k):
                    act.wait_ge(count_in, 16 * (w + 1))
                    nc.scalar.activation(L[:, k, :], L[:, k, :], ACT.Ln, bias=floor[:], scale=4.0).then_inc(logged, 1)

                def totals(w, k):
                    act.wait_ge(e_turned, G * (w + 1))
                    wait_pos(act, landed, 16 * TABLES * (w - 1))
                    nc.scalar.copy(total[:, k, :, :], totals_ps()).then_inc(totalled, 1)

                def square(w, k):
                    act.wait_ge(done, w + 1)
                    wait_pos(act, resquared, w - 1)
                    nc.scalar.activation(square_out[:, k, :], window(H, w), ACT.Square,
                                         accum_out=ss[:, bass.ds(w, 1)]).then_inc(resquared, 1)

                def window_part(w, k, ahead=True):
                    if ahead and layer == 0:
                        logs(w + 2, k)
                        wait_pos(act, warmed, w)
                        nc.scalar.activation(warm[:], floor[:], ACT.Exp).then_inc(warmed, 1)
                    if not (isinstance(w, int) and w == 0):
                        square(w - 1, 1 - k)
                    moves(w, k, [0, 1, 2])
                    exps(w + 1, 1 - k)
                    moves(w, k, [4])
                    high(w + 1, 1 - k)
                    totals(w, k)
                    moves(w, k, [6])

                act.wait_ge(consts, 1)
                if layer == 0:
                    logs(0, 0)
                    logs(1, 1)
                exps(0, 0)
                high(0, 0)
                for_pairs(act, window_part, W - 3)
                window_part(W - 3, 0)
                window_part(W - 2, 1, ahead=False)
                moves(W - 1, 0, [0, 1, 2, 4])
                totals(W - 1, 0)
                moves(W - 1, 0, [6])
                square(W - 2, 1)
                square(W - 1, 0)

            @block.gpsimd
            def _(pool):
                nc.gpsimd.memset(floor[:], FLOOR).then_inc(consts, 1)
                nc.gpsimd.memset(attr[:, :, :, MUL:MUL + 1], 1.0).then_inc(consts, 1)

                def scatter(w, k):
                    pool.wait_ge(totalled, w + 1)
                    pool.sem_inc(tick, 1)
                    pool.wait_ge(placed, w + 1)
                    pool.sem_inc(tick, 1)
                    if not (isinstance(w, int) and w == 0):
                        pool.wait_ge(landed, 16 * TABLES * w)
                        pool.sem_inc(tick, 1)
                    for q in range(TABLES):
                        pool.indirect_dma_start(
                            out=self.io["sums"], out_offset=bass.IndirectOffsetOnAxis(ap=place[:, k, q:q + 1], axis=0),
                            in_=total[:, k, q, :], in_offset=None, compute_op=ALU.add).then_inc(landed, 16)

                def store_logs(w, k):
                    if layer == 0:
                        pool.wait_ge(masked, w + 1)
                        pool.sem_inc(tick, 1)
                        if not (isinstance(w, int) and w == 0):
                            pool.wait_ge(stored, 16 * w)
                            pool.sem_inc(tick, 1)
                        pool.dma_start(table[bass.ds(w, 1), :, :].rearrange("w p f -> p (w f)"),
                                       L[:, k, :]).then_inc(stored, 16)

                store_logs(0, 0)
                store_logs(1, 1)
                for_pairs(pool, lambda w, k: (store_logs(w + 2, k), scatter(w, k)), W - 3)
                store_logs(W - 1, 0)
                scatter(W - 3, 0)
                scatter(W - 2, 1)
                scatter(W - 1, 0)
                if layer == 0:
                    pool.wait_ge(stored, 16 * W)
                pool.wait_ge(landed, 16 * TABLES * W)

            @block.vector
            def _(dve):
                def mask(w, k):
                    if layer == 0:
                        dve.wait_ge(logged, w + 1)
                        nc.vector.scalar_tensor_tensor(L[:, k, :], L[:, k, :], -NO_EDGE, L[:, k, :], ALU.mult,
                                                       ALU.min).then_inc(masked, 1)

                def logit(w, k, ahead=False):
                    if layer == 0:
                        dve.wait_ge(masked, w + 1)
                        dve.wait_ge(stored, 16 * (w + 1))
                    else:
                        dve.wait_ge(count_in, 16 * (w + 1))
                    for c in range(NSC):
                        if ahead and c == NSC // 2:
                            mask(w + 1, 1 - k)
                        cols = slice(c * SC, (c + 1) * SC)
                        dve.wait_ge(scored, NSC * w + c + 1)
                        nc.vector.scalar_tensor_tensor(L[:, k, cols], ps[:, c % 4, 0:SC], betas[:, layer:layer + 1],
                                                       L[:, k, cols], ALU.mult, ALU.add).then_inc(logits, 1)
                    dve.wait_ge(logits, NSC * (w + 1))
                    t = Tally(chain, w * 3 - 2 if not isinstance(w, int) or w else 0)
                    t.link(dve, nc.vector.tensor_reduce(mx[:, k:k + 1], L[:, k, :], AX.X, ALU.max))
                    nc.vector.tensor_scalar(neg[:, k:k + 1], mx[:, k:k + 1], -1.0, None,
                                            ALU.mult).then_inc(max_ready, 1)

                def moved(w, k, g):
                    dve.wait_ge(e_turned, G * w + g + 1)
                    out_, in_ = move(w, k, g)
                    nc.vector.tensor_copy(out_, in_).then_inc(moved_v, 1)

                def match(w, k):
                    dve.wait_ge(attr_in, 32 * (w + 1))
                    wait_pos(dve, e_turned, G * (w - 1))
                    nc.vector.tensor_tensor(same[:, k, :, :], ids[:, k, :].rearrange("p (q e) -> p q e", q=TABLES),
                                            srcf[:, bass.ds(four(w), TABLES)].unsqueeze(2)
                                            .to_broadcast([P, TABLES, P]), ALU.is_equal).then_inc(matched, 1)

                def before(w, k):
                    dve.wait_ge(matched, w + 1)
                    nc.vector.tensor_tensor(first[:], same[:, k, :, :],
                                            self.lower[:].unsqueeze(1).to_broadcast([P, TABLES, P]),
                                            ALU.mult).then_inc(placing, 1)
                    dve.wait_ge(placing, 3 * w + 1)
                    nc.vector.tensor_reduce(earlier[:, k, :], first[:], AX.X, ALU.add).then_inc(placing, 1)

                def skips(w, k):
                    dve.wait_ge(placing, 3 * w + 2)
                    nc.vector.scalar_tensor_tensor(skip[:, k, :], earlier[:, k, :], 0.5,
                                                   spare[:, bass.ds(four(w), TABLES)], ALU.is_gt,
                                                   ALU.max).then_inc(placing, 1)

                def spots(w, k):
                    dve.wait_ge(placing, 3 * w + 3)
                    nc.vector.tensor_tensor(spot[:, k, :], skip[:, k, :], away[:, bass.ds(four(w), TABLES)],
                                            ALU.mult).then_inc(spotted, 1)

                def places_of(w, k):
                    dve.wait_ge(spotted, w + 1)
                    wait_pos(dve, landed, 16 * TABLES * (w - 1))
                    nc.vector.tensor_tensor(place[:, k, :], spot[:, k, :], home[:, bass.ds(four(w), TABLES)],
                                            ALU.add).then_inc(placed, 1)

                def low(w, k):
                    dve.wait_ge(e_high, w + 1)
                    wait_pos(dve, e_turned, G * (w - 1))
                    nc.vector.tensor_tensor(parts[1][:, k, :], Ex[:], parts[0][:, k, :],
                                            ALU.subtract).then_inc(e_low, 1)

                def finish(w, k):
                    t = Tally(chain, w * 3 + (1 if isinstance(w, int) and w == W - 1 else 2))
                    t.link(dve, nc.vector.reciprocal(rden[:, k:k + 1], den[:, k:k + 1]))
                    t.link(dve, nc.vector.scalar_tensor_tensor(rden[:, k:k + 1], mx[:, k:k + 1], 0.1 * NO_EDGE,
                                                               rden[:, k:k + 1], ALU.is_gt, ALU.mult))
                    dve.wait_ge(mixed, w + 1)
                    nc.vector.tensor_scalar(window(H, w), ps[:, 6 + k, 0:D], rden[:, k:k + 1], 0.0, ALU.mult,
                                            ALU.max).then_inc(done, 1)

                def window_part(w, k, ahead=True):
                    v, kv = w + 1, 1 - k
                    logit(v, kv, ahead)
                    moved(w, k, 3)
                    match(v, kv)
                    before(v, kv)
                    moved(w, k, 5)
                    skips(v, kv)
                    low(v, kv)
                    spots(v, kv)
                    finish(w, k)
                    places_of(v, kv)

                mask(0, 0)
                mask(1, 1)
                logit(0, 0)
                match(0, 0)
                before(0, 0)
                skips(0, 0)
                low(0, 0)
                spots(0, 0)
                places_of(0, 0)
                if layer == 0:
                    dve.wait_ge(self.kept, 16)
                for_pairs(dve, window_part, W - 3)
                window_part(W - 3, 0)
                window_part(W - 2, 1, ahead=False)
                moved(W - 1, 0, 3)
                moved(W - 1, 0, 5)
                finish(W - 1, 0)

    def prepare_attention(self, betas, places):
        nc, io = self.nc, self.io
        srcf, spare, home, away = places
        loaded, scaled, consts, homes = (self.sem("p_" + x) for x in ("in", "scaled", "consts", "homes"))
        with ExitStack() as ctx:
            base = self.sb(ctx, "p_base", [P, TABLES])
            dump = self.sb(ctx, "p_dump", [P, TABLES])
            src_i = self.sb(ctx, "p_src", [P, PAIR_TILES], I32)
            block = ctx.enter_context(nc.Block())

            def by_table(t):
                return t[:].rearrange("p (g q) -> p g q", q=TABLES)

            @block.sync
            def _(sp):
                sp.dma_start(betas[:], io["betas"].to_broadcast([P, 4])).then_inc(loaded, 16)
                sp.dma_start(src_i[:], io["src_t"]).then_inc(loaded, 16)
                sp.dma_start(io["x_kept"].rearrange("(w p) d -> p w d", p=P), self.X[:]).then_inc(self.kept, 16)

            @block.gpsimd
            def _(pool):
                nc.gpsimd.iota(base[:], [[TROWS, TABLES]], base=0, channel_multiplier=0,
                               allow_small_or_imprecise_dtypes=True)
                nc.gpsimd.iota(dump[:], [[TROWS, TABLES]], base=NPAD, channel_multiplier=1,
                               allow_small_or_imprecise_dtypes=True).then_inc(consts, 1)

            @block.vector
            def _(dve):
                dve.wait_ge(loaded, 32)
                dve.wait_ge(consts, 1)
                nc.vector.tensor_scalar(betas[:], betas[:], 1.0 / (SN * SN), None, ALU.mult)
                nc.vector.tensor_copy(srcf[:], src_i[:]).then_inc(scaled, 1)
                dve.wait_ge(scaled, 1)
                nc.vector.tensor_scalar(spare[:], srcf[:], float(N), None, ALU.is_ge)
                every = lambda t: t[:].unsqueeze(1).to_broadcast([P, PAIR_TILES // TABLES, TABLES])
                nc.vector.tensor_tensor(by_table(home), by_table(srcf), every(base), ALU.add).then_inc(homes, 1)
                dve.wait_ge(homes, 1)
                nc.vector.tensor_tensor(by_table(away), every(dump), by_table(home), ALU.subtract)
    def add_norm(self):
        nc = self.nc
        summed = self.sem("e_summed")
        loaded = [self.sem(f"e_loaded{k}") for k in range(W // 5)]
        with ExitStack() as ctx:
            Y = self.sb(ctx, "e_Y", [P, W, D])
            scalar_part, vector_begin, vector_part, _ = self.norm_end(ctx, "e", Y)
            block = ctx.enter_context(nc.Block())

            @block.sync
            def _(sp):
                for k in range(W // 5):
                    sp.dma_start(Y[:, 5 * k:5 * k + 5, :], self.io["x_kept"][5 * k * P:(5 * k + 5) * P, :]
                                 .rearrange("(w p) d -> p w d", p=P)).then_inc(loaded[k], 16)

            @block.scalar
            def _(act):
                scalar_part(act)

            @block.vector
            def _(dve):
                vector_begin(dve)
                for k in range(W // 5):
                    dve.wait_ge(loaded[k], 16)
                    five = slice(5 * k, 5 * k + 5)
                    nc.vector.tensor_tensor(Y[:, five, :], self.X[:, five, :], Y[:, five, :],
                                            ALU.add).then_inc(summed, 1)
                vector_part(dve, summed, W // 5)

    def layer2_nodes(self):
        nc, io, ps = self.nc, self.io, self.ps
        C = MUL + 1
        KH = HID // P
        loaded, u_ready, bias_sum, bias_ready = (self.sem("g_" + x) for x in ("loaded", "u", "bsum", "bias"))
        tab_in, mean_ready, turned, moved = (self.sem("g_" + x) for x in ("tab", "mean", "turned", "moved"))
        hid_ready, hid_moved, o_ready, resid, chain, consts, staged = (self.sem("g_" + x) for x in (
            "hid", "hmoved", "o", "resid", "chain", "consts", "staged"))
        with ExitStack() as ctx:
            sb = lambda name, shape, dt=F32: self.sb(ctx, name, shape, dt)
            W1x = sb("W1x", [P, 2, HID])
            W1a = sb("W1a", [MUL, HID])
            W1u = sb("W1u", [P, HID])
            W2 = sb("W2", [P, KH, D])
            ucol = sb("ucol", [P, 1])
            b1 = sb("b1", [P, KH])
            bias = sb("bias", [P, KH])
            b2 = sb("b2", [1, D])
            ones = sb("g_ones", [1, P])
            tabs = sb("tabs", [P, 4, TABLES, C])
            pair = sb("g_pair", [P, 4, 2, C])
            summ = sb("g_sum", [P, 4, C])
            inv = sb("g_inv", [P, 4])
            mean = sb("g_mean", [P, 4, P])
            stage = sb("g_stage", [P, 4, D])
            xT = sb("xT", [P, 3, 4 * P])
            hid = sb("g_hidT", [P, KH, 4 * P])
            Y = sb("Yg", [P, W, D])
            scalar_part, vector_begin, vector_part, _ = self.norm_end(ctx, "gn", Y)
            sums = io["sums"].rearrange("(t r) c -> t r c", t=TABLES)
            block = ctx.enter_context(nc.Block())

            def loop(eng, body):
                body(0, 4)
                with eng.Fori(1, W // 4) as i:
                    body(i, 4)
                body(W // 4, W % 4)

            @block.sync
            def _(sp):
                sp.dma_start(W1x[:], io["W1"][0:D, :].rearrange("(t p) n -> p t n", p=P)).then_inc(loaded, 16)
                sp.dma_start(W1a[:], io["W1"][D:D + MUL, :]).then_inc(loaded, 16)
                sp.dma_start(W1u[:], io["W1"][D + MUL:D + MUL + P, :]).then_inc(loaded, 16)
                sp.dma_start(W2[:], io["W2"].rearrange("(t p) n -> p t n", p=P)).then_inc(loaded, 16)
                sp.dma_start(ucol[:], io["u"][0:1, :].rearrange("o p -> p o"),
                             allow_slow_non_contiguous=True).then_inc(loaded, 16)
                sp.dma_start(b1[:], io["b1"]).then_inc(loaded, 16)
                sp.dma_start(b2[:], io["b2"]).then_inc(loaded, 16)

                def body(i, m):
                    wait_pos(sp, mean_ready, i)
                    for w in range(m):
                        sp.dma_start(tabs[:, w, :, :],
                                     sums[:, bass.ds((i * 4 + w) * P, P), :].rearrange("t p c -> p t c")
                                     ).then_inc(tab_in, 16)
                loop(sp, body)

            @block.gpsimd
            def _(pool):
                def body(i, m):
                    wait_pos(pool, turned, 3 * i)
                    nc.gpsimd.tensor_copy(stage[:, 0:m, :], self.X[:, bass.ds(i * 4, m), :]).then_inc(staged, 1)
                loop(pool, body)

            @block.vector
            def _(dve):
                vector_begin(dve)
                nc.vector.memset(mean[:], 0.0)
                nc.vector.memset(ones[:], 1.0).then_inc(consts, 1)
                dve.wait_ge(consts, 1)
                dve.wait_ge(loaded, 112)
                dve.wait_ge(bias_sum, 1)
                nc.vector.tensor_tensor(bias[:], ps[:, 7, 0:KH], b1[:], ALU.add).then_inc(bias_ready, 1)

                def means(t, i, m):
                    dve.wait_ge(tab_in, 64 * i + 16 * m)
                    t.link(dve, nc.vector.tensor_tensor(pair[:, 0:m], tabs[:, 0:m, 0:2, :], tabs[:, 0:m, 2:4, :],
                                                        ALU.add))
                    t.link(dve, nc.vector.tensor_tensor(summ[:, 0:m], pair[:, 0:m, 0, :], pair[:, 0:m, 1, :],
                                                        ALU.add))
                    t.link(dve, nc.vector.tensor_scalar(inv[:, 0:m], summ[:, 0:m, MUL], 1.0, None, ALU.max))
                    t.link(dve, nc.vector.reciprocal(inv[:, 0:m], inv[:, 0:m]))
                    wait_pos(dve, moved, 3 * i)
                    for w in range(m):
                        last = nc.vector.tensor_scalar(mean[:, w, 0:MUL], summ[:, w, 0:MUL], inv[:, w:w + 1], None,
                                                       ALU.mult)
                    last.then_inc(mean_ready, 1)

                def body(i, m):
                    t = Tally(chain, i * 4)
                    means(t, i, m)
                    for w in range(m):
                        dve.wait_ge(o_ready, 4 * i + w + 1)
                        y = window(Y, 4 * i + w)
                        nc.vector.tensor_tensor(y, ps[:, 5 + w % 2, 0:D], window(self.X, 4 * i + w),
                                                ALU.add).then_inc(resid, 1)
                loop(dve, body)
                vector_part(dve, resid, W)

            @block.tensor
            def _(pe):
                pe.wait_ge(loaded, 112)
                pe.wait_ge(consts, 1)
                for t in range(KH):
                    last = nc.tensor.matmul(ps[:, 7, t:t + 1], W1u[:, t * P:(t + 1) * P], ucol[:], start=True,
                                            stop=True)
                last.then_inc(bias_sum, 1)

                def body(i, m):
                    n = m * P
                    pe.wait_ge(staged, i + 1)
                    for t in range(2):
                        for w in range(m):
                            last = nc.tensor.transpose(ps[:, t, w * P:(w + 1) * P],
                                                       stage[:, w, t * P:(t + 1) * P], self.ident[:])
                        last.then_inc(turned, 1)
                    pe.wait_ge(mean_ready, i + 1)
                    for w in range(m):
                        last = nc.tensor.transpose(ps[:, 2, w * P:(w + 1) * P], mean[:, w, :], self.ident[:])
                    last.then_inc(turned, 1)
                    pe.wait_ge(moved, 3 * i + 3)
                    for h in range(KH):
                        if h >= 2:
                            pe.wait_ge(hid_moved, KH * i + h - 1)
                        cols = slice(h * P, (h + 1) * P)
                        out = ps[:, 3 + h % 2, 0:n]
                        nc.tensor.matmul(out, W1x[:, 0, cols], xT[:, 0, 0:n], start=True, stop=False)
                        nc.tensor.matmul(out, W1x[:, 1, cols], xT[:, 1, 0:n], start=False, stop=False)
                        nc.tensor.matmul(out, W1a[:, cols], xT[0:MUL, 2, 0:n], start=False,
                                         stop=True).then_inc(hid_ready, 1)
                    pe.wait_ge(hid_moved, KH * (i + 1))
                    for w in range(m):
                        wait_pos(pe, resid, 4 * i + w - 1)
                        out = ps[:, 5 + w % 2, 0:D]
                        for h in range(KH):
                            nc.tensor.matmul(out, hid[:, h, w * P:(w + 1) * P], W2[:, h, :], start=h == 0, stop=False)
                        nc.tensor.matmul(out, ones[:], b2[:], start=False, stop=True).then_inc(o_ready, 1)
                loop(pe, body)

            @block.scalar
            def _(act):
                act.wait_ge(bias_ready, 1)

                def body(i, m):
                    n = m * P
                    wait_pos(act, o_ready, 4 * i)
                    for t in range(3):
                        rows = P if t < 2 else MUL
                        act.wait_ge(turned, 3 * i + t + 1)
                        nc.scalar.copy(xT[0:rows, t, 0:n], ps[0:rows, t, 0:n]).then_inc(moved, 1)
                    for h in range(KH):
                        act.wait_ge(hid_ready, KH * i + h + 1)
                        nc.scalar.activation(hid[:, h, 0:n], ps[:, 3 + h % 2, 0:n], ACT.Relu,
                                             bias=bias[:, h:h + 1]).then_inc(hid_moved, 1)
                loop(act, body)
                scalar_part(act)

    def layer3_edges(self, AGG):
        nc, io, ps = self.nc, self.io, self.ps
        ld = [self.sem(f"h_edges_in{k}") for k in range(UNROLL)]
        xg = [self.sem(f"h_rows_in{k}") for k in range(UNROLL)]
        once, biased, stored, zeroed = (self.sem("h_" + x) for x in ("once", "biased", "stored", "zeroed"))
        edge_ready, pre_ready, msg_ready, hot = (self.sem("h_" + x) for x in ("edge", "pre", "msg", "hot"))
        summed, added, locals_ready, tick = (self.sem("h_" + x) for x in ("summed", "added", "locals", "tick"))
        with ExitStack() as ctx:
            sb = lambda name, shape, dt=F32: self.sb(ctx, name, shape, dt)
            We = sb("We", [P, D])
            be = sb("be", [P, D])
            XB = sb("XB", [P, W, D])
            sd = sb("h_sd", [P, UNROLL, 2, 2], I32)
            attr = sb("h_attr", [P, UNROLL, SE])
            rows = sb("h_rows", [P, UNROLL, 2, D])
            pre = sb("h_pre", [P, 2, 2, D])
            msg = sb("h_msg", [P, 2, 2, D])
            dl = sb("h_dl", [P, 2, 2])
            oh = sb("h_oh", [P, 4, P])
            block = ctx.enter_context(nc.Block())

            def step(i, b):
                return i * UNROLL + b, b % UNROLL, i + b // UNROLL

            def loop(eng, body):
                body(0)
                with eng.Fori(1, ITERS - 1) as i:
                    body(i)
                body(ITERS - 1)

            @block.sync
            def _(sp):
                sp.dma_start(We[:], io["W_edge"]).then_inc(once, 16)
                sp.dma_start(be[:], io["b_edge"].to_broadcast([P, D])).then_inc(once, 16)
                for w in range(0, W, 5):
                    sp.wait_ge(biased, w + 5)
                    sp.dma_start(io["rows3"][w * P:(w + 5) * P, :].rearrange("(w p) d -> p w d", p=P),
                                 XB[:, w:w + 5, :]).then_inc(stored, 16)

                def body(i):
                    for b in range(UNROLL):
                        s, k, _ = step(i, b)
                        wait_pos(sp, summed, s - UNROLL + 1)
                        o = sp.value_load(self.off[0:1, bass.ds(s, 1)], min_val=0, max_val=EP - SE)
                        sp.dma_start(sd[:, k, :, :], io["sd"][bass.ds(o, SE), :]
                                     .rearrange("(p t) c -> p t c", t=2)).then_inc(ld[k], 16)
                        sp.dma_start(attr[:, k, :], io["attr128"][:, bass.ds(o, SE)]).then_inc(ld[k], 16)
                loop(sp, body)

            @block.gpsimd
            def _(pool):
                pool.wait_ge(stored, 16 * (W // 5))
                pool.sem_inc(tick, 1)

                def body(i):
                    for k in range(UNROLL):
                        pool.wait_ge(ld[k], 32 * (i + 1))
                        pool.sem_inc(tick, 1)
                        for q in range(2):
                            pool.indirect_dma_start(
                                out=rows[:, k, q, :], out_offset=None, in_=io["rows3"],
                                in_offset=bass.IndirectOffsetOnAxis(ap=sd[:, k, q, 0:1], axis=0)).then_inc(xg[k], 16)
                loop(pool, body)

            @block.tensor
            def _(pe):
                pe.wait_ge(once, 32)

                def edge(i, b):
                    s, k, it = step(i, b)
                    pe.wait_ge(ld[k], 32 * (it + 1))
                    wait_pos(pe, pre_ready, s - 1)
                    by_tile = attr[:, k, :].rearrange("f (p t) -> f t p", t=2)
                    for q in range(2):
                        last = nc.tensor.matmul(ps[:, b % 2, q * D:(q + 1) * D], by_tile[:, q, :], We[:], start=True,
                                                stop=True)
                    last.then_inc(edge_ready, 1)

                def body(i):
                    for b in range(UNROLL):
                        s = i * UNROLL + b
                        if not (isinstance(s, int) and s + 1 == STEPS):
                            edge(i, b + 1)
                        pe.wait_ge(msg_ready, s + 1)
                        pe.wait_ge(hot, s + 1)
                        wait_pos(pe, added, s - 1)
                        for q in range(2):
                            last = nc.tensor.matmul(ps[:, 2 + b % 2, 0:D], oh[:, (2 * b + q) % 4, :],
                                                    msg[:, b % 2, q, :], start=q == 0, stop=q == 1)
                        last.then_inc(summed, 1)
                edge(0, 0)
                loop(pe, body)

            @block.scalar
            def _(act):
                def body(i):
                    for b in range(UNROLL):
                        s = i * UNROLL + b
                        act.wait_ge(pre_ready, s + 1)
                        wait_pos(act, summed, s - 1)
                        nc.scalar.activation(msg[:, b % 2, :, :], pre[:, b % 2, :, :],
                                             ACT.Relu).then_inc(msg_ready, 1)
                loop(act, body)

            @block.vector
            def _(dve):
                dve.wait_ge(once, 32)
                for_fives(dve, lambda w: nc.vector.tensor_tensor(window(XB, w), window(self.X, w), be[:],
                                                                 ALU.add).then_inc(biased, 1))
                nc.vector.memset(AGG[:], 0.0).then_inc(zeroed, 1)
                dve.wait_ge(zeroed, 1)

                def local(i, b):
                    s, k, it = step(i, b)
                    dve.wait_ge(ld[k], 32 * (it + 1))
                    nc.vector.tensor_tensor(dl[:, b % 2, :], sd[:, k, :, 1],
                                            self.win_col[:, bass.ds(s, 1)].to_broadcast([P, 2]),
                                            ALU.subtract).then_inc(locals_ready, 1)

                def add(s, p):
                    w = dve.value_load(self.win[0:1, bass.ds(s, 1)], min_val=0, max_val=W - 1)
                    dve.wait_ge(summed, s + 1)
                    wait_pos(dve, added, s)
                    a = window(AGG, w)
                    nc.vector.tensor_tensor(a, a, ps[:, 2 + p, 0:D], ALU.add).then_inc(added, 1)

                def body(i):
                    for b in range(UNROLL):
                        s = i * UNROLL + b
                        dve.wait_ge(locals_ready, s + 1)
                        for q in range(2):
                            last = nc.vector.tensor_scalar(oh[:, (2 * b + q) % 4, :], self.iota[:],
                                                           dl[:, b % 2, q:q + 1], None, ALU.is_equal)
                        last.then_inc(hot, 1)
                        if not (isinstance(s, int) and s + 1 == STEPS):
                            local(i, b + 1)
                        dve.wait_ge(xg[b], 32 * (i + 1))
                        dve.wait_ge(edge_ready, s + 1)
                        wait_pos(dve, msg_ready, s - 1)
                        nc.vector.tensor_tensor(pre[:, b % 2, :, :].rearrange("p t d -> p (t d)"), ps[:, b % 2, :],
                                                rows[:, b, :, :].rearrange("p t d -> p (t d)"),
                                                ALU.add).then_inc(pre_ready, 1)
                        if not (isinstance(s, int) and s == 0):
                            add(s - 1, (b - 1) % 2)
                local(0, 0)
                loop(dve, body)
                add(STEPS - 1, (STEPS - 1) % 2)

    def layer3_nodes(self, AGG):
        nc, io, ps = self.nc, self.io, self.ps
        loaded, eps1, h_ready, turned, moved = (self.sem("i_" + x) for x in ("loaded", "eps1", "h", "turned", "moved"))
        z1, r1, z2, r2 = (self.sem("i_" + x) for x in ("z1", "r1", "z2", "r2"))
        chain, bvar, bstd, coef, act_done, back, resid = (self.sem("i_" + x) for x in (
            "chain", "bvar", "bstd", "coef", "act", "back", "resid"))
        stored, bn_eps = self.sem("i_stored"), self.sem("i_bneps")
        CH = [(c, min(512, N - c)) for c in range(0, N, 512)]
        with ExitStack() as ctx:
            sb = lambda name, shape, dt=F32: self.sb(ctx, name, shape, dt)
            V1, V2 = sb("V1", [P, 2, D]), sb("V2", [P, 2, D])
            c1, c2, gamma, beta = (sb("i_" + x, [P, 2]) for x in ("c1", "c2", "gamma", "beta"))
            eps = sb("i_eps", [P, 1])
            beps = sb("i_beps", [P, 1])
            stage = sb("i_stage", [P, 4 * D])
            zr = sb("zr", [P, 2, 2, P])
            hT = sb("hT", [P, 2, 512])
            gT = sb("gT", [P, 2, 512])
            Z = sb("Zi", [P, 2, NPAD])
            bst = sb("i_bst", [P, 2, len(CH), 6])
            bmv = sb("i_bmv", [P, 2, 2])
            bsd = sb("i_bsd", [P, 2])
            mul, shf = sb("i_mul", [P, 2]), sb("i_shf", [P, 2])
            Y = sb("Yi", [P, W, D])
            scalar_part, vector_begin, vector_part, written = self.norm_end(ctx, "last", Y)
            block = ctx.enter_context(nc.Block())

            def loop(eng, body):
                body(0, 4)
                with eng.Fori(1, W // 4) as i:
                    body(i, 4)
                body(W // 4, W % 4)

            @block.sync
            def _(sp):
                for name, tile in (("V1", V1), ("V2", V2)):
                    sp.dma_start(tile[:], io[name].rearrange("(t p) n -> p t n", p=P)).then_inc(loaded, 16)
                for name, tile in (("c1", c1), ("c2", c2), ("gamma", gamma), ("beta", beta)):
                    sp.dma_start(tile[:], io[name]).then_inc(loaded, 16)
                sp.dma_start(eps[:], io["eps"].to_broadcast([P, 1])).then_inc(loaded, 16)
                for w in range(0, W, 5):
                    sp.wait_ge(written, w + 5)
                    full = min(w + 5, W - 1)
                    sp.dma_start(io["out"][w * P:full * P, :].rearrange("(w p) d -> p w d", p=P),
                                 self.X[:, w:full, :]).then_inc(stored, 16)
                sp.dma_start(io["out"][(W - 1) * P:N, :], self.X[0:TAIL, W - 1, :]).then_inc(stored, 16)
                sp.wait_ge(stored, 16 * (W // 5 + 1))

            @block.vector
            def _(dve):
                vector_begin(dve)
                dve.wait_ge(loaded, 112)
                nc.vector.memset(beps[:], 1.0e-5).then_inc(bn_eps, 1)
                nc.vector.tensor_scalar(eps[:], eps[:], 1.0, None, ALU.add).then_inc(eps1, 1)
                dve.wait_ge(eps1, 1)

                def update(i, m):
                    wait_pos(dve, turned, 2 * i)
                    group = lambda x: x[:, bass.ds(i * 4, m), :].rearrange("p w d -> p (w d)")
                    nc.vector.scalar_tensor_tensor(stage[:, 0:m * D], group(self.X), eps[:], group(AGG),
                                                   ALU.mult, ALU.add).then_inc(h_ready, 1)
                loop(dve, update)
                t = Tally(chain, 0)
                dve.wait_ge(r2, 2 * (W // 4 + 1))
                for h in range(2):
                    for c, (lo, m) in enumerate(CH):
                        nc.vector.bn_stats(bst[:, h, c, :], Z[:, h, lo:lo + m])
                t.link(dve, nc.vector.engine_nop())
                for h in range(2):
                    nc.vector.bn_aggr(bmv[:, h, :], bst[:, h, :, :].rearrange("p c s -> p (c s)"))
                nc.vector.engine_nop().then_inc(bvar, 1)
                dve.wait_ge(bstd, 1)
                t.link(dve, nc.vector.reciprocal(bsd[:], bsd[:]))
                t.link(dve, nc.vector.tensor_tensor(mul[:], gamma[:], bsd[:], ALU.mult))
                t.link(dve, nc.vector.tensor_tensor(shf[:], bmv[:, :, 0], mul[:], ALU.mult))
                nc.vector.tensor_tensor(shf[:], beta[:], shf[:], ALU.subtract).then_inc(coef, 1)

                def residual(w, k):
                    dve.wait_ge(back, w + 1)
                    nc.vector.tensor_tensor(window(Y, w), ps[:, k, 0:D], window(self.X, w), ALU.add).then_inc(resid, 1)
                for_pairs(dve, residual)
                residual(W - 1, 0)
                vector_part(dve, resid, W)

            @block.tensor
            def _(pe):
                pe.wait_ge(loaded, 112)

                def body(i, m):
                    n = m * P
                    pe.wait_ge(h_ready, i + 1)
                    for t in range(2):
                        for w in range(m):
                            last = nc.tensor.transpose(ps[:, t, w * P:(w + 1) * P],
                                                       stage[:, w * D + t * P:w * D + (t + 1) * P], self.ident[:])
                        last.then_inc(turned, 1)
                    pe.wait_ge(moved, 2 * i + 2)
                    for h in range(2):
                        out = ps[:, 2 + h, 0:n]
                        for t in range(2):
                            last = nc.tensor.matmul(out, V1[:, t, h * P:(h + 1) * P], hT[:, t, 0:n], start=t == 0,
                                                    stop=t == 1)
                        last.then_inc(z1, 1)
                    pe.wait_ge(r1, 2 * i + 2)
                    for h in range(2):
                        wait_pos(pe, r2, 2 * i)
                        out = ps[:, 4 + h, 0:n]
                        for t in range(2):
                            last = nc.tensor.matmul(out, V2[:, t, h * P:(h + 1) * P], gT[:, t, 0:n], start=t == 0,
                                                    stop=t == 1)
                        last.then_inc(z2, 1)
                loop(pe, body)

                def turn(w, k):
                    pe.wait_ge(act_done, 2 * w + 2)
                    wait_pos(pe, resid, w - 1)
                    for h in range(2):
                        last = nc.tensor.transpose(ps[:, k, h * P:(h + 1) * P], zr[:, k, h, :], self.ident[:])
                    last.then_inc(back, 1)
                for_pairs(pe, turn)
                turn(W - 1, 0)

            @block.scalar
            def _(act):
                act.wait_ge(loaded, 112)

                def body(i, m):
                    n = m * P
                    wait_pos(act, z1, 2 * i)
                    for t in range(2):
                        act.wait_ge(turned, 2 * i + t + 1)
                        nc.scalar.copy(hT[:, t, 0:n], ps[:, t, 0:n]).then_inc(moved, 1)
                    wait_pos(act, z2, 2 * i)
                    for h in range(2):
                        act.wait_ge(z1, 2 * i + h + 1)
                        nc.scalar.activation(gT[:, h, 0:n], ps[:, 2 + h, 0:n], ACT.Relu,
                                             bias=c1[:, h:h + 1]).then_inc(r1, 1)
                    for h in range(2):
                        act.wait_ge(z2, 2 * i + h + 1)
                        nc.scalar.activation(Z[:, h, bass.ds(i * 512, n)], ps[:, 4 + h, 0:n], ACT.Identity,
                                             bias=c2[:, h:h + 1]).then_inc(r2, 1)
                loop(act, body)
                act.wait_ge(bvar, 1)
                act.wait_ge(bn_eps, 1)
                nc.scalar.activation(bsd[:], bmv[:, :, 1], ACT.Sqrt, bias=beps[:]).then_inc(bstd, 1)
                act.wait_ge(coef, 1)

                def relu(w, k):
                    wait_pos(act, back, w - 1)
                    for h in range(2):
                        nc.scalar.activation(zr[:, k, h, :], Z[:, h, bass.ds(w * P, P)], ACT.Relu,
                                             bias=shf[:, h:h + 1], scale=mul[:, h:h + 1]).then_inc(act_done, 1)
                for_pairs(act, relu)
                relu(W - 1, 0)
                scalar_part(act)


def gnn_stack(nc, io):
    with ExitStack() as ctx:
        prog = Program(nc, ctx, io)
        with ExitStack() as inner:
            prog.zeros = prog.sb(inner, "zeros", [P, NPAD])
            prog.setup()
            prog.end_stage()
            ACC = prog.sb(inner, "ACC", [P, W * ACW])
            prog.layer0_edges(ACC)
            prog.end_stage()
            prog.layer0_nodes(ACC)
            prog.end_stage()
        with ExitStack() as inner:
            T = [prog.sb(inner, f"T{x}", [P, 2, NPAD], F16) for x in ("hi", "lo")]
            HS = [prog.sb(inner, f"H{x}", [P, W, D], F16) for x in ("hi", "lo")]
            betas = prog.sb(inner, "betas", [P, 4])
            squares = prog.sb(inner, "squares", [P, W])
            places = [prog.sb(inner, "p_" + x, [P, PAIR_TILES]) for x in ("srcf", "spare", "home", "away")]
            prog.prepare_attention(betas, places)
            prog.end_stage()
            for layer in range(4):
                prog.attention(layer, T, HS, betas, places, squares)
                prog.end_stage()
        prog.add_norm()
        prog.end_stage()
        prog.layer2_nodes()
        prog.end_stage()
        with ExitStack() as inner:
            AGG = prog.sb(inner, "AGG", [P, W, D])
            prog.layer3_edges(AGG)
            prog.end_stage()
            prog.layer3_nodes(AGG)


def kernel(**inputs):
    import numpy as np
    import concourse.bacc as bacc
    from concourse.bass_utils import run_bass_kernel_spmd

    nc = bacc.Bacc("TRN2", target_bir_lowering=False, num_devices=1)
    a = {name: np.asarray(value) for name, value in inputs.items()}
    src, dst = a["src"], a["dst"]
    spare = EP - E
    src_in = np.concatenate([src, np.zeros(spare, src.dtype)])
    src_id = np.concatenate([src, np.full(spare, PAD_ID, src.dtype)])
    dst_id = np.concatenate([dst, np.full(spare, PAD_ID, dst.dtype)])
    rows = lambda v: np.concatenate([v, np.zeros((spare, v.shape[1]), v.dtype)])
    arrays = {
        "x": a["x"],
        "x_blocks": np.concatenate([a["x"][:, :MUL]] + [a["x"][:, MUL + m::3] for m in range(3)], axis=1),
        "sd": np.stack([src_in, dst_id], axis=1),
        "ids": src_id.reshape(1, EP),
        "src_t": src_id[:PAIR_TILES * P].reshape(PAIR_TILES, P).T,
        "dst_t": dst_id[:PAIR_TILES * P].reshape(PAIR_TILES, P).T,
        "attr4": rows(a["edge_attr_4"]),
        "emb": rows(a["edge_attr_10"]).T,
        "attr64": rows(a["edge_attr_64"]),
        "attr128": rows(a["edge_attr_128"]).T,
        "w_00_0": a["L0_gnn_w_00_0"], "w_11_0": a["L0_gnn_w_11_0"],
        "w_01_1": a["L0_gnn_w_01_1"], "w_10_1": a["L0_gnn_w_10_1"],
        "fc_w1": a["L0_gnn_fc_w1"], "fc_w2": a["L0_gnn_fc_w2"],
        "betas": a["L1_gnn_betas"].reshape(1, 4),
        "u": a["L2_gnn_u"], "W1": a["L2_gnn_W1"], "b1": a["L2_gnn_b1"].reshape(4, P).T,
        "W2": a["L2_gnn_W2"], "b2": a["L2_gnn_b2"].reshape(1, D),
        "W_edge": a["L3_gnn_W_edge"], "b_edge": a["L3_gnn_b_edge"].reshape(1, D),
        "V1": a["L3_gnn_W1"], "c1": a["L3_gnn_b1"].reshape(2, P).T,
        "V2": a["L3_gnn_W2"], "c2": a["L3_gnn_b2"].reshape(2, P).T,
        "eps": a["L3_gnn_eps"].reshape(1, 1),
        "gamma": a["L3_gnn_gamma"].reshape(2, P).T, "beta": a["L3_gnn_beta"].reshape(2, P).T,
    }
    arrays = {f"in_{name}": np.ascontiguousarray(value) for name, value in arrays.items()}
    io = {name[3:]: nc.dram_tensor(name, v.shape, mybir.dt.from_np(v.dtype), kind="ExternalInput").ap()
          for name, v in arrays.items()}
    io["counts"] = nc.dram_tensor("counts", (CELLS + 2 * P, 1), F32, kind="Internal").ap()
    io["sums"] = nc.dram_tensor("sums", (TABLES * TROWS, 65), F32, kind="Internal").ap()
    io["x_kept"] = nc.dram_tensor("x_kept", (NPAD, D), F32, kind="Internal").ap()
    io["rows3"] = nc.dram_tensor("rows3", (NPAD, D), F32, kind="Internal").ap()
    io["out"] = nc.dram_tensor("out", (N, D), F32, kind="ExternalOutput").ap()
    gnn_stack(nc, io)
    result = run_bass_kernel_spmd(nc, [arrays], core_ids=[0])
    return result.results[0]["out"]
```
